# Optimizing a Trainium2 kernel written in Bass

```python
import numpy as np
import jax
import jax.numpy as jnp

def _softmax(x, axis=-1):
    return jax.nn.softmax(x, axis=axis)

def _gelu(x):
    return jax.nn.gelu(x, approximate=True)

def _silu(x):
    return jax.nn.silu(x)

def _sigmoid(x):
    return jax.nn.sigmoid(x)

def _layernorm(x, axis=-1, eps=1e-05):
    m = jnp.mean(x, axis=axis, keepdims=True)
    v = jnp.var(x, axis=axis, keepdims=True)
    return (x - m) / jnp.sqrt(v + eps)

def _scatter_add(tgt, idx, src, axis=0):
    return tgt.at[idx].add(src)

def _segment_sum(src, seg, n):
    return jax.ops.segment_sum(src, seg, n)
kernel_name = 'mk_prb_d1_jaxref_r8_add70f'

def setup_inputs(seed: int=0):
    np.random.seed(seed)
    _w = jnp.asarray

    def _L0_attn_setup():
        import jax, jax.numpy as jnp
        import numpy as np
        B, L, D = (4, 256, 128)
        H, DK, DV = (4, 32, 32)
        CHUNK = 32
        MIN_FLOOR, MAX_FLOOR = (0.01, 0.1)
        EPS = 1e-05

        def _l2norm(x):
            return x * jax.lax.rsqrt(jnp.sum(x * x, -1, keepdims=True) + 1e-06)

        def _causal_dwconv(x, w):
            b, l, c = x.shape
            k = w.shape[-1]
            xt = jnp.transpose(x, (0, 2, 1))
            y = jax.lax.conv_general_dilated(xt, w[:, None, :], (1,), [(k - 1, 0)], dimension_numbers=('NCH', 'OIH', 'NCH'), feature_group_count=c)
            return jnp.transpose(y, (0, 2, 1))

        def _delta_rule_chunkwise(q, k, v, beta, chunk=CHUNK):
            b, h, l, dk = q.shape
            dv = v.shape[-1]
            q = _l2norm(q)
            k = _l2norm(k)
            v = v * beta[..., None]
            kb = k * beta[..., None]
            n = l // chunk
            resh = lambda t: t.reshape(b, h, n, chunk, t.shape[-1])
            q, k, v, kb = (resh(q), resh(k), resh(v), resh(kb))
            tri = jnp.triu(jnp.ones((chunk, chunk), bool))
            strict = jnp.triu(jnp.ones((chunk, chunk), bool), 1)
            att = jnp.where(tri, 0.0, -(kb @ jnp.swapaxes(k, -1, -2)))
            for i in range(1, chunk):
                upd = jnp.einsum('bhnj,bhnjk->bhnk', att[..., i, :], att)
                att = att.at[..., i, :i].add(upd[..., :i])
            att = att + jnp.eye(chunk, dtype=att.dtype)
            u = att @ v
            w = att @ kb

            def step(S, xs):
                q_i, k_i, u_i, w_i = xs
                local = jnp.where(strict, 0.0, q_i @ jnp.swapaxes(k_i, -1, -2))
                u_adj = u_i - w_i @ S
                o_i = q_i @ S + local @ u_adj
                return (S + jnp.swapaxes(k_i, -1, -2) @ u_adj, o_i)
            xs = tuple((jnp.moveaxis(t, 2, 0) for t in (q, k, u, w)))
            S0 = jnp.zeros((b, h, dk, dv), q.dtype)
            S, o = jax.lax.scan(step, S0, xs)
            return (jnp.moveaxis(o, 0, 2).reshape(b, h, l, dv), S)

        def _rmsnorm(x, w):
            return x * jax.lax.rsqrt(jnp.mean(x * x, -1, keepdims=True) + EPS) * w
        key = jax.random.key(seed)
        ks = jax.random.split(key, 16)
        s = 0.02
        return {'hidden_states': jax.random.normal(ks[0], (B, L, D), jnp.float32), 'W_q': jax.random.normal(ks[1], (D, H * DK), jnp.float32) * s, 'W_k': jax.random.normal(ks[2], (D, H * DK), jnp.float32) * s, 'W_v': jax.random.normal(ks[3], (D, H * DV), jnp.float32) * s, 'W_b': jax.random.normal(ks[4], (D, H), jnp.float32) * s, 'conv_w_q': jax.random.normal(ks[5], (H * DK, 4), jnp.float32) * 0.3, 'conv_w_k': jax.random.normal(ks[6], (H * DK, 4), jnp.float32) * 0.3, 'conv_w_v': jax.random.normal(ks[7], (H * DV, 4), jnp.float32) * 0.3, 'fir_short_w': jax.random.normal(ks[8], (H, DV, 3), jnp.float32) * 0.1, 'fir_long_w': jax.random.normal(ks[9], (H, DV, 31), jnp.float32) * 0.1, 'W_fuse1': jax.random.normal(ks[10], (D + 3 * H * DV, 2 * D), jnp.float32) * s, 'b_fuse1': jnp.zeros((2 * D,), jnp.float32), 'W_fuse2': jax.random.normal(ks[11], (2 * D, H * 4), jnp.float32) * s, 'b_fuse2': jnp.zeros((H * 4,), jnp.float32).at[3::4].set(4.0), 'others_log_tau': jnp.zeros((H,), jnp.float32), 'norm_w': jnp.ones((DV,), jnp.float32), 'W_o': jax.random.normal(ks[12], (H * DV, D), jnp.float32) * s}
    _L0_attn_in = _L0_attn_setup()

    def _L0_ffn_setup():
        import jax, jax.numpy as jnp
        import numpy as np
        E, H, F, K = (8, 128, 256, 2)
        B, S = (2, 256)
        key = jax.random.key(seed)
        ks = jax.random.split(key, 8)

        def w(k, shape, fan_in):
            return jax.random.normal(k, shape, jnp.float32) / np.float32(np.sqrt(fan_in))
        return {'x': jax.random.normal(ks[0], (B, S, H), jnp.float32), 'Wgate': w(ks[1], (H, E), H), 'bgate': jnp.zeros((E,), jnp.float32), 'W1': w(ks[2], (E, H, F), H), 'b1': jnp.zeros((E, F), jnp.float32), 'W2': w(ks[3], (E, H, F), H), 'b2': jnp.zeros((E, F), jnp.float32), 'Wg': w(ks[4], (E, F, F), F), 'bg': jnp.zeros((E, F), jnp.float32), 'Wl': w(ks[5], (E, F, F), F), 'bl': jnp.zeros((E, F), jnp.float32), 'W3': w(ks[6], (E, F, H), F), 'b3': jnp.zeros((E, H), jnp.float32)}
    _L0_ffn_in = _L0_ffn_setup()
    _d = {'L0_attn_hidden_states': _L0_attn_in['hidden_states'], 'L0_attn_W_q': _L0_attn_in['W_q'], 'L0_attn_W_k': _L0_attn_in['W_k'], 'L0_attn_W_v': _L0_attn_in['W_v'], 'L0_attn_W_b': _L0_attn_in['W_b'], 'L0_attn_conv_w_q': _L0_attn_in['conv_w_q'], 'L0_attn_conv_w_k': _L0_attn_in['conv_w_k'], 'L0_attn_conv_w_v': _L0_attn_in['conv_w_v'], 'L0_attn_fir_short_w': _L0_attn_in['fir_short_w'], 'L0_attn_fir_long_w': _L0_attn_in['fir_long_w'], 'L0_attn_W_fuse1': _L0_attn_in['W_fuse1'], 'L0_attn_b_fuse1': _L0_attn_in['b_fuse1'], 'L0_attn_W_fuse2': _L0_attn_in['W_fuse2'], 'L0_attn_b_fuse2': _L0_attn_in['b_fuse2'], 'L0_attn_others_log_tau': _L0_attn_in['others_log_tau'], 'L0_attn_norm_w': _L0_attn_in['norm_w'], 'L0_attn_W_o': _L0_attn_in['W_o'], 'L0_ffn_Wgate': _L0_ffn_in['Wgate'], 'L0_ffn_bgate': _L0_ffn_in['bgate'], 'L0_ffn_W1': _L0_ffn_in['W1'], 'L0_ffn_b1': _L0_ffn_in['b1'], 'L0_ffn_W2': _L0_ffn_in['W2'], 'L0_ffn_b2': _L0_ffn_in['b2'], 'L0_ffn_Wg': _L0_ffn_in['Wg'], 'L0_ffn_bg': _L0_ffn_in['bg'], 'L0_ffn_Wl': _L0_ffn_in['Wl'], 'L0_ffn_bl': _L0_ffn_in['bl'], 'L0_ffn_W3': _L0_ffn_in['W3'], 'L0_ffn_b3': _L0_ffn_in['b3']}
    _x0 = _d['L0_attn_hidden_states']
    _d['L0_attn_hidden_states'] = jax.random.normal(jax.random.fold_in(jax.random.key(seed), 1), (4, 1024, 128), dtype=_x0.dtype)
    del _x0
    return _d

def reference(L0_attn_hidden_states, L0_attn_W_q, L0_attn_W_k, L0_attn_W_v, L0_attn_W_b, L0_attn_conv_w_q, L0_attn_conv_w_k, L0_attn_conv_w_v, L0_attn_fir_short_w, L0_attn_fir_long_w, L0_attn_W_fuse1, L0_attn_b_fuse1, L0_attn_W_fuse2, L0_attn_b_fuse2, L0_attn_others_log_tau, L0_attn_norm_w, L0_attn_W_o, L0_ffn_Wgate, L0_ffn_bgate, L0_ffn_W1, L0_ffn_b1, L0_ffn_W2, L0_ffn_b2, L0_ffn_Wg, L0_ffn_bg, L0_ffn_Wl, L0_ffn_bl, L0_ffn_W3, L0_ffn_b3):

    def _L0_attn_ref(hidden_states, W_q, W_k, W_v, W_b, conv_w_q, conv_w_k, conv_w_v, fir_short_w, fir_long_w, W_fuse1, b_fuse1, W_fuse2, b_fuse2, others_log_tau, norm_w, W_o):
        import jax, jax.numpy as jnp
        import numpy as np
        B, L, D = (4, 256, 128)
        H, DK, DV = (4, 32, 32)
        CHUNK = 32
        MIN_FLOOR, MAX_FLOOR = (0.01, 0.1)
        EPS = 1e-05

        def _l2norm(x):
            return x * jax.lax.rsqrt(jnp.sum(x * x, -1, keepdims=True) + 1e-06)

        def _causal_dwconv(x, w):
            b, l, c = x.shape
            k = w.shape[-1]
            xt = jnp.transpose(x, (0, 2, 1))
            y = jax.lax.conv_general_dilated(xt, w[:, None, :], (1,), [(k - 1, 0)], dimension_numbers=('NCH', 'OIH', 'NCH'), feature_group_count=c)
            return jnp.transpose(y, (0, 2, 1))

        def _delta_rule_chunkwise(q, k, v, beta, chunk=CHUNK):
            b, h, l, dk = q.shape
            dv = v.shape[-1]
            q = _l2norm(q)
            k = _l2norm(k)
            v = v * beta[..., None]
            kb = k * beta[..., None]
            n = l // chunk
            resh = lambda t: t.reshape(b, h, n, chunk, t.shape[-1])
            q, k, v, kb = (resh(q), resh(k), resh(v), resh(kb))
            tri = jnp.triu(jnp.ones((chunk, chunk), bool))
            strict = jnp.triu(jnp.ones((chunk, chunk), bool), 1)
            att = jnp.where(tri, 0.0, -(kb @ jnp.swapaxes(k, -1, -2)))
            for i in range(1, chunk):
                upd = jnp.einsum('bhnj,bhnjk->bhnk', att[..., i, :], att)
                att = att.at[..., i, :i].add(upd[..., :i])
            att = att + jnp.eye(chunk, dtype=att.dtype)
            u = att @ v
            w = att @ kb

            def step(S, xs):
                q_i, k_i, u_i, w_i = xs
                local = jnp.where(strict, 0.0, q_i @ jnp.swapaxes(k_i, -1, -2))
                u_adj = u_i - w_i @ S
                o_i = q_i @ S + local @ u_adj
                return (S + jnp.swapaxes(k_i, -1, -2) @ u_adj, o_i)
            xs = tuple((jnp.moveaxis(t, 2, 0) for t in (q, k, u, w)))
            S0 = jnp.zeros((b, h, dk, dv), q.dtype)
            S, o = jax.lax.scan(step, S0, xs)
            return (jnp.moveaxis(o, 0, 2).reshape(b, h, l, dv), S)

        def _rmsnorm(x, w):
            return x * jax.lax.rsqrt(jnp.mean(x * x, -1, keepdims=True) + EPS) * w
        b, l, d = hidden_states.shape
        q = jax.nn.silu(_causal_dwconv(hidden_states @ W_q, conv_w_q))
        k = jax.nn.silu(_causal_dwconv(hidden_states @ W_k, conv_w_k))
        v = jax.nn.silu(_causal_dwconv(hidden_states @ W_v, conv_w_v))
        q = q.reshape(b, l, H, DK)
        k = k.reshape(b, l, H, DK)
        v = v.reshape(b, l, H, DV)
        beta = jax.nn.sigmoid(hidden_states @ W_b)
        delta_out, _ = _delta_rule_chunkwise(jnp.transpose(q, (0, 2, 1, 3)), jnp.transpose(k, (0, 2, 1, 3)), jnp.transpose(v, (0, 2, 1, 3)), jnp.transpose(beta, (0, 2, 1)))
        delta_out = jnp.transpose(delta_out, (0, 2, 1, 3))
        vc = v.reshape(b, l, H * DV)
        fir_s = _causal_dwconv(vc, fir_short_w.reshape(H * DV, -1)).reshape(b, l, H, DV)
        fir_l = _causal_dwconv(vc, fir_long_w.reshape(H * DV, -1)).reshape(b, l, H, DV)
        gate_in = jnp.concatenate([hidden_states, fir_s.reshape(b, l, -1), fir_l.reshape(b, l, -1), delta_out.reshape(b, l, -1)], -1)
        hid = jax.nn.gelu(gate_in @ W_fuse1 + b_fuse1, approximate=False)
        logits = (hid @ W_fuse2 + b_fuse2).reshape(b, l, H, 4)
        p_raw = jax.nn.sigmoid(logits[..., 3])
        floor = MIN_FLOOR + (MAX_FLOOR - MIN_FLOOR) * (1.0 - p_raw)
        p_val = (1.0 - floor) * p_raw
        tau = jnp.exp(others_log_tau)
        others = jax.nn.softmax(logits[..., :3] / tau[None, None, :, None], -1)
        p_ctx = (1.0 - p_val)[..., None] * others
        o = p_ctx[..., 0:1] * fir_s + p_ctx[..., 1:2] * fir_l + p_ctx[..., 2:3] * delta_out + p_val[..., None] * v
        o = _rmsnorm(o, norm_w)
        return o.reshape(b, l, H * DV) @ W_o

    def _L0_ffn_ref(x, Wgate, bgate, W1, b1, W2, b2, Wg, bg, Wl, bl, W3, b3):
        import jax, jax.numpy as jnp
        import numpy as np
        E, H, F, K = (8, 128, 256, 2)
        B, S = (2, 256)
        gout = x @ Wgate + bgate
        topv, topi = jax.lax.top_k(gout, K)
        topw = jax.nn.softmax(topv, axis=-1)
        combine = jnp.sum(jax.nn.one_hot(topi, E, dtype=x.dtype) * topw[..., None], axis=-2)
        x1 = jnp.einsum('bsh,ehf->bsef', x, W1) + b1
        x2 = jnp.einsum('bsh,ehf->bsef', x, W2) + b2
        z = x1 * x2
        g = jnp.einsum('bsef,efg->bseg', z, Wg) + bg
        o = g * jax.nn.sigmoid(g) * (jnp.einsum('bsef,efg->bseg', z, Wl) + bl)
        y = jnp.einsum('bsef,efh->bseh', o, W3) + b3
        return jnp.einsum('bse,bseh->bsh', combine, y)
    x = L0_attn_hidden_states
    xn = _layernorm(x, axis=-1)
    x = x + _L0_attn_ref(xn, L0_attn_W_q, L0_attn_W_k, L0_attn_W_v, L0_attn_W_b, L0_attn_conv_w_q, L0_attn_conv_w_k, L0_attn_conv_w_v, L0_attn_fir_short_w, L0_attn_fir_long_w, L0_attn_W_fuse1, L0_attn_b_fuse1, L0_attn_W_fuse2, L0_attn_b_fuse2, L0_attn_others_log_tau, L0_attn_norm_w, L0_attn_W_o) + _L0_ffn_ref(xn, L0_ffn_Wgate, L0_ffn_bgate, L0_ffn_W1, L0_ffn_b1, L0_ffn_W2, L0_ffn_b2, L0_ffn_Wg, L0_ffn_bg, L0_ffn_Wl, L0_ffn_bl, L0_ffn_W3, L0_ffn_b3)
    return x

_drawn_inputs = setup_inputs


def setup_inputs(seed=0):
    import zlib

    import numpy as np

    out = dict(_drawn_inputs(seed))
    spreads = {'L0_attn_b_fuse1': (0.0, 0.8),
     'L0_attn_others_log_tau': (0.0, 0.8),
     'L0_attn_norm_w': (1.0, 0.2),
     'L0_ffn_bgate': (0.0, 0.1),
     'L0_ffn_b1': (0.0, 0.1),
     'L0_ffn_b2': (0.0, 0.1),
     'L0_ffn_bg': (0.0, 0.1),
     'L0_ffn_bl': (0.0, 0.1),
     'L0_ffn_b3': (0.0, 0.1)}
    factors = {'L0_attn_W_q': 8.0,
     'L0_attn_W_k': 8.0,
     'L0_attn_W_b': 8.0,
     'L0_attn_conv_w_q': 8.0,
     'L0_attn_conv_w_k': 8.0,
     'L0_attn_fir_short_w': 8.0,
     'L0_attn_fir_long_w': 8.0,
     'L0_attn_W_fuse1': 8.0,
     'L0_attn_W_fuse2': 8.0}
    for name, (base, spread) in spreads.items():
        noise = np.random.default_rng([zlib.crc32(name.encode()), seed]).standard_normal(out[name].shape)
        drawn = base * np.exp(spread * noise) if base else spread * noise
        out[name] = jnp.asarray(drawn.astype(out[name].dtype))
    for name, factor in factors.items():
        out[name] = (out[name] * factor).astype(out[name].dtype)
    return out
```

```python
import concourse.bass as bass
from concourse import mybir
from contextlib import ExitStack

FP = mybir.dt.float32
ALU = mybir.AluOpType
ACT = mybir.ActivationFunctionType
AX = mybir.AxisListType

SEQS, STEPS, D = 4, 1024, 128
HEADS, HD = 4, 32
CHUNK = 32
CPW = 4
WSTEPS = CHUNK * CPW
WINDOWS = STEPS // WSTEPS
WTOK = SEQS * WSTEPS
P = 128
EXPERTS, FF = 8, 256
FJ = FF // P
K_CONV, K_SHORT, K_LONG = 4, 3, 31
HALO = K_LONG - 1
RUNS = CPW * SEQS
BLOCKS = SEQS * CPW * HEADS
KH = CHUNK // 2
LN_EPS, L2_EPS, RMS_EPS = 1e-5, 1e-6, 1e-5
FLOOR_MIN, FLOOR_MAX = 0.01, 0.1


class Queue:

    def __init__(self, sem):
        self.sem, self.count, self.waited, self.steps = sem, 0, {}, []

    def wait(self, *tokens):
        for sem, value in tokens:
            if self.waited.get(sem.name, 0) < value:
                self.waited[sem.name] = value
                self.steps.append(lambda eng, s=sem, v=value: eng.wait_ge(s, v))

    def more(self, call):
        self.steps.append(call)

    def do(self, call):
        self.count += 1
        self.steps.append(lambda eng, s=self.sem: call(eng).then_inc(s, 1))
        return (self.sem, self.count)

    def fence(self):
        if self.count:
            self.wait((self.sem, self.count))

    def play(self, eng):
        for step in self.steps:
            step(eng)


class Arrivals:

    def __init__(self, sem):
        self.sem, self.count = sem, 0

    def dma(self, queue, out, in_):
        self.count += 16
        queue.steps.append(lambda eng, s=self.sem: eng.dma_start(out, in_).then_inc(s, 16))
        return (self.sem, self.count)


def layer(nc, hidden, W_q, W_k, W_v, W_b, conv_w_q, conv_w_k, conv_w_v, fir_short_w, fir_long_w,
          W_fuse1, b_fuse1, W_fuse2, b_fuse2, others_log_tau, norm_w, W_o,
          Wgate, bgate, W1, b1, W2, b2, Wg, bg, Wl, bl, W3, b3, out):
    ctx = ExitStack()
    with ctx:
        def sb(name, *shape, dt=FP):
            return ctx.enter_context(nc.sbuf_tensor(name, list(shape), dt))

        def bank(name):
            return ctx.enter_context(nc.psum_tensor(name, [P, 512], FP))

        def sem(name):
            return ctx.enter_context(nc.semaphore(name))

        def arrivals(name):
            return Arrivals(sem(name))

        route_d = nc.dram_tensor("route_d", (2, EXPERTS, WTOK), FP, kind="Internal").ap()
        system_d = nc.dram_tensor("system_d", (2, BLOCKS, CHUNK, CHUNK), FP, kind="Internal").ap()
        inverse_d = nc.dram_tensor("inverse_d", (2, BLOCKS, CHUNK, CHUNK), FP, kind="Internal").ap()

        w_up = sb("w_up", P, EXPERTS, 2, FF)
        w_gl = sb("w_gl", P, EXPERTS, FJ, 2, FF)
        w_dn = sb("w_dn", P, EXPERTS, FJ, D)
        bias_rows = sb("bias_rows", 4 * EXPERTS * FJ + 2, P)
        bias_cols = sb("bias_cols", P, 4 * EXPERTS * FJ + 2)
        b3_sb = sb("b3_sb", EXPERTS, D)
        w_qkv = sb("w_qkv", P, 3, D)
        w_rb = sb("w_rb", P, EXPERTS + HEADS)
        conv_w = sb("conv_w", P, 3, K_CONV)
        short_w = sb("short_w", P, K_SHORT)
        long_w = sb("long_w", P, K_LONG)
        w_f1 = sb("w_f1", P, 4, 2 * D)
        w_f2 = sb("w_f2", P, 2, HEADS * 4)
        w_o = sb("w_o", P, D)
        w_on = sb("w_on", P, D)
        nw_col = sb("nw_col", P, 1)
        bgate_row = sb("bgate_row", P, EXPERTS)
        bf2_row = sb("bf2_row", P, HEADS * 4)
        tau_row = sb("tau_row", P, HEADS)
        inv_tau = sb("inv_tau", P, HEADS)

        ident = sb("ident", P, P)
        block_mask = sb("block_mask", P, P)
        causal_bd = sb("causal_bd", P, P)
        before_bd = sb("before_bd", P, P)
        before = sb("before", P, CHUNK)
        diagonal = sb("diagonal", P, CHUNK)
        earlier8 = sb("earlier8", P, EXPERTS, EXPERTS)
        minus_half = sb("minus_half", P, 16)
        solve_start = sb("solve_start", P, KH, CHUNK)

        xt = [sb(f"xt{n}", P, CPW, D) for n in range(2)]
        stats = sb("stats", P, CPW, 6)
        moments = sb("moments", P, CPW, 2)
        rstd = sb("rstd", P, CPW)
        xf = [sb(f"xf{n}", P, WTOK) for n in range(2)]
        glog = sb("glog", P, CPW, EXPERTS)
        rank = sb("rank", P, CPW * EXPERTS)
        gmax = sb("gmax", P, CPW)
        gsig = sb("gsig", P, 2, CPW, EXPERTS)
        gsum = sb("gsum", P, CPW)
        route = sb("route", P, CPW, EXPERTS)
        route_T = sb("route_T", EXPERTS, WTOK)
        beta = sb("beta", P, CPW, HEADS)
        beta_mask = sb("beta_mask", P, CPW, HEADS, CHUNK)
        pre = sb("pre", P, RUNS, K_CONV - 1 + CHUNK)
        conv_halo = sb("conv_halo", P, 3, SEQS, K_CONV - 1)
        acc = sb("acc", P, CPW, SEQS, CHUNK)
        gate = sb("gate", P, CPW, SEQS, CHUNK)
        beats, ties = (acc[:].rearrange("p c b i -> p (c b i)")[:, n * 256:(n + 1) * 256]
                       .rearrange("p (c e j) -> p c e j", c=CPW, e=EXPERTS) for n in range(2))
        v_act = [sb(f"v_act{n}", P, RUNS, HALO + CHUNK) for n in range(2)]
        square = sb("square", P, CPW, HEADS, HD)
        sumsq = sb("sumsq", P, CPW, HEADS)
        q_n = square[:].rearrange("p c h e -> p c (h e)")
        k_n = [sb(f"k_n{n}", P, CPW, D) for n in range(2)]
        k_b = [sb(f"k_b{n}", P, CPW, D) for n in range(2)]
        v_b = [sb(f"v_b{n}", P, CPW, D) for n in range(2)]
        q_T = [sb(f"q_T{n}", P, CPW, SEQS, CHUNK) for n in range(2)]
        k_T = sb("k_T", P, CPW, SEQS, CHUNK)
        kq_bd = sb("kq_bd", P, 2, SEQS, 2, HEADS, CHUNK)
        system = sb("system", P, CPW, HEADS, CHUNK)
        local = [sb(f"local{n}", P, CPW, HEADS, CHUNK) for n in range(2)]
        solve_L = sb("solve_L", P, CHUNK, CHUNK)
        solve_T = sb("solve_T", P, KH, CHUNK)
        solve_prod = acc[:].rearrange("p c b i -> p (c b i)")

        inv_bd = sb("inv_bd", P, CPW, HEADS, SEQS, CHUNK)
        kn_bd = [sb(f"kn_bd{n}", P, SEQS, D) for n in range(2)]
        local_bd = [sb(f"local_bd{n}", P, HEADS, SEQS, CHUNK) for n in range(2)]
        state = sb("state", P, SEQS, D)
        u_adj = sb("u_adj", P, D)
        delta = sb("delta", P, CPW, D)
        delta_T = sb("delta_T", P, WTOK)
        fir_s = sb("fir_s", P, CPW, SEQS, CHUNK)
        fir_l = sb("fir_l", P, CPW, SEQS, CHUNK)
        hid = [sb(f"hid{n}", P, WTOK) for n in range(2)]
        u_sb = hid[0][:, :].rearrange("p (c d) -> p c d", c=CPW)
        w_T = hid[1][:, :].rearrange("p (c b i) -> p c b i", c=CPW, b=SEQS)
        lg = sb("lg", P, CPW, HEADS, 4)
        p_raw = sb("p_raw", P, CPW, HEADS)
        p_val = sb("p_val", P, CPW, HEADS)
        p_rest = sb("p_rest", P, CPW, HEADS)
        l3 = sb("l3", P, CPW, HEADS, 3)
        l3max = sb("l3max", P, CPW, HEADS)
        l3sig = sb("l3sig", P, 2, CPW, HEADS, 3)
        l3sum = sb("l3sum", P, CPW, HEADS)
        mix = sb("mix", P, CPW, HEADS, HD)
        mix_part = [sb(f"mix_part{n}", P, CPW, HEADS, HD) for n in range(2)]
        ssq_o = sb("ssq_o", P, CPW, HEADS)
        o_T = mix_part[1][:].rearrange("p c h e -> p (c h e)")
        x_res = sb("x_res", P, CPW, D)
        y_T = [sb(f"y_T{n}", P, WTOK) for n in range(2)]

        up1 = sb("up1", P, WTOK)
        z = [[sb(f"z{e}{j}", P, WTOK) for j in range(FJ)] for e in range(2)]
        sig = [sb(f"sig{n}", P, WTOK) for n in range(2)]
        gated = [sb(f"gated{n}", P, WTOK) for n in range(2)]
        route_bc = [sb(f"route_bc{n}", P, WTOK) for n in range(3)]

        ps_x1, ps_x2, ps_g, ps_l, ps_y = (bank(n) for n in ("ps_x1", "ps_x2", "ps_g", "ps_l", "ps_y"))
        ps_state, ps_a, ps_b = bank("ps_state"), bank("ps_a"), bank("ps_b")

        pe, act, dve, pool = (Queue(sem(n)) for n in ("s_pe", "s_act", "s_dve", "s_pool"))
        sp = Queue(None)
        in_small, in_out = arrivals("in_small"), arrivals("in_out")
        in_expert = [arrivals(f"in_expert{e}") for e in range(EXPERTS)]
        in_x = [arrivals(f"in_x{n}") for n in range(2)]
        in_xres = arrivals("in_xres")
        in_route = [arrivals(f"in_route{n}") for n in range(2)]
        in_route_bc = [arrivals(f"in_route_bc{n}") for n in range(3)]
        in_system, in_solve, in_inverse, in_inv_bd = (
            arrivals(n) for n in ("in_system", "in_solve", "in_inverse", "in_inv_bd"))
        tok = {}

        def had(*keys):
            return [tok[k] for k in keys if k in tok]

        def runs(tile):
            return tile[:].rearrange("p c b i -> p (c b) i")

        def runs_flat(ap):
            return ap.rearrange("p (r i) -> p r i", i=CHUNK)

        def spread_halo(tile, halo):
            return pool.do(lambda g: g.tensor_copy(tile[:, SEQS:, 0:halo], tile[:, 0:RUNS - SEQS, CHUNK:CHUNK + halo]))

        def chunks(tile):
            flat = tile[:].rearrange("p c b i -> p c (b i)")
            return [flat[:, c, :] for c in range(CPW)]

        def over(ap, *shape):
            return ap.to_broadcast(list(shape))

        def heads_bc(ap):
            return over(ap.unsqueeze(3), P, CPW, HEADS, HD)

        def as_heads(ap):
            return ap.rearrange("p (c h e) -> p c h e", c=CPW, h=HEADS)

        def rows_of(b, w):
            return slice(w * WSTEPS, (w + 1) * WSTEPS)

        for b in range(SEQS):
            tok["x", 0] = in_x[0].dma(sp, xt[0][CHUNK * b:CHUNK * b + CHUNK, :, :],
                                      hidden[b, rows_of(b, 0), :].rearrange("(c i) d -> i c d", i=CHUNK))
        nb = EXPERTS * FJ
        loads = [(w_rb[:, 0:EXPERTS], Wgate), (w_rb[:, EXPERTS:], W_b),
                 (bgate_row[:, :], bgate.partition_broadcast(P))]
        loads += [(bias_rows[n * nb:(n + 1) * nb, :], t.rearrange("e (k p) -> (e k) p", p=P))
                  for n, t in enumerate((b1, b2, bg, bl))]
        loads += [(bias_rows[4 * nb:4 * nb + 2, :], b_fuse1.rearrange("(k p) -> k p", p=P))]
        loads += [(w_qkv[:, n, :], t) for n, t in enumerate((W_q, W_k, W_v))]
        loads += [(conv_w[:, n, :], t) for n, t in enumerate((conv_w_q, conv_w_k, conv_w_v))]
        loads += [(b3_sb[:, :], b3), (tau_row[:, :], others_log_tau.partition_broadcast(P)),
                  (bf2_row[:, :], b_fuse2.partition_broadcast(P)),
                  (short_w[:, :], fir_short_w.rearrange("h e k -> (h e) k")),
                  (long_w[:, :], fir_long_w.rearrange("h e k -> (h e) k")),
                  (w_f1[:, :, :], W_fuse1.rearrange("(k p) n -> p k n", p=P)),
                  (w_f2[:, :, :], W_fuse2.rearrange("(k p) n -> p k n", p=P)), (w_o[:, :], W_o)]
        loads += [(nw_col[HD * h:HD * h + HD, :], norm_w.rearrange("(e a) -> e a", a=1)) for h in range(HEADS)]
        for dst, src in loads:
            tok["small"] = in_small.dma(sp, dst, src)
        for e in range(EXPERTS):
            for dst, src in ((w_up[:, e, 0, :], W1[e]), (w_up[:, e, 1, :], W2[e]),
                             (w_gl[:, e, :, 0, :], Wg[e].rearrange("(k p) n -> p k n", p=P)),
                             (w_gl[:, e, :, 1, :], Wl[e].rearrange("(k p) n -> p k n", p=P)),
                             (w_dn[:, e, :, :], W3[e].rearrange("(k p) n -> p k n", p=P))):
                tok["expert", e] = in_expert[e].dma(sp, dst, src)

        pool.do(lambda g: g.memset(ident[:, :], 0.0))
        pool.do(lambda g: g.memset(causal_bd[:, :], 1.0))
        pool.do(lambda g: g.memset(before_bd[:, :], 1.0))
        pool.do(lambda g: g.memset(earlier8[:, :, :], 1.0))
        pool.do(lambda g: g.memset(solve_start[:, :, :], 0.0))
        pool.do(lambda g: g.memset(block_mask[:, :], 0.0))
        filled = pool.do(lambda g: g.memset(minus_half[:, :], -0.5))
        pool.wait(filled)
        tok["ident"] = pool.do(lambda g: g.affine_select(
            out=ident[:, :], in_=ident[:, :], compare_op=ALU.not_equal, fill=1.0, base=0,
            pattern=[[-1, P]], channel_multiplier=1))
        pool.do(lambda g: g.affine_select(
            out=causal_bd[:, :], in_=causal_bd[:, :], compare_op=ALU.is_ge, fill=0.0, base=0,
            pattern=[[1, P]], channel_multiplier=-1))
        pool.do(lambda g: g.affine_select(
            out=before_bd[:, :], in_=before_bd[:, :], compare_op=ALU.is_gt, fill=0.0, base=0,
            pattern=[[-1, P]], channel_multiplier=1))
        pool.do(lambda g: g.affine_select(
            out=earlier8[:, :, :], in_=earlier8[:, :, :], compare_op=ALU.is_gt, fill=0.0, base=0,
            pattern=[[1, EXPERTS], [-1, EXPERTS]], channel_multiplier=0))
        for half in range(2):
            part = solve_start[64 * half:64 * half + 64, :, :]
            pool.fence()
            pool.do(lambda g, part=part, half=half: g.affine_select(
                out=part, in_=part, compare_op=ALU.not_equal, fill=1.0, base=KH * half,
                pattern=[[1, KH], [-1, CHUNK]], channel_multiplier=0))
        for h in range(HEADS):
            pool.fence()
            masks = pool.do(lambda g, h=h: g.memset(block_mask[HD * h:HD * h + HD, HD * h:HD * h + HD], 1.0))
        pool.wait(masks)
        pool.do(lambda g: g.tensor_tensor(causal_bd[:, :], causal_bd[:, :], block_mask[:, :], ALU.mult))
        tok["masks"] = pool.do(lambda g: g.tensor_tensor(before_bd[:, :], before_bd[:, :], block_mask[:, :], ALU.mult))
        for t in (conv_halo, v_act[1], kq_bd, kn_bd[0], kn_bd[1], inv_bd, state):
            flat = t[:].rearrange({3: "p a b -> p (a b)", 4: "p a b c -> p (a b c)", 5: "p a b c d -> p (a b c d)",
                                   6: "p a b c d e -> p (a b c d e)"}[len(t.shape)])
            tok["zeroed"] = pool.do(lambda g, flat=flat: g.memset(flat, 0.0))
        dve.wait(tok["masks"])
        dve.do(lambda v: v.tensor_reduce(before[:, :], before_bd[:, :].rearrange("p (b j) -> p j b", b=SEQS),
                                         AX.X, ALU.add))
        tok["diag"] = dve.do(lambda v: v.tensor_reduce(
            diagonal[:, :], ident[:, :].rearrange("p (b j) -> p j b", b=SEQS), AX.X, ALU.add))

        act.wait(tok["small"])
        tok["inv_tau"] = act.do(lambda a: a.activation(inv_tau[:, :], tau_row[:, :], ACT.Exp, scale=-1.0))
        dve.wait(tok["small"])
        tok["w_on"] = dve.do(lambda v: v.tensor_scalar(w_on[:, :], w_o[:, :], nw_col[:, 0:1], None, ALU.mult))
        pe.wait(tok["small"], tok["ident"])
        nrows = 4 * nb + 2
        tok["bias_ps"] = pe.do(lambda t: t.transpose(ps_b[:, 0:nrows], bias_rows[:, :], ident[0:nrows, 0:nrows]))
        act.wait(tok["bias_ps"])
        tok["bias"] = act.do(lambda a: a.activation(bias_cols[:, :], ps_b[:, 0:nrows], ACT.Copy))
        tok["ps_b free"] = tok["bias"]

        def bias_of(n, e, j):
            c = n * nb + e * FJ + j
            return bias_cols[:, c:c + 1]

        def transposed(eng_tokens, pieces, rows=P):
            pe.wait(*eng_tokens, tok["ident"], *had("ps_a free"))
            for n, piece in enumerate(pieces):
                t = pe.do(lambda t, n=n, piece=piece: t.transpose(ps_a[0:rows, n * P:(n + 1) * P], piece, ident[:, :]))
            return t

        def prepare(w):
            par, x = w % 2, xt[w % 2]
            if w + 1 < WINDOWS:
                sp.wait(*had(("xn T", w - 1)))
                for b in range(SEQS):
                    tok["x", w + 1] = in_x[1 - par].dma(
                        sp, xt[1 - par][CHUNK * b:CHUNK * b + CHUNK, :, :],
                        hidden[b, rows_of(b, w + 1), :].rearrange("(c i) d -> i c d", i=CHUNK))
            dve.wait(tok["x", w])
            for c in range(CPW):
                s = dve.do(lambda v, c=c: v.bn_stats(stats[:, c, :], x[:, c, :]))
            dve.wait(s)
            for c in range(CPW):
                m = dve.do(lambda v, c=c: v.bn_aggr(moments[:, c, :], stats[:, c, :]))
            pool.wait(m)
            r = pool.do(lambda g: g.tensor_scalar(rstd[:, :], moments[:, :, 1], LN_EPS, None, ALU.add))
            pool.wait(r)
            r = pool.do(lambda g: g.tensor_tensor(rstd[:, :], rstd[:, :], minus_half[:, 0:CPW], ALU.pow))
            yield
            dve.wait(r)
            for c in range(CPW):
                n = dve.do(lambda v, c=c: v.tensor_scalar(x[:, c, :], x[:, c, :], moments[:, c, 0:1],
                                                          rstd[:, c:c + 1], ALU.subtract, ALU.mult))
            tok["normed", w] = n
            yield
            tok["xn T", w] = transposed([n], [x[:, c, :] for c in range(CPW)])
            yield
            while w >= 2 and (("ffn read", w - 2) not in tok or ("fuse read", w - 2) not in tok):
                yield
            act.wait(tok["xn T", w], *had(("ffn read", w - 2), ("fuse read", w - 2), ("qkv read", w - 2)))
            tok["xf", w] = tok["ps_a free"] = act.do(lambda a: a.activation(xf[par][:, :], ps_a[:, :], ACT.Copy))
            yield
            pe.wait(tok["xf", w], tok["ps_a free"], tok["small"])
            nr = EXPERTS + HEADS
            for c in range(CPW):
                lgt = pe.do(lambda t, c=c: t.matmul(ps_a[:, c * nr:(c + 1) * nr], xf[par][:, c * P:(c + 1) * P],
                                                    w_rb[:, :], start=True, stop=True))
            yield
            ps = ps_a[:, 0:CPW * nr].rearrange("p (c n) -> p c n", n=nr)
            dve.wait(lgt, tok["small"])
            g = dve.do(lambda v: v.tensor_tensor(
                glog[:, :, :], ps[:, :, 0:EXPERTS], over(bgate_row[:, :].unsqueeze(1), P, CPW, EXPERTS), ALU.add))
            act.wait(g, *had(("v_b", w - 1), ("beta_mask", w - 1), ("k_b", w - 1)))
            tok["beta", w] = tok["ps_a free"] = act.do(
                lambda a: a.activation(beta[:, :, :], ps[:, :, EXPERTS:], ACT.Sigmoid))
            dve.wait(g)
            full = (P, CPW, EXPERTS, EXPERTS)
            other = over(glog[:, :, :].unsqueeze(2), *full)
            own = over(glog[:, :, :].unsqueeze(3), *full)
            dve.do(lambda v: v.tensor_tensor(ties[:, :, :, :], other, own, ALU.is_equal))
            bt = dve.do(lambda v: v.tensor_tensor(beats[:, :, :, :], other, own, ALU.is_gt))
            mx = dve.do(lambda v: v.tensor_reduce(gmax[:, :], glog[:, :, :], AX.X, ALU.max))
            dve.wait(bt, mx)
            d = dve.do(lambda v: v.tensor_tensor(
                glog[:, :, :], glog[:, :, :], over(gmax[:, :].unsqueeze(2), P, CPW, EXPERTS), ALU.subtract))
            t = dve.do(lambda v: v.tensor_tensor(
                ties[:, :, :, :], ties[:, :, :, :], over(earlier8[:, :, :].unsqueeze(1), *full), ALU.mult))
            act.wait(d)
            act.do(lambda a: a.activation(gsig[:, 0, :, :], glog[:, :, :], ACT.Sigmoid))
            sg = act.do(lambda a: a.activation(gsig[:, 1, :, :], glog[:, :, :], ACT.Sigmoid, scale=-1.0))
            dve.wait(t)
            t = dve.do(lambda v: v.tensor_tensor(beats[:, :, :, :], beats[:, :, :, :], ties[:, :, :, :], ALU.add))
            dve.wait(t)
            t = dve.do(lambda v: v.tensor_reduce(
                rank[:, :], beats[:, :, :, :].rearrange("p c e j -> p (c e) j"), AX.X, ALU.add))
            yield
            dve.wait(sg)
            rc = dve.do(lambda v: v.reciprocal(gsig[:, 1, :, :], gsig[:, 1, :, :]))
            dve.wait(rc, t)
            ex = dve.do(lambda v: v.tensor_tensor(gsig[:, 0, :, :], gsig[:, 0, :, :], gsig[:, 1, :, :], ALU.mult))
            dve.wait(ex)
            gv = gsig[:, 0, :, :].rearrange("p c e -> p (c e)")
            ex = dve.do(lambda v: v.scalar_tensor_tensor(gv, rank[:, :], 1.5, gv, ALU.is_lt, ALU.mult))
            dve.wait(ex)
            sm = dve.do(lambda v: v.tensor_reduce(gsum[:, :], gsig[:, 0, :, :], AX.X, ALU.add))
            dve.wait(sm)
            rc = dve.do(lambda v: v.reciprocal(gsum[:, :], gsum[:, :]))
            dve.wait(rc, *had(("route T", w - 1)))
            rt = dve.do(lambda v: v.tensor_tensor(
                route[:, :, :], gsig[:, 0, :, :], over(gsum[:, :].unsqueeze(2), P, CPW, EXPERTS), ALU.mult))
            yield
            tok["route T", w] = transposed([rt], [route[:, c, :] for c in range(CPW)], rows=EXPERTS)
            yield
            while w >= 1 and ("b3", w - 1) not in tok:
                yield
            act.wait(tok["route T", w], *had(("b3", w - 1), ("route_d", w - 1)))
            tok["route_T", w] = tok["ps_a free"] = act.do(
                lambda a: a.activation(route_T[:, :], ps_a[0:EXPERTS, :], ACT.Copy))
            sp.wait(tok["route_T", w], *had(("route_bc last", w - 2)))
            tok["route_d", w] = in_route[par].dma(sp, route_d[par], route_T[:, :])
            yield

        def project(w, n):
            par = w % 2
            pe.wait(tok["xf", w], tok["small"], *had("ps_a free"))
            pr = tok["qkv read", w] = pe.do(lambda t: t.matmul(ps_a[:, :], w_qkv[:, n, :], xf[par][:, :], start=True, stop=True))
            yield
            act.wait(pr, *had("halo kept", "conv"))
            cp = tok["ps_a free"] = act.do(lambda a: a.activation(
                pre[:, :, K_CONV - 1:], runs_flat(ps_a[:, :]), ACT.Copy))
            pool.wait(tok["zeroed"], *had("conv"))
            hl = pool.do(lambda g: g.tensor_copy(pre[:, 0:SEQS, 0:K_CONV - 1], conv_halo[:, n, :, :]))
            pool.wait(cp, hl)
            hl = spread_halo(pre, K_CONV - 1)
            tok["halo kept"] = pool.do(lambda g: g.tensor_copy(conv_halo[:, n, :, :], pre[:, RUNS - SEQS:, CHUNK:]))
            yield
            dve.wait(cp, hl, tok["small"], *had("silu"))
            for k in range(K_CONV):
                if k == 0:
                    c = dve.do(lambda v: v.tensor_scalar(runs(acc), pre[:, :, 0:CHUNK], conv_w[:, n, 0:1], None, ALU.mult))
                else:
                    dve.wait(c)
                    c = dve.do(lambda v, k=k: v.scalar_tensor_tensor(
                        runs(acc), pre[:, :, k:k + CHUNK], conv_w[:, n, k:k + 1], runs(acc), ALU.mult, ALU.add))
                if k % 2:
                    yield
            tok["conv"] = c
            act.wait(c, *had("silu", "qk T", ("v act", w - 1)))
            sg = act.do(lambda a: a.activation(gate[:, :, :, :], acc[:, :, :, :], ACT.Sigmoid))
            yield
            dve.wait(sg)
            tok["silu"] = dve.do(lambda v: v.tensor_tensor(gate[:, :, :, :], acc[:, :, :, :], gate[:, :, :, :], ALU.mult))
            yield

        def normed(w, dst, last_reader):
            t = tok["qk T"] = transposed([tok["silu"]], chunks(gate))
            yield
            act.wait(t, *had("sumsq", ("q_n T", w)))
            sq = act.do(lambda a: a.activation(square[:].rearrange("p c h e -> p (c h e)"), ps_a[:, :], ACT.Square))
            yield
            dve.wait(sq, *had("rnorm read"))
            s = tok["sumsq"] = dve.do(lambda v: v.tensor_reduce(sumsq[:, :, :], square[:, :, :, :], AX.X, ALU.add))
            flat = sumsq[:, :, :].rearrange("p c h -> p (c h)")
            pool.wait(s)
            a = pool.do(lambda g: g.tensor_scalar(flat, flat, L2_EPS, None, ALU.add))
            pool.wait(a)
            r = pool.do(lambda g: g.tensor_tensor(flat, flat, minus_half[:, :], ALU.pow))
            yield
            dve.wait(r, *had(*last_reader))
            tok["rnorm read"] = tok["ps_a free"] = tok["normed qk"] = dve.do(
                lambda v: v.tensor_tensor(dst[:, :, :].rearrange("p c (h e) -> p c h e", h=HEADS), as_heads(ps_a[:, :]), heads_bc(sumsq[:, :, :]), ALU.mult))
            yield

        def attend(w):
            par = w % 2
            yield from project(w, 0)
            yield from normed(w, q_n, [("q_n T", w - 1)])
            tok["q_n T", w] = transposed([tok["normed qk"]], [q_n[:, c, :] for c in range(CPW)])
            yield
            while w >= 2 and ("recurred", w - 2) not in tok:
                yield
            act.wait(tok["q_n T", w], *had(("recurred", w - 2)))
            tok["q_T", w] = tok["ps_a free"] = act.do(
                lambda a: a.activation(q_T[par][:].rearrange("p c b i -> p (c b i)"), ps_a[:, :], ACT.Copy))
            yield from project(w, 1)
            yield from normed(w, k_n[par], [("recurred", w - 2)])
            kt = transposed([tok["normed qk"]], [k_n[par][:, c, :] for c in range(CPW)])
            pool.wait(tok["normed qk"], tok["beta", w], *had(("recurred", w - 2)))
            tok["k_b", w] = pool.do(lambda g: g.tensor_tensor(
                as_heads(k_b[par][:, :, :].rearrange("p c d -> p (c d)")),
                as_heads(k_n[par][:, :, :].rearrange("p c d -> p (c d)")), heads_bc(beta[:, :, :]), ALU.mult))
            pool.wait(tok["diag"], *had(("system", w - 1)))
            tok["beta_mask", w] = pool.do(lambda g: g.tensor_tensor(
                beta_mask[:, :, :, :], heads_bc(beta[:, :, :]),
                over(before[:, :].unsqueeze(1), P, CPW * HEADS, CHUNK).rearrange("p (c h) j -> p c h j", c=CPW), ALU.mult))
            yield
            act.wait(kt, *had(("products", w - 1), ("kq_bd", w - 1)))
            kT = tok["ps_a free"] = act.do(lambda a: a.activation(k_T[:].rearrange("p c b i -> p (c b i)"), ps_a[:, :], ACT.Copy))
            yield
            for pair in range(CPW // 2):
                c0 = 2 * pair
                pool.wait(kT, tok["q_T", w], tok["zeroed"], *had("products"))
                act.wait(kT, *had("products"), tok["zeroed"])
                for h in range(HEADS):
                    rows = slice(HD * h, HD * h + HD)
                    pool.fence()
                    cq = pool.do(lambda g, h=h, rows=rows, c0=c0: g.tensor_copy(
                        kq_bd[rows, :, :, 1, h, :].rearrange("p c b i -> p (c b) i"),
                        q_T[par][rows, c0:c0 + 2, :, :].rearrange("p c b i -> p (c b) i")))
                    ck = act.do(lambda a, h=h, rows=rows, c0=c0: a.activation(
                        kq_bd[rows, :, :, 0, h, :].rearrange("p c b i -> p (c b) i"),
                        k_T[rows, c0:c0 + 2, :, :].rearrange("p c b i -> p (c b) i"), ACT.Copy))
                pool.fence()
                tok["kq_bd", w] = cq
                yield
                pe.wait(kT, cq, ck, *had("ps_a free"))
                for c in range(2):
                    for b in range(SEQS):
                        pr = pe.do(lambda t, c=c, b=b, c0=c0: t.matmul(
                            ps_a[CHUNK * b:CHUNK * b + CHUNK, c * 256:(c + 1) * 256], k_T[:, c0 + c, b, :],
                            kq_bd[:, c, b, :, :, :].rearrange("p s h i -> p (s h i)"), start=True, stop=True,
                            tile_position=(0, CHUNK * b)))
                tok["products"] = tok["products", w] = pr
                yield
                ps = ps_a[:, :].rearrange("p (c s h i) -> p c s h i", c=2, s=2, h=HEADS)
                dve.wait(pr, tok["beta_mask", w], *had(("system_d", w - 1)))
                for c in range(2):
                    L = dve.do(lambda v, c=c, c0=c0: v.tensor_tensor(
                        system[:, c0 + c, :, :], ps[:, c, 0], beta_mask[:, c0 + c, :, :], ALU.mult))
                act.wait(L, *had(("recurred", w - 2)))
                tok["local", w] = tok["ps_a free"] = act.do(lambda a, c0=c0: a.activation(
                    local[par][:, c0:c0 + 2, :, :].rearrange("p c h i -> p c (h i)"),
                    ps_a[:, :].rearrange("p (c s n) -> p c s n", c=2, s=2)[:, :, 1, :], ACT.Copy))
                yield
            pool.wait(L)
            flat = system[:].rearrange("p c h j -> p (c h) j")
            tok["system", w] = pool.do(lambda g: g.tensor_tensor(
                flat, flat, over(diagonal[:, :].unsqueeze(1), P, CPW * HEADS, CHUNK), ALU.subtract))
            sp.wait(tok["system", w], *had(("solve in", w - 2)))
            for b in range(SEQS):
                n0 = b * CPW * HEADS
                tok["system_d", w] = in_system.dma(
                    sp, system_d[par, n0:n0 + CPW * HEADS].rearrange("n i j -> i n j"),
                    flat[CHUNK * b:CHUNK * b + CHUNK])
            sp.wait(tok["system_d", w], *had(("solved", w - 1)))
            for half in range(2):
                tok["solve in", w] = in_solve.dma(
                    sp, solve_L[64 * half:64 * half + 64, :, :], system_d[par])
            yield from project(w, 2)
            while w >= 2 and ("v again", w - 2) not in tok:
                yield
            pool.wait(tok["silu"], tok["zeroed"], *had(("fir", w - 2), ("v again", w - 2), ("v act", w - 1)))
            pool.do(lambda g: g.tensor_copy(v_act[par][:, 0:SEQS, 0:HALO], v_act[1 - par][:, RUNS - SEQS:, CHUNK:]))
            vc = pool.do(lambda g: g.tensor_copy(v_act[par][:, :, HALO:], runs(gate)))
            pool.wait(vc)
            tok["v act", w] = spread_halo(v_act[par], HALO)
            vt = tok["qk T"] = transposed([tok["silu"]], chunks(gate))
            yield
            dve.wait(vt, tok["beta", w], *had(("recurred", w - 2)))
            tok["v_b", w] = tok["ps_a free"] = dve.do(lambda v: v.tensor_tensor(
                as_heads(v_b[par][:, :, :].rearrange("p c d -> p (c d)")), as_heads(ps_a[:, :]), heads_bc(beta[:, :, :]), ALU.mult))
            yield
            act.wait(*had(("inverse_d", w - 1)), tok["ident"])
            pool.wait(masks)
            st = act.do(lambda a: a.activation(solve_T[:, :, :], solve_start[:, :, :], ACT.Copy))
            dve.wait(tok["solve in", w], st)
            last = st
            for i in range(1, CHUNK):
                k = min(i, KH)
                prod = solve_prod[:, 0:k * (i + 1)].rearrange("p (k j) -> p k j", k=k)
                dve.wait(last)
                m = dve.do(lambda v, i=i, k=k, prod=prod: v.tensor_tensor(
                    prod, solve_T[:, 0:k, 0:i + 1], over(solve_L[:, i, 0:i + 1].unsqueeze(1), P, k, i + 1), ALU.mult))
                if i % 4 == 0:
                    yield
                dve.wait(m)
                last = dve.do(lambda v, i=i, k=k, prod=prod: v.tensor_reduce(
                    solve_T[:, 0:k, i], prod, AX.X, ALU.add, negate=True))
                if i > 16 or i % 2:
                    yield
            tok["solved", w] = last
            sp.wait(last, *had(("inv_bd", w - 2)))
            for half in range(2):
                tok["inverse_d", w] = in_inverse.dma(
                    sp, inverse_d[par, :, KH * half:KH * half + KH, :], solve_T[64 * half:64 * half + 64, :, :])
            yield

        def filters(w):
            par = w % 2
            while ("v act", w) not in tok:
                yield
            while w >= 1 and ("fir T", w - 1) not in tok:
                yield
            v = v_act[par]
            dve.wait(tok["v act", w], tok["small"], *had(("fir T", w - 1), ("fuse read", w - 1)))

            def tap(queue, dst, weights, taps, k, first):
                src = v[:, :, HALO - taps + 1 + k:HALO - taps + 1 + k + CHUNK]
                if first:
                    return queue.do(lambda e: e.tensor_scalar(runs(dst), src, weights[:, k:k + 1], None, ALU.mult))
                return queue.do(lambda e: e.scalar_tensor_tensor(
                    runs(dst), src, weights[:, k:k + 1], runs(dst), ALU.mult, ALU.add))

            taps = [(fir_s, short_w, K_SHORT, k) for k in range(K_SHORT)]
            taps += [(fir_l, long_w, K_LONG, k) for k in range(K_LONG)]
            d = None
            for dst, weights, n, k in taps:
                if d:
                    dve.wait(d)
                d = tap(dve, dst, weights, n, k, k == 0)
                yield
            tok["fir", w] = d

        def transposed_b(tokens, pieces):
            pe.wait(*tokens, *had("ps_b free"))
            for n, piece in enumerate(pieces):
                t = pe.do(lambda t, n=n, piece=piece: t.transpose(ps_b[:, n * P:(n + 1) * P], piece, ident[:, :]))
            return t

        def finish(w):
            par = w % 2
            while ("inverse_d", w) not in tok:
                yield
            sp.wait(tok["inverse_d", w], tok["zeroed"], *had(("w_T ps", w - 1)))
            for b in range(SEQS):
                n0 = b * CPW * HEADS
                tok["inv_bd", w] = in_inv_bd.dma(
                    sp, inv_bd[CHUNK * b:CHUNK * b + CHUNK, :, :, b, :].rearrange("p c h i -> p (c h) i"),
                    inverse_d[par, n0:n0 + CPW * HEADS].rearrange("n k i -> k n i"))
            yield
            yield
            pe.wait(tok["inv_bd", w], tok["v_b", w], tok["k_b", w], *had("ps_b free"))
            for c in range(CPW):
                for h in range(HEADS):
                    cols = slice(HD * h, HD * h + HD)
                    u = pe.do(lambda t, c=c, h=h, cols=cols: t.matmul(
                        ps_b[:, c * D + HD * h:c * D + HD * h + HD],
                        inv_bd[:, c, h, :, :].rearrange("p b i -> p (b i)"), v_b[par][:, c, cols], start=True, stop=True))
            yield
            act.wait(u, *had(("fuse2", w - 1)))
            uc = tok["ps_b free"] = act.do(lambda a: a.activation(u_sb[:].rearrange("p c d -> p (c d)"), ps_b[:, :], ACT.Copy))
            yield
            pe.wait(uc)
            for c in range(CPW):
                for h in range(HEADS):
                    cols = slice(HD * h, HD * h + HD)
                    wt = pe.do(lambda t, c=c, h=h, cols=cols: t.matmul(
                        ps_b[cols, c * P:(c + 1) * P], k_b[par][:, c, cols],
                        inv_bd[:, c, h, :, :].rearrange("p b i -> p (b i)"), start=True, stop=True,
                        tile_position=(0, HD * h)))
                if c % 2:
                    yield
            tok["w_T ps", w] = wt
            act.wait(wt, *had(("recurred", w - 1), ("fuse2", w - 1)))
            wc = tok["ps_b free"] = act.do(lambda a: a.activation(w_T[:].rearrange("p c b i -> p (c b i)"), ps_b[:, :], ACT.Copy))
            yield
            for c in range(CPW):
                last_chunk = w == WINDOWS - 1 and c == CPW - 1
                cp = (w * CPW + c) % 2
                act.wait(tok["zeroed"], *had(("state ps", cp)))
                for b in range(SEQS):
                    rows = slice(CHUNK * b, CHUNK * b + CHUNK)
                    kd = act.do(lambda a, b=b, rows=rows, c=c, cp=cp: a.activation(
                        kn_bd[cp][rows, b, :], k_n[par][rows, c, :], ACT.Copy))
                dve.wait(tok["local", w], tok["masks"], *had(("local read", cp)))
                ld = dve.do(lambda v, c=c, cp=cp: v.tensor_tensor(
                    local_bd[cp][:, :, :, :], over(local[par][:, c, :, :].unsqueeze(2), P, HEADS, SEQS, CHUNK),
                    over(causal_bd[:, :].rearrange("p (b i) -> p b i", b=SEQS).unsqueeze(1), P, HEADS, SEQS, CHUNK), ALU.mult))
                pe.wait(wc, tok["q_T", w], tok["zeroed"], *had("ps_b free", "state"))
                for b in range(SEQS):
                    rows = slice(CHUNK * b, CHUNK * b + CHUNK)
                    ws = pe.do(lambda t, b=b, rows=rows, c=c: t.matmul(
                        ps_b[rows, 0:D], w_T[:, c, b, :], state[:, b, :], start=True, stop=True, tile_position=(0, CHUNK * b)))
                for b in range(SEQS):
                    rows = slice(CHUNK * b, CHUNK * b + CHUNK)
                    qs = pe.do(lambda t, b=b, rows=rows, c=c: t.matmul(
                        ps_b[rows, D:2 * D], q_T[par][:, c, b, :], state[:, b, :], start=True, stop=False,
                        tile_position=(0, CHUNK * b), skip_group_check=True))
                yield
                dve.wait(qs, *had("u_adj read"))
                ua = dve.do(lambda v, c=c: v.tensor_tensor(u_adj[:, :], u_sb[:, c, :], ps_b[:, 0:D], ALU.subtract))
                yield
                pe.wait(ua, kd, ld)
                if not last_chunk:
                    for b in range(SEQS):
                        sps = pe.do(lambda t, b=b, cp=cp, first=(w == 0 and c == 0 and b == 0): t.matmul(
                            ps_state[:, b * D:(b + 1) * D], kn_bd[cp][:, b, :], u_adj[:, :], start=first, stop=True,
                            skip_group_check=True))
                    tok["state ps", cp] = sps
                for h in range(HEADS):
                    cols = slice(HD * h, HD * h + HD)
                    lo = pe.do(lambda t, h=h, cols=cols, cp=cp: t.matmul(
                        ps_b[:, D + HD * h:D + HD * h + HD], local_bd[cp][:, h, :, :].rearrange("p b i -> p (b i)"),
                        u_adj[:, cols], start=False, stop=True, skip_group_check=True))
                tok["u_adj read"] = tok["local read", cp] = lo
                yield
                if not last_chunk:
                    dve.wait(sps)
                    tok["state"] = dve.do(lambda v: v.tensor_tensor(
                        state[:, :, :], ps_state[:, :].rearrange("p (b n) -> p b n", b=SEQS),
                        over(block_mask[:, :].unsqueeze(1), P, SEQS, D), ALU.mult))
                act.wait(lo, *had(("mixed", w - 1)))
                dl = tok["ps_b free"] = act.do(lambda a, c=c: a.activation(delta[:, c, :], ps_b[:, D:2 * D], ACT.Copy))
                if c == CPW - 1:
                    tok["recurred", w] = lo
                yield
            t = transposed_b([dl], [delta[:, c, :] for c in range(CPW)])
            yield
            act.wait(t, *had(("fuse read", w - 1), ("v mixed", w - 1)))
            dT = tok["ps_b free"] = act.do(lambda a: a.activation(delta_T[:, :], ps_b[:, :], ACT.Copy))
            yield
            while ("fir", w) not in tok:
                yield
            for m in range(2):
                pe.wait(dT, tok["fir", w], tok["xf", w], tok["ps_b free"])
                rhs = [xf[par][:, :], fir_s[:].rearrange("p c b i -> p (c b i)"),
                       fir_l[:].rearrange("p c b i -> p (c b i)"), delta_T[:, :]]
                for k in range(4):
                    f = pe.do(lambda t, k=k, m=m, r=rhs[k]: t.matmul(
                        ps_b[:, :], w_f1[:, k, m * P:(m + 1) * P], r,
                        start=k == 0, stop=k == 3))
                    if k % 2:
                        yield
                act.wait(f, tok["bias"])
                hp = tok["ps_b free"] = act.do(lambda a, m=m: a.activation(
                    hid[m][:, :], ps_b[:, :], ACT.Identity, bias=bias_cols[:, 4 * nb + m:4 * nb + m + 1]))
                yield
            act.wait(hp)
            for m in range(2):
                tok["hid"] = act.do(lambda a, m=m: a.activation(hid[m][:, :], hid[m][:, :], ACT.Gelu))
            yield
            tok["fuse read", w] = f
            pe.wait(tok["hid"], *had("ps_b free"))
            for c in range(CPW):
                for m in range(2):
                    f2 = pe.do(lambda t, c=c, m=m: t.matmul(
                        ps_b[:, c * 16:(c + 1) * 16], hid[m][:, c * P:(c + 1) * P], w_f2[:, m, :], start=m == 0, stop=m == 1))
            tok["fuse2", w] = f2
            yield
            dve.wait(f2, *had("p used"))
            l = tok["ps_b free"] = dve.do(lambda v: v.tensor_tensor(
                lg[:].rearrange("p c h k -> p c (h k)"), ps_b[:, 0:CPW * 16].rearrange("p (c n) -> p c n", n=16),
                over(bf2_row[:, :].unsqueeze(1), P, CPW, 16), ALU.add))
            act.wait(l)
            s = act.do(lambda a: a.activation(p_raw[:, :, :], lg[:, :, :, 3], ACT.Sigmoid))
            dve.wait(l, tok["inv_tau"])
            l = dve.do(lambda v: v.tensor_tensor(
                l3[:, :, :, :], lg[:, :, :, 0:3],
                over(inv_tau[:, :].unsqueeze(1).unsqueeze(3), P, CPW, HEADS, 3), ALU.mult))
            dve.wait(l)
            l = dve.do(lambda v: v.tensor_reduce(l3max[:, :, :], l3[:, :, :, :], AX.X, ALU.max))
            dve.wait(l)
            l = dve.do(lambda v: v.tensor_tensor(
                l3[:, :, :, :], l3[:, :, :, :], over(l3max[:, :, :].unsqueeze(3), P, CPW, HEADS, 3), ALU.subtract))
            act.wait(l)
            act.do(lambda a: a.activation(l3sig[:, 0], l3[:, :, :, :], ACT.Sigmoid))
            sg = act.do(lambda a: a.activation(l3sig[:, 1], l3[:, :, :, :], ACT.Sigmoid, scale=-1.0))
            dve.wait(s)
            a1 = dve.do(lambda v: v.tensor_scalar(p_val[:, :, :], p_raw[:, :, :], FLOOR_MAX - FLOOR_MIN, 1.0 - FLOOR_MAX, ALU.mult, ALU.add))
            dve.wait(a1)
            a1 = dve.do(lambda v: v.tensor_tensor(p_val[:, :, :], p_val[:, :, :], p_raw[:, :, :], ALU.mult))
            dve.wait(a1)
            a1 = dve.do(lambda v: v.tensor_scalar(p_rest[:, :, :], p_val[:, :, :], -1.0, 1.0, ALU.mult, ALU.add))
            yield
            dve.wait(sg)
            r = dve.do(lambda v: v.reciprocal(l3sig[:, 1], l3sig[:, 1]))
            dve.wait(r)
            r = dve.do(lambda v: v.tensor_tensor(l3sig[:, 0], l3sig[:, 0], l3sig[:, 1], ALU.mult))
            dve.wait(r)
            r = dve.do(lambda v: v.tensor_reduce(l3sum[:, :, :], l3sig[:, 0], AX.X, ALU.add))
            dve.wait(r)
            r = dve.do(lambda v: v.reciprocal(l3sum[:, :, :], l3sum[:, :, :]))
            dve.wait(r, a1)
            r = dve.do(lambda v: v.tensor_tensor(l3sum[:, :, :], l3sum[:, :, :], p_rest[:, :, :], ALU.mult))
            dve.wait(r)
            pc = dve.do(lambda v: v.tensor_tensor(
                l3[:, :, :, :], l3sig[:, 0], over(l3sum[:, :, :].unsqueeze(3), P, CPW, HEADS, 3), ALU.mult))
            yield
            t = transposed_b([], chunks(fir_s))
            pool.wait(pc, dl, *had(("mixed", w - 1), ("out ps", w - 1)))
            m2 = pool.do(lambda g: g.tensor_tensor(
                mix_part[1][:, :, :, :], as_heads(delta[:].rearrange("p c d -> p (c d)")), heads_bc(l3[:, :, :, 2]), ALU.mult))
            yield
            dve.wait(t, pc, *had(("o_T ps", w - 1)))
            m0 = tok["ps_b free"] = dve.do(lambda v: v.tensor_tensor(
                mix[:, :, :, :], as_heads(ps_b[:, :]), heads_bc(l3[:, :, :, 0]), ALU.mult))
            yield
            t = tok["fir T", w] = transposed_b([], chunks(fir_l))
            pool.wait(m0, m2)
            s = pool.do(lambda g: g.tensor_tensor(mix[:, :, :, :], mix[:, :, :, :], mix_part[1][:, :, :, :], ALU.add))
            yield
            dve.wait(t)
            m1 = tok["ps_b free"] = dve.do(lambda v: v.tensor_tensor(
                mix_part[0][:, :, :, :], as_heads(ps_b[:, :]), heads_bc(l3[:, :, :, 1]), ALU.mult))
            pool.wait(m1, s)
            s = pool.do(lambda g: g.tensor_tensor(mix[:, :, :, :], mix[:, :, :, :], mix_part[0][:, :, :, :], ALU.add))
            yield
            pool.wait(tok["fuse read", w])
            vc = tok["v again", w] = pool.do(lambda g: g.tensor_copy(
                runs_flat(delta_T[:, :]), v_act[par][:, :, HALO:]))
            yield
            t = tok["v mixed", w] = transposed_b([vc], [delta_T[:, c * P:(c + 1) * P] for c in range(CPW)])
            yield
            dve.wait(t, s)
            m1 = tok["ps_b free"] = tok["p used"] = dve.do(lambda v: v.tensor_tensor(
                mix_part[1][:, :, :, :], as_heads(ps_b[:, :]), heads_bc(p_val[:, :, :]), ALU.mult))
            dve.wait(m1)
            s = tok["mixed", w] = dve.do(lambda v: v.tensor_tensor(mix[:, :, :, :], mix[:, :, :, :], mix_part[1][:, :, :, :], ALU.add))
            act.wait(s)
            s = act.do(lambda a: a.activation(mix_part[0][:, :, :, :], mix[:, :, :, :], ACT.Square))
            yield
            dve.wait(s)
            s = dve.do(lambda v: v.tensor_reduce(ssq_o[:, :, :], mix_part[0][:, :, :, :], AX.X, ALU.add))
            pool.wait(s)
            flat = ssq_o[:, :, :].rearrange("p c h -> p (c h)")
            s = pool.do(lambda g: g.tensor_scalar(flat, flat, 1.0 / HD, RMS_EPS, ALU.mult, ALU.add))
            pool.wait(s)
            s = pool.do(lambda g: g.tensor_tensor(flat, flat, minus_half[:, :], ALU.pow))
            pool.wait(s)
            s = tok["mixed", w] = pool.do(lambda g: g.tensor_tensor(
                mix[:, :, :, :], mix[:, :, :, :], heads_bc(ssq_o[:, :, :]), ALU.mult))
            yield
            sp.wait(*had(("stored", w - 1)))
            for b in range(SEQS):
                tok["x_res", w] = in_xres.dma(sp, x_res[CHUNK * b:CHUNK * b + CHUNK, :, :],
                                              hidden[b, rows_of(b, w), :].rearrange("(c i) d -> i c d", i=CHUNK))
            yield
            t = tok["o_T ps", w] = transposed_b([s], [mix[:, c, :, :].rearrange("p h e -> p (h e)") for c in range(CPW)])
            yield
            act.wait(t, *had(("out ps", w - 1)))
            oT = tok["ps_b free"] = act.do(lambda a: a.activation(o_T, ps_b[:, :], ACT.Copy))
            yield
            while ("y_T", w) not in tok:
                yield
            pe.wait(oT, tok["y_T", w], tok["w_on"])
            for c in range(CPW):
                pe.do(lambda t, c=c: t.matmul(ps_b[:, c * D:(c + 1) * D], o_T[:, c * P:(c + 1) * P], w_on[:, :], start=True, stop=False))
                t = pe.do(lambda t, c=c: t.matmul(ps_b[:, c * D:(c + 1) * D], y_T[par][:, c * P:(c + 1) * P], ident[:, :], start=False, stop=True))
            tok["out ps", w] = t
            yield
            dve.wait(t, tok["x_res", w])
            s = tok["summed", w] = tok["ps_b free"] = dve.do(lambda v: v.tensor_tensor(
                x_res[:].rearrange("p c d -> p (c d)"), ps_b[:, :], x_res[:].rearrange("p c d -> p (c d)"), ALU.add))
            sp.wait(s)
            for b in range(SEQS):
                tok["stored", w] = in_out.dma(
                    sp, out[b, rows_of(b, w), :].rearrange("(c i) d -> i c d", i=CHUNK), x_res[CHUNK * b:CHUNK * b + CHUNK, :, :])
            yield

        def load_route(w, e):
            slot = (w * EXPERTS + e) % 3
            while ("route_d", w) not in tok:
                yield
            sp.wait(tok["route_d", w], *had(("sigc", slot)))
            tok["route_bc", w, e] = tok["route_bc last", w] = in_route_bc[slot].dma(
                sp, route_bc[slot][:, :], route_d[w % 2, e, :].partition_broadcast(P))

        def up(w, e, j):
            par, cols, zb = w % 2, slice(j * P, (j + 1) * P), z[e % 2][j]
            pe.wait(tok["xf", w], tok["expert", e], *had("up1"))
            x1 = pe.do(lambda t: t.matmul(ps_x1[:, :], w_up[:, e, 0, cols], xf[par][:, :], start=True, stop=True))
            pe.wait(*had("z"))
            x2 = pe.do(lambda t: t.matmul(ps_x2[:, :], w_up[:, e, 1, cols], xf[par][:, :], start=True, stop=True))
            tok["ffn read", w] = x2
            act.wait(x1, tok["bias"], *had("z"))
            a = tok["up1"] = act.do(lambda a: a.activation(up1[:, :], ps_x1[:, :], ACT.Identity, bias=bias_of(0, e, j)))
            dve.wait(a, x2, *had(("z read", e % 2)))
            tok["z"] = tok["z", w, e, j] = dve.do(lambda v: v.scalar_tensor_tensor(
                zb[:, :], ps_x2[:, :], bias_of(1, e, j), up1[:, :], ALU.add, ALU.mult))

        def mid(w, e, j):
            cols, slot = slice(j * P, (j + 1) * P), (w * EXPERTS + e) % 3
            pe.wait(tok["z", w, e, 0], tok["z", w, e, 1], tok["expert", e], *had("t"))
            for k in range(FJ):
                g = pe.do(lambda t, k=k: t.matmul(ps_g[:, :], w_gl[:, e, k, 0, cols], z[e % 2][k][:, :], start=k == 0, stop=k == FJ - 1))
            act.wait(g, *had(("o", j)))
            s = act.do(lambda a: a.activation(sig[j][:, :], ps_g[:, :], ACT.Sigmoid, bias=bias_of(2, e, j)))
            yield
            pe.wait(*had("o"))
            for k in range(FJ):
                l = pe.do(lambda t, k=k: t.matmul(ps_l[:, :], w_gl[:, e, k, 1, cols], z[e % 2][k][:, :], start=k == 0, stop=k == FJ - 1))
            tok["z read", e % 2] = l
            pool.wait(s, tok["route_bc", w, e])
            c = tok["sigc", slot] = pool.do(lambda g: g.tensor_tensor(sig[j][:, :], sig[j][:, :], route_bc[slot][:, :], ALU.mult))
            yield
            dve.wait(c, g)
            t = tok["t"] = dve.do(lambda v: v.scalar_tensor_tensor(
                sig[j][:, :], ps_g[:, :], bias_of(2, e, j), sig[j][:, :], ALU.add, ALU.mult))
            dve.wait(t, l, *had(("y read", j)))
            tok["o"] = tok["o", j] = dve.do(lambda v: v.scalar_tensor_tensor(
                gated[j][:, :], ps_l[:, :], bias_of(3, e, j), sig[j][:, :], ALU.add, ALU.mult))

        def down(w, e, j):
            pe.wait(tok["o", j])
            if e == 0 and j == 0:
                pe.wait(tok["route_T", w], tok["small"], *had(("y_T", w - 1)))
                tok["b3", w] = pe.do(lambda t: t.matmul(ps_y[:, :], b3_sb[:, :], route_T[:, :], start=True, stop=False))
            last = e == EXPERTS - 1 and j == FJ - 1
            tok["y ps"] = tok["y read", j] = pe.do(lambda t: t.matmul(
                ps_y[:, :], w_dn[:, e, j, :], gated[j][:, :], start=False, stop=last))

        def experts():
            order = [(w, e) for w in range(WINDOWS) for e in range(EXPERTS)]

            def y_out(w):
                act.wait(tok["y ps"], *had(("out ps", w - 2)))
                tok["y_T", w] = act.do(lambda a: a.activation(y_T[w % 2][:, :], ps_y[:, :], ACT.Copy))

            def need(w):
                while ("xf", w) not in tok:
                    yield

            for w, e in order[:2]:
                yield from load_route(w, e)
            yield from need(0)
            for j in range(FJ):
                up(0, 0, j)
                yield
            for n, (w, e) in enumerate(order):
                nxt = order[n + 1] if n + 1 < len(order) else None
                if n + 2 < len(order):
                    yield from load_route(*order[n + 2])
                if nxt:
                    yield from need(nxt[0])
                for j in range(FJ):
                    if nxt:
                        up(*nxt, j)
                        yield
                    yield from mid(w, e, j)
                    if j or n:
                        pj, pe_ = (0, (w, e)) if j else (1, order[n - 1])
                        while pe_[0] >= 2 and ("out ps", pe_[0] - 2) not in tok:
                            yield
                        down(*pe_, pj)
                        if not j and pe_[1] == EXPERTS - 1:
                            y_out(pe_[0])
                    yield
            down(*order[-1], 1)
            y_out(WINDOWS - 1)

        def first():
            for w in range(WINDOWS):
                yield from prepare(w)
                yield from attend(w)

        def second():
            for w in range(WINDOWS):
                yield from finish(w)

        def third():
            for w in range(WINDOWS):
                yield from filters(w)

        streams = [experts(), first(), second(), third()]
        while streams:
            for s in list(streams):
                if next(s, "ended") == "ended":
                    streams.remove(s)
        sp.wait(tok["stored", WINDOWS - 1])

        block = ctx.enter_context(nc.Block())

        @block.sync
        def _(eng):
            sp.play(eng)

        @block.gpsimd
        def _(eng):
            pool.play(eng)

        @block.scalar
        def _(eng):
            act.play(eng)

        @block.vector
        def _(eng):
            dve.play(eng)

        @block.tensor
        def _(eng):
            pe.play(eng)


NAMES = ["L0_attn_" + n for n in (
    "hidden_states W_q W_k W_v W_b conv_w_q conv_w_k conv_w_v fir_short_w fir_long_w W_fuse1 b_fuse1 "
    "W_fuse2 b_fuse2 others_log_tau norm_w W_o").split()]
NAMES += ["L0_ffn_" + n for n in "Wgate bgate W1 b1 W2 b2 Wg bg Wl bl W3 b3".split()]


def kernel(**inputs):
    import numpy as np
    import concourse.bacc as bacc
    from concourse.bass_utils import run_bass_kernel_spmd

    nc = bacc.Bacc("TRN2", target_bir_lowering=False, num_devices=1)
    arrays = {n: np.ascontiguousarray(inputs[n]) for n in NAMES}
    aps = [nc.dram_tensor(n, a.shape, mybir.dt.from_np(a.dtype), kind="ExternalInput").ap() for n, a in arrays.items()]
    out = nc.dram_tensor("out", (SEQS, STEPS, D), FP, kind="ExternalOutput").ap()
    layer(nc, *aps, out)
    return run_bass_kernel_spmd(nc, [arrays], core_ids=[0]).results[0]["out"]
```

```python
import concourse.bass as bass
from concourse import mybir
from contextlib import ExitStack

FP = mybir.dt.float32
ALU = mybir.AluOpType
ACT = mybir.ActivationFunctionType
AX = mybir.AxisListType

SEQS, STEPS, D = 4, 1024, 128
HEADS, HD = 4, 32
CHUNK = 32
CPW = 4
WSTEPS = CHUNK * CPW
WINDOWS = STEPS // WSTEPS
WTOK = SEQS * WSTEPS
P = 128
EXPERTS, FF = 8, 256
FJ = FF // P
K_CONV, K_SHORT, K_LONG = 4, 3, 31
HALO = K_LONG - 1
RUNS = CPW * SEQS
BLOCKS = SEQS * CPW * HEADS
KH = CHUNK // 2
LN_EPS, L2_EPS, RMS_EPS = 1e-5, 1e-6, 1e-5
FLOOR_MIN, FLOOR_MAX = 0.01, 0.1


class Queue:

    def __init__(self, sem):
        self.sem, self.count, self.waited, self.steps = sem, 0, {}, []

    def wait(self, *tokens):
        for sem, value in tokens:
            if self.waited.get(sem.name, 0) < value:
                self.waited[sem.name] = value
                self.steps.append(lambda eng, s=sem, v=value: eng.wait_ge(s, v))

    def more(self, call):
        self.steps.append(call)

    def do(self, call):
        self.count += 1
        self.steps.append(lambda eng, s=self.sem: call(eng).then_inc(s, 1))
        return (self.sem, self.count)

    def fence(self):
        if self.count:
            self.wait((self.sem, self.count))

    def play(self, eng):
        for step in self.steps:
            step(eng)


class Arrivals:

    def __init__(self, sem):
        self.sem, self.count = sem, 0

    def dma(self, queue, out, in_):
        self.count += 16
        queue.steps.append(lambda eng, s=self.sem: eng.dma_start(out, in_).then_inc(s, 16))
        return (self.sem, self.count)


class Bank:

    def __init__(self, tile):
        self.tile, self.held, self.read = tile, False, []

    def leave(self, *tokens):
        self.read, self.held = list(tokens), False


def layer(nc, hidden, W_q, W_k, W_v, W_b, conv_w_q, conv_w_k, conv_w_v, fir_short_w, fir_long_w,
          W_fuse1, b_fuse1, W_fuse2, b_fuse2, others_log_tau, norm_w, W_o,
          Wgate, bgate, W1, b1, W2, b2, Wg, bg, Wl, bl, W3, b3, out):
    ctx = ExitStack()
    with ctx:
        def sb(name, *shape, dt=FP):
            return ctx.enter_context(nc.sbuf_tensor(name, list(shape), dt))

        def bank(name):
            return ctx.enter_context(nc.psum_tensor(name, [P, 512], FP))

        def sem(name):
            return ctx.enter_context(nc.semaphore(name))

        def arrivals(name):
            return Arrivals(sem(name))

        route_d = nc.dram_tensor("route_d", (2, EXPERTS, WTOK), FP, kind="Internal").ap()
        system_d = nc.dram_tensor("system_d", (2, BLOCKS, CHUNK, CHUNK), FP, kind="Internal").ap()
        inverse_d = nc.dram_tensor("inverse_d", (2, BLOCKS, CHUNK, CHUNK), FP, kind="Internal").ap()

        w_up = sb("w_up", P, EXPERTS, 2, FF)
        w_gl = sb("w_gl", P, EXPERTS, FJ, 2, FF)
        w_dn = sb("w_dn", P, EXPERTS, FJ, D)
        bias_rows = sb("bias_rows", 4 * EXPERTS * FJ + 2, P)
        bias_cols = sb("bias_cols", P, 4 * EXPERTS * FJ + 2)
        b3_sb = sb("b3_sb", EXPERTS, D)
        w_qkv = sb("w_qkv", P, 3, D)
        w_rb = sb("w_rb", P, EXPERTS + HEADS)
        conv_w = sb("conv_w", P, 3, K_CONV)
        short_w = sb("short_w", P, K_SHORT)
        long_w = sb("long_w", P, K_LONG)
        w_f1 = sb("w_f1", P, 4, 2 * D)
        w_f2 = sb("w_f2", P, 2, HEADS * 4)
        w_o = sb("w_o", P, D)
        w_on = sb("w_on", P, D)
        nw_col = sb("nw_col", P, 1)
        bgate_row = sb("bgate_row", P, EXPERTS)
        bf2_row = sb("bf2_row", P, HEADS * 4)
        tau_row = sb("tau_row", P, HEADS)
        inv_tau = sb("inv_tau", P, HEADS)

        ident = sb("ident", P, P)
        block_mask = sb("block_mask", P, P)
        causal_bd = sb("causal_bd", P, P)
        before_bd = sb("before_bd", P, P)
        before = sb("before", P, CHUNK)
        diagonal = sb("diagonal", P, CHUNK)
        earlier8 = sb("earlier8", P, EXPERTS, EXPERTS)
        minus_half = sb("minus_half", P, 16)
        solve_start = sb("solve_start", P, KH, CHUNK)

        xt = [sb(f"xt{n}", P, CPW, D) for n in range(2)]
        stats = sb("stats", P, CPW, 6)
        moments = sb("moments", P, CPW, 2)
        rstd = sb("rstd", P, CPW)
        xf = [sb(f"xf{n}", P, WTOK) for n in range(2)]
        glog = sb("glog", P, CPW, EXPERTS)
        rank = sb("rank", P, CPW * EXPERTS)
        gmax = sb("gmax", P, CPW)
        gsig = sb("gsig", P, 2, CPW, EXPERTS)
        gsum = sb("gsum", P, CPW)
        route = sb("route", P, CPW, EXPERTS)
        route_T = sb("route_T", EXPERTS, WTOK)
        beta_ring = [sb(f"beta{n}", P, CPW, HEADS) for n in range(2)]
        beta_mask = sb("beta_mask", P, CPW, HEADS, CHUNK)
        pre = sb("pre", P, RUNS, K_CONV - 1 + CHUNK)
        conv_halo = sb("conv_halo", P, 3, SEQS, K_CONV - 1)
        acc = sb("acc", P, CPW, SEQS, CHUNK)
        gate = sb("gate", P, CPW, SEQS, CHUNK)
        beats, ties = (sb(n, P, CPW, EXPERTS, EXPERTS) for n in ("beats", "ties"))
        v_act = [sb(f"v_act{n}", P, RUNS, HALO + CHUNK) for n in range(2)]
        square = sb("square", P, CPW, HEADS, HD)
        sumsq = sb("sumsq", P, CPW, HEADS)
        q_n = square[:].rearrange("p c h e -> p c (h e)")
        k_n = [sb(f"k_n{n}", P, CPW, D) for n in range(2)]
        k_b = [sb(f"k_b{n}", P, CPW, D) for n in range(2)]
        v_b = [sb(f"v_b{n}", P, CPW, D) for n in range(2)]
        q_T = [sb(f"q_T{n}", P, CPW, SEQS, CHUNK) for n in range(2)]
        k_T = sb("k_T", P, CPW, SEQS, CHUNK)
        kq_bd = sb("kq_bd", P, 2, SEQS, 2, HEADS, CHUNK)
        system = sb("system", P, CPW, HEADS, CHUNK)
        local = [sb(f"local{n}", P, CPW, HEADS, CHUNK) for n in range(2)]
        solve_L = sb("solve_L", P, CHUNK, CHUNK)
        solve_T = sb("solve_T", P, KH, CHUNK)
        solve_prod = sb("solve_prod", P, KH * CHUNK)

        inv_bd = sb("inv_bd", P, CPW, HEADS, SEQS, CHUNK)
        kn_bd = [sb(f"kn_bd{n}", P, SEQS, D) for n in range(2)]
        local_bd = [sb(f"local_bd{n}", P, HEADS, SEQS, CHUNK) for n in range(2)]
        state = sb("state", P, SEQS, D)
        u_adj = sb("u_adj", P, D)
        delta = sb("delta", P, CPW, D)
        delta_T = sb("delta_T", P, WTOK)
        fir_s = sb("fir_s", P, CPW, SEQS, CHUNK)
        fir_l = sb("fir_l", P, CPW, SEQS, CHUNK)
        hid = [sb(f"hid{n}", P, WTOK) for n in range(2)]
        u_sb = hid[0][:, :].rearrange("p (c d) -> p c d", c=CPW)
        w_T = hid[1][:, :].rearrange("p (c b i) -> p c b i", c=CPW, b=SEQS)
        lg = sb("lg", P, CPW, HEADS, 4)
        p_raw = sb("p_raw", P, CPW, HEADS)
        p_val = sb("p_val", P, CPW, HEADS)
        p_rest = sb("p_rest", P, CPW, HEADS)
        l3 = sb("l3", P, CPW, HEADS, 3)
        l3max = sb("l3max", P, CPW, HEADS)
        l3sig = sb("l3sig", P, 2, CPW, HEADS, 3)
        l3sum = sb("l3sum", P, CPW, HEADS)
        mix = sb("mix", P, CPW, HEADS, HD)
        mix_part = [sb(f"mix_part{n}", P, CPW, HEADS, HD) for n in range(2)]
        ssq_o = sb("ssq_o", P, CPW, HEADS)
        o_T = mix_part[1][:].rearrange("p c h e -> p (c h e)")
        x_res = sb("x_res", P, CPW, D)
        y_T = [sb(f"y_T{n}", P, WTOK) for n in range(2)]

        up1 = sb("up1", P, WTOK)
        z = [[sb(f"z{e}{j}", P, WTOK) for j in range(FJ)] for e in range(2)]
        sig = [sb(f"sig{n}", P, WTOK) for n in range(2)]
        gated = [sb(f"gated{n}", P, WTOK) for n in range(2)]
        route_bc = [sb(f"route_bc{n}", P, WTOK) for n in range(3)]

        ps_x1, ps_x2, ps_g, ps_l, ps_y = (bank(n) for n in ("ps_x1", "ps_x2", "ps_g", "ps_l", "ps_y"))
        ps_state = bank("ps_state")
        shared = [Bank(bank(f"ps_shared{n}")) for n in range(2)]

        pe, act, dve, pool = (Queue(sem(n)) for n in ("s_pe", "s_act", "s_dve", "s_pool"))
        sp = Queue(None)
        in_small, in_out = arrivals("in_small"), arrivals("in_out")
        in_expert = [arrivals(f"in_expert{e}") for e in range(EXPERTS)]
        in_x = [arrivals(f"in_x{n}") for n in range(2)]
        in_xres = arrivals("in_xres")
        in_route = [arrivals(f"in_route{n}") for n in range(2)]
        in_route_bc = [arrivals(f"in_route_bc{n}") for n in range(3)]
        in_system, in_solve, in_inverse, in_inv_bd = (
            arrivals(n) for n in ("in_system", "in_solve", "in_inverse", "in_inv_bd"))
        tok = {}

        def had(*keys):
            return [tok[k] for k in keys if k in tok]

        def runs(tile):
            return tile[:].rearrange("p c b i -> p (c b) i")

        def runs_flat(ap):
            return ap.rearrange("p (r i) -> p r i", i=CHUNK)

        def spread_halo(tile, halo):
            return pool.do(lambda g: g.tensor_copy(tile[:, SEQS:, 0:halo], tile[:, 0:RUNS - SEQS, CHUNK:CHUNK + halo]))

        def chunks(tile):
            flat = tile[:].rearrange("p c b i -> p c (b i)")
            return [flat[:, c, :] for c in range(CPW)]

        def over(ap, *shape):
            return ap.to_broadcast(list(shape))

        def heads_bc(ap):
            return over(ap.unsqueeze(3), P, CPW, HEADS, HD)

        def as_heads(ap):
            return ap.rearrange("p (c h e) -> p c h e", c=CPW, h=HEADS)

        def rows_of(b, w):
            return slice(w * WSTEPS, (w + 1) * WSTEPS)

        for b in range(SEQS):
            tok["x", 0] = in_x[0].dma(sp, xt[0][CHUNK * b:CHUNK * b + CHUNK, :, :],
                                      hidden[b, rows_of(b, 0), :].rearrange("(c i) d -> i c d", i=CHUNK))
        nb = EXPERTS * FJ
        loads = [(w_rb[:, 0:EXPERTS], Wgate), (w_rb[:, EXPERTS:], W_b),
                 (bgate_row[:, :], bgate.partition_broadcast(P))]
        loads += [(bias_rows[n * nb:(n + 1) * nb, :], t.rearrange("e (k p) -> (e k) p", p=P))
                  for n, t in enumerate((b1, b2, bg, bl))]
        loads += [(bias_rows[4 * nb:4 * nb + 2, :], b_fuse1.rearrange("(k p) -> k p", p=P))]
        loads += [(w_qkv[:, n, :], t) for n, t in enumerate((W_q, W_k, W_v))]
        loads += [(conv_w[:, n, :], t) for n, t in enumerate((conv_w_q, conv_w_k, conv_w_v))]
        loads += [(b3_sb[:, :], b3), (tau_row[:, :], others_log_tau.partition_broadcast(P)),
                  (bf2_row[:, :], b_fuse2.partition_broadcast(P)),
                  (short_w[:, :], fir_short_w.rearrange("h e k -> (h e) k")),
                  (long_w[:, :], fir_long_w.rearrange("h e k -> (h e) k")),
                  (w_f1[:, :, :], W_fuse1.rearrange("(k p) n -> p k n", p=P)),
                  (w_f2[:, :, :], W_fuse2.rearrange("(k p) n -> p k n", p=P)), (w_o[:, :], W_o)]
        loads += [(nw_col[HD * h:HD * h + HD, :], norm_w.rearrange("(e a) -> e a", a=1)) for h in range(HEADS)]
        for dst, src in loads:
            tok["small"] = in_small.dma(sp, dst, src)
        for e in range(EXPERTS):
            for dst, src in ((w_up[:, e, 0, :], W1[e]), (w_up[:, e, 1, :], W2[e]),
                             (w_gl[:, e, :, 0, :], Wg[e].rearrange("(k p) n -> p k n", p=P)),
                             (w_gl[:, e, :, 1, :], Wl[e].rearrange("(k p) n -> p k n", p=P)),
                             (w_dn[:, e, :, :], W3[e].rearrange("(k p) n -> p k n", p=P))):
                tok["expert", e] = in_expert[e].dma(sp, dst, src)

        pool.do(lambda g: g.memset(ident[:, :], 0.0))
        pool.do(lambda g: g.memset(causal_bd[:, :], 1.0))
        pool.do(lambda g: g.memset(before_bd[:, :], 1.0))
        pool.do(lambda g: g.memset(earlier8[:, :, :], 1.0))
        pool.do(lambda g: g.memset(solve_start[:, :, :], 0.0))
        pool.do(lambda g: g.memset(block_mask[:, :], 0.0))
        filled = pool.do(lambda g: g.memset(minus_half[:, :], -0.5))
        pool.wait(filled)
        tok["ident"] = pool.do(lambda g: g.affine_select(
            out=ident[:, :], in_=ident[:, :], compare_op=ALU.not_equal, fill=1.0, base=0,
            pattern=[[-1, P]], channel_multiplier=1))
        pool.do(lambda g: g.affine_select(
            out=causal_bd[:, :], in_=causal_bd[:, :], compare_op=ALU.is_ge, fill=0.0, base=0,
            pattern=[[1, P]], channel_multiplier=-1))
        pool.do(lambda g: g.affine_select(
            out=before_bd[:, :], in_=before_bd[:, :], compare_op=ALU.is_gt, fill=0.0, base=0,
            pattern=[[-1, P]], channel_multiplier=1))
        pool.do(lambda g: g.affine_select(
            out=earlier8[:, :, :], in_=earlier8[:, :, :], compare_op=ALU.is_gt, fill=0.0, base=0,
            pattern=[[1, EXPERTS], [-1, EXPERTS]], channel_multiplier=0))
        for half in range(2):
            part = solve_start[64 * half:64 * half + 64, :, :]
            pool.fence()
            pool.do(lambda g, part=part, half=half: g.affine_select(
                out=part, in_=part, compare_op=ALU.not_equal, fill=1.0, base=KH * half,
                pattern=[[1, KH], [-1, CHUNK]], channel_multiplier=0))
        for h in range(HEADS):
            pool.fence()
            masks = pool.do(lambda g, h=h: g.memset(block_mask[HD * h:HD * h + HD, HD * h:HD * h + HD], 1.0))
        pool.wait(masks)
        pool.do(lambda g: g.tensor_tensor(causal_bd[:, :], causal_bd[:, :], block_mask[:, :], ALU.mult))
        tok["masks"] = pool.do(lambda g: g.tensor_tensor(before_bd[:, :], before_bd[:, :], block_mask[:, :], ALU.mult))
        for t in (conv_halo, v_act[1], kq_bd, kn_bd[0], kn_bd[1], inv_bd, state):
            flat = t[:].rearrange({3: "p a b -> p (a b)", 4: "p a b c -> p (a b c)", 5: "p a b c d -> p (a b c d)",
                                   6: "p a b c d e -> p (a b c d e)"}[len(t.shape)])
            tok["zeroed"] = pool.do(lambda g, flat=flat: g.memset(flat, 0.0))
        dve.wait(tok["masks"])
        dve.do(lambda v: v.tensor_reduce(before[:, :], before_bd[:, :].rearrange("p (b j) -> p j b", b=SEQS),
                                         AX.X, ALU.add))
        tok["diag"] = dve.do(lambda v: v.tensor_reduce(
            diagonal[:, :], ident[:, :].rearrange("p (b j) -> p j b", b=SEQS), AX.X, ALU.add))

        act.wait(tok["small"])
        tok["inv_tau"] = act.do(lambda a: a.activation(inv_tau[:, :], tau_row[:, :], ACT.Exp, scale=-1.0))
        dve.wait(tok["small"])
        tok["w_on"] = dve.do(lambda v: v.tensor_scalar(w_on[:, :], w_o[:, :], nw_col[:, 0:1], None, ALU.mult))
        pe.wait(tok["small"], tok["ident"])
        nrows = 4 * nb + 2
        tok["bias_ps"] = pe.do(lambda t: t.transpose(shared[1].tile[:, 0:nrows], bias_rows[:, :], ident[0:nrows, 0:nrows]))
        act.wait(tok["bias_ps"])
        tok["bias"] = act.do(lambda a: a.activation(bias_cols[:, :], shared[1].tile[:, 0:nrows], ACT.Copy))
        shared[1].leave(tok["bias"])

        def bias_of(n, e, j):
            c = n * nb + e * FJ + j
            return bias_cols[:, c:c + 1]

        def take():
            while all(b.held for b in shared):
                yield
            got = next(b for b in shared if not b.held)
            got.held = True
            pe.wait(*got.read)
            return got, got.tile

        def transposed(to, tokens, pieces, rows=P):
            pe.wait(*tokens, tok["ident"])
            for n, piece in enumerate(pieces):
                t = pe.do(lambda t, n=n, piece=piece: t.transpose(to.tile[0:rows, n * P:(n + 1) * P], piece, ident[:, :]))
            return t

        def prepare(w):
            par, x, beta = w % 2, xt[w % 2], beta_ring[w % 2]
            if w + 1 < WINDOWS:
                sp.wait(*had(("xn T", w - 1)))
                for b in range(SEQS):
                    tok["x", w + 1] = in_x[1 - par].dma(
                        sp, xt[1 - par][CHUNK * b:CHUNK * b + CHUNK, :, :],
                        hidden[b, rows_of(b, w + 1), :].rearrange("(c i) d -> i c d", i=CHUNK))
            dve.wait(tok["x", w])
            for c in range(CPW):
                s = dve.do(lambda v, c=c: v.bn_stats(stats[:, c, :], x[:, c, :]))
            dve.wait(s)
            for c in range(CPW):
                m = dve.do(lambda v, c=c: v.bn_aggr(moments[:, c, :], stats[:, c, :]))
            pool.wait(m)
            r = pool.do(lambda g: g.tensor_scalar(rstd[:, :], moments[:, :, 1], LN_EPS, None, ALU.add))
            pool.wait(r)
            r = pool.do(lambda g: g.tensor_tensor(rstd[:, :], rstd[:, :], minus_half[:, 0:CPW], ALU.pow))
            yield
            dve.wait(r)
            for c in range(CPW):
                n = dve.do(lambda v, c=c: v.tensor_scalar(x[:, c, :], x[:, c, :], moments[:, c, 0:1],
                                                          rstd[:, c:c + 1], ALU.subtract, ALU.mult))
            tok["normed", w] = n
            yield
            while w >= 2 and (("ffn read", w - 2) not in tok or ("fuse read", w - 2) not in tok
                              or ("qkv read", w - 2) not in tok):
                yield
            yield
            bk, ps = yield from take()
            tok["xn T", w] = transposed(bk, [n], [x[:, c, :] for c in range(CPW)])
            yield
            act.wait(tok["xn T", w], *had(("ffn read", w - 2), ("fuse read", w - 2), ("qkv read", w - 2)))
            tok["xf", w] = act.do(lambda a, ps=ps: a.activation(xf[par][:, :], ps[:, :], ACT.Copy))
            bk.leave(tok["xf", w])
            yield
            while w >= 2 and ("v_b", w - 2) not in tok:
                yield
            bk, ps = yield from take()
            pe.wait(tok["xf", w], tok["small"])
            nr = EXPERTS + HEADS
            for c in range(CPW):
                lgt = pe.do(lambda t, c=c, ps=ps: t.matmul(ps[:, c * nr:(c + 1) * nr], xf[par][:, c * P:(c + 1) * P],
                                                    w_rb[:, :], start=True, stop=True))
            yield
            view = ps[:, 0:CPW * nr].rearrange("p (c n) -> p c n", n=nr)
            dve.wait(lgt, tok["small"])
            g = dve.do(lambda v, view=view: v.tensor_tensor(
                glog[:, :, :], view[:, :, 0:EXPERTS], over(bgate_row[:, :].unsqueeze(1), P, CPW, EXPERTS), ALU.add))
            act.wait(g, *had(("v_b", w - 2), ("beta_mask", w - 2), ("k_b", w - 2)))
            tok["beta", w] = act.do(
                lambda a, view=view: a.activation(beta[:, :, :], view[:, :, EXPERTS:], ACT.Sigmoid))
            bk.leave(tok["beta", w])
            dve.wait(g)
            full = (P, CPW, EXPERTS, EXPERTS)
            other = over(glog[:, :, :].unsqueeze(2), *full)
            own = over(glog[:, :, :].unsqueeze(3), *full)
            dve.do(lambda v: v.tensor_tensor(ties[:, :, :, :], other, own, ALU.is_equal))
            bt = dve.do(lambda v: v.tensor_tensor(beats[:, :, :, :], other, own, ALU.is_gt))
            mx = dve.do(lambda v: v.tensor_reduce(gmax[:, :], glog[:, :, :], AX.X, ALU.max))
            dve.wait(bt, mx)
            d = dve.do(lambda v: v.tensor_tensor(
                glog[:, :, :], glog[:, :, :], over(gmax[:, :].unsqueeze(2), P, CPW, EXPERTS), ALU.subtract))
            t = dve.do(lambda v: v.tensor_tensor(
                ties[:, :, :, :], ties[:, :, :, :], over(earlier8[:, :, :].unsqueeze(1), *full), ALU.mult))
            act.wait(d)
            act.do(lambda a: a.activation(gsig[:, 0, :, :], glog[:, :, :], ACT.Sigmoid))
            sg = act.do(lambda a: a.activation(gsig[:, 1, :, :], glog[:, :, :], ACT.Sigmoid, scale=-1.0))
            dve.wait(t)
            t = dve.do(lambda v: v.tensor_tensor(beats[:, :, :, :], beats[:, :, :, :], ties[:, :, :, :], ALU.add))
            dve.wait(t)
            t = dve.do(lambda v: v.tensor_reduce(
                rank[:, :], beats[:, :, :, :].rearrange("p c e j -> p (c e) j"), AX.X, ALU.add))
            yield
            dve.wait(sg)
            rc = dve.do(lambda v: v.reciprocal(gsig[:, 1, :, :], gsig[:, 1, :, :]))
            dve.wait(rc, t)
            ex = dve.do(lambda v: v.tensor_tensor(gsig[:, 0, :, :], gsig[:, 0, :, :], gsig[:, 1, :, :], ALU.mult))
            dve.wait(ex)
            gv = gsig[:, 0, :, :].rearrange("p c e -> p (c e)")
            ex = dve.do(lambda v: v.scalar_tensor_tensor(gv, rank[:, :], 1.5, gv, ALU.is_lt, ALU.mult))
            dve.wait(ex)
            sm = dve.do(lambda v: v.tensor_reduce(gsum[:, :], gsig[:, 0, :, :], AX.X, ALU.add))
            dve.wait(sm)
            rc = dve.do(lambda v: v.reciprocal(gsum[:, :], gsum[:, :]))
            dve.wait(rc, *had(("route T", w - 1)))
            rt = dve.do(lambda v: v.tensor_tensor(
                route[:, :, :], gsig[:, 0, :, :], over(gsum[:, :].unsqueeze(2), P, CPW, EXPERTS), ALU.mult))
            yield
            while w >= 1 and ("b3", w - 1) not in tok:
                yield
            yield
            bk, ps = yield from take()
            tok["route T", w] = transposed(bk, [rt], [route[:, c, :] for c in range(CPW)], rows=EXPERTS)
            yield
            act.wait(tok["route T", w], *had(("b3", w - 1), ("route_d", w - 1)))
            tok["route_T", w] = act.do(
                lambda a, ps=ps: a.activation(route_T[:, :], ps[0:EXPERTS, :], ACT.Copy))
            bk.leave(tok["route_T", w])
            sp.wait(tok["route_T", w], *had(("route_bc last", w - 2)))
            tok["route_d", w] = in_route[par].dma(sp, route_d[par], route_T[:, :])
            yield

        def project(w, n):
            par = w % 2
            bk, ps = yield from take()
            pe.wait(tok["xf", w], tok["small"])
            pr = pe.do(lambda t, ps=ps: t.matmul(ps[:, :], w_qkv[:, n, :], xf[par][:, :], start=True, stop=True))
            yield
            act.wait(pr, *had("halo kept", "conv"))
            cp = act.do(lambda a, ps=ps: a.activation(
                pre[:, :, K_CONV - 1:], runs_flat(ps[:, :]), ACT.Copy))
            bk.leave(cp)
            if n == 2:
                tok["qkv read", w] = pr
            pool.wait(tok["zeroed"], *had("conv"))
            hl = pool.do(lambda g: g.tensor_copy(pre[:, 0:SEQS, 0:K_CONV - 1], conv_halo[:, n, :, :]))
            pool.wait(cp, hl)
            hl = spread_halo(pre, K_CONV - 1)
            tok["halo kept"] = pool.do(lambda g: g.tensor_copy(conv_halo[:, n, :, :], pre[:, RUNS - SEQS:, CHUNK:]))
            yield
            dve.wait(cp, hl, tok["small"], *had("silu"))
            for k in range(K_CONV):
                if k == 0:
                    c = dve.do(lambda v: v.tensor_scalar(runs(acc), pre[:, :, 0:CHUNK], conv_w[:, n, 0:1], None, ALU.mult))
                else:
                    dve.wait(c)
                    c = dve.do(lambda v, k=k: v.scalar_tensor_tensor(
                        runs(acc), pre[:, :, k:k + CHUNK], conv_w[:, n, k:k + 1], runs(acc), ALU.mult, ALU.add))
                if k % 2:
                    yield
            tok["conv"] = c
            act.wait(c, *had("silu", "qk T", ("v act", w - 1)))
            sg = act.do(lambda a: a.activation(gate[:, :, :, :], acc[:, :, :, :], ACT.Sigmoid))
            yield
            dve.wait(sg)
            tok["silu"] = dve.do(lambda v: v.tensor_tensor(gate[:, :, :, :], acc[:, :, :, :], gate[:, :, :, :], ALU.mult))
            yield

        def normed(w, dst, last_reader):
            yield
            bk, ps = yield from take()
            t = tok["qk T"] = transposed(bk, [tok["silu"]], chunks(gate))
            yield
            act.wait(t, *had("sumsq", ("q_n T", w)))
            sq = act.do(lambda a, ps=ps: a.activation(square[:].rearrange("p c h e -> p (c h e)"), ps[:, :], ACT.Square))
            yield
            dve.wait(sq, *had("rnorm read"))
            s = tok["sumsq"] = dve.do(lambda v: v.tensor_reduce(sumsq[:, :, :], square[:, :, :, :], AX.X, ALU.add))
            flat = sumsq[:, :, :].rearrange("p c h -> p (c h)")
            pool.wait(s)
            a = pool.do(lambda g: g.tensor_scalar(flat, flat, L2_EPS, None, ALU.add))
            pool.wait(a)
            r = pool.do(lambda g: g.tensor_tensor(flat, flat, minus_half[:, :], ALU.pow))
            yield
            yield
            dve.wait(r, *had(*last_reader))
            tok["rnorm read"] = tok["normed qk"] = dve.do(
                lambda v, ps=ps: v.tensor_tensor(dst[:, :, :].rearrange("p c (h e) -> p c h e", h=HEADS), as_heads(ps[:, :]), heads_bc(sumsq[:, :, :]), ALU.mult))
            bk.leave(tok["rnorm read"])
            yield

        def attend(w):
            par, beta = w % 2, beta_ring[w % 2]
            while ("beta", w) not in tok:
                yield
            yield from project(w, 0)
            yield from normed(w, q_n, [("q_n T", w - 1)])
            while w >= 2 and ("recurred", w - 2) not in tok:
                yield
            yield
            bk, ps = yield from take()
            tok["q_n T", w] = transposed(bk, [tok["normed qk"]], [q_n[:, c, :] for c in range(CPW)])
            yield
            act.wait(tok["q_n T", w], *had(("recurred", w - 2)))
            tok["q_T", w] = act.do(
                lambda a, ps=ps: a.activation(q_T[par][:].rearrange("p c b i -> p (c b i)"), ps[:, :], ACT.Copy))
            bk.leave(tok["q_T", w])
            yield from project(w, 1)
            yield from normed(w, k_n[par], [("recurred", w - 2)])
            yield
            bk, ps = yield from take()
            kt = transposed(bk, [tok["normed qk"]], [k_n[par][:, c, :] for c in range(CPW)])
            pool.wait(tok["normed qk"], tok["beta", w], *had(("recurred", w - 2)))
            tok["k_b", w] = pool.do(lambda g: g.tensor_tensor(
                as_heads(k_b[par][:, :, :].rearrange("p c d -> p (c d)")),
                as_heads(k_n[par][:, :, :].rearrange("p c d -> p (c d)")), heads_bc(beta[:, :, :]), ALU.mult))
            pool.wait(tok["diag"], *had(("system", w - 1)))
            tok["beta_mask", w] = pool.do(lambda g: g.tensor_tensor(
                beta_mask[:, :, :, :], heads_bc(beta[:, :, :]),
                over(before[:, :].unsqueeze(1), P, CPW * HEADS, CHUNK).rearrange("p (c h) j -> p c h j", c=CPW), ALU.mult))
            yield
            act.wait(kt, *had(("products", w - 1), ("kq_bd", w - 1)))
            kT = act.do(lambda a, ps=ps: a.activation(k_T[:].rearrange("p c b i -> p (c b i)"), ps[:, :], ACT.Copy))
            bk.leave(kT)
            yield
            for pair in range(CPW // 2):
                c0 = 2 * pair
                pool.wait(kT, tok["q_T", w], tok["zeroed"], *had("products"))
                act.wait(kT, *had("products"), tok["zeroed"])
                for h in range(HEADS):
                    rows = slice(HD * h, HD * h + HD)
                    pool.fence()
                    cq = pool.do(lambda g, h=h, rows=rows, c0=c0: g.tensor_copy(
                        kq_bd[rows, :, :, 1, h, :].rearrange("p c b i -> p (c b) i"),
                        q_T[par][rows, c0:c0 + 2, :, :].rearrange("p c b i -> p (c b) i")))
                    ck = act.do(lambda a, h=h, rows=rows, c0=c0: a.activation(
                        kq_bd[rows, :, :, 0, h, :].rearrange("p c b i -> p (c b) i"),
                        k_T[rows, c0:c0 + 2, :, :].rearrange("p c b i -> p (c b) i"), ACT.Copy))
                pool.fence()
                tok["kq_bd", w] = cq
                yield
                yield
                bk, ps = yield from take()
                pe.wait(kT, cq, ck)
                for c in range(2):
                    for b in range(SEQS):
                        pr = pe.do(lambda t, c=c, b=b, c0=c0, ps=ps: t.matmul(
                            ps[CHUNK * b:CHUNK * b + CHUNK, c * 256:(c + 1) * 256], k_T[:, c0 + c, b, :],
                            kq_bd[:, c, b, :, :, :].rearrange("p s h i -> p (s h i)"), start=True, stop=True,
                            tile_position=(0, CHUNK * b)))
                tok["products"] = tok["products", w] = pr
                yield
                view = ps[:, :].rearrange("p (c s h i) -> p c s h i", c=2, s=2, h=HEADS)
                dve.wait(pr, tok["beta_mask", w], *had(("system_d", w - 1)))
                for c in range(2):
                    L = dve.do(lambda v, c=c, c0=c0, view=view: v.tensor_tensor(
                        system[:, c0 + c, :, :], view[:, c, 0], beta_mask[:, c0 + c, :, :], ALU.mult))
                act.wait(L, *had(("recurred", w - 2)))
                tok["local", w] = act.do(lambda a, c0=c0, ps=ps: a.activation(
                    local[par][:, c0:c0 + 2, :, :].rearrange("p c h i -> p c (h i)"),
                    ps[:, :].rearrange("p (c s n) -> p c s n", c=2, s=2)[:, :, 1, :], ACT.Copy))
                bk.leave(tok["local", w])
                yield
            pool.wait(L)
            flat = system[:].rearrange("p c h j -> p (c h) j")
            tok["system", w] = pool.do(lambda g: g.tensor_tensor(
                flat, flat, over(diagonal[:, :].unsqueeze(1), P, CPW * HEADS, CHUNK), ALU.subtract))
            sp.wait(tok["system", w], *had(("solve in", w - 2)))
            for b in range(SEQS):
                n0 = b * CPW * HEADS
                tok["system_d", w] = in_system.dma(
                    sp, system_d[par, n0:n0 + CPW * HEADS].rearrange("n i j -> i n j"),
                    flat[CHUNK * b:CHUNK * b + CHUNK])
            while w >= 1 and ("solved", w - 1) not in tok:
                yield
            sp.wait(tok["system_d", w], *had(("solved", w - 1)))
            for half in range(2):
                tok["solve in", w] = in_solve.dma(
                    sp, solve_L[64 * half:64 * half + 64, :, :], system_d[par])
            yield from project(w, 2)
            while w >= 2 and ("v again", w - 2) not in tok:
                yield
            pool.wait(tok["silu"], tok["zeroed"], *had(("fir", w - 2), ("v again", w - 2), ("v act", w - 1)))
            pool.do(lambda g: g.tensor_copy(v_act[par][:, 0:SEQS, 0:HALO], v_act[1 - par][:, RUNS - SEQS:, CHUNK:]))
            vc = pool.do(lambda g: g.tensor_copy(v_act[par][:, :, HALO:], runs(gate)))
            pool.wait(vc)
            tok["v act", w] = spread_halo(v_act[par], HALO)
            yield
            bk, ps = yield from take()
            vt = tok["qk T"] = transposed(bk, [tok["silu"]], chunks(gate))
            yield
            dve.wait(vt, tok["beta", w], *had(("recurred", w - 2)))
            tok["v_b", w] = dve.do(lambda v, ps=ps: v.tensor_tensor(
                as_heads(v_b[par][:, :, :].rearrange("p c d -> p (c d)")), as_heads(ps[:, :]), heads_bc(beta[:, :, :]), ALU.mult))
            bk.leave(tok["v_b", w])
            yield

        def invert(w):
            par = w % 2
            while ("solve in", w) not in tok:
                yield
            while w >= 2 and ("inv_bd", w - 2) not in tok:
                yield
            act.wait(*had(("inverse_d", w - 1)), tok["ident"])
            pool.wait(masks)
            st = act.do(lambda a: a.activation(solve_T[:, :, :], solve_start[:, :, :], ACT.Copy))
            dve.wait(tok["solve in", w], st)
            last = st
            for i in range(1, CHUNK):
                k = min(i, KH)
                prod = solve_prod[:, 0:k * (i + 1)].rearrange("p (k j) -> p k j", k=k)
                dve.wait(last)
                m = dve.do(lambda v, i=i, k=k, prod=prod: v.tensor_tensor(
                    prod, solve_T[:, 0:k, 0:i + 1], over(solve_L[:, i, 0:i + 1].unsqueeze(1), P, k, i + 1), ALU.mult))
                if i % 4 == 0:
                    yield
                dve.wait(m)
                last = dve.do(lambda v, i=i, k=k, prod=prod: v.tensor_reduce(
                    solve_T[:, 0:k, i], prod, AX.X, ALU.add, negate=True))
                if i > 16 or i % 2:
                    yield
            tok["solved", w] = last
            sp.wait(last, *had(("inv_bd", w - 2)))
            for half in range(2):
                tok["inverse_d", w] = in_inverse.dma(
                    sp, inverse_d[par, :, KH * half:KH * half + KH, :], solve_T[64 * half:64 * half + 64, :, :])
            yield

        def filters(w):
            par = w % 2
            while ("v act", w) not in tok:
                yield
            while w >= 1 and ("fir T", w - 1) not in tok:
                yield
            v = v_act[par]
            dve.wait(tok["v act", w], tok["small"], *had(("fir T", w - 1), ("fuse read", w - 1)))

            def tap(queue, dst, weights, taps, k, first):
                src = v[:, :, HALO - taps + 1 + k:HALO - taps + 1 + k + CHUNK]
                if first:
                    return queue.do(lambda e: e.tensor_scalar(runs(dst), src, weights[:, k:k + 1], None, ALU.mult))
                return queue.do(lambda e: e.scalar_tensor_tensor(
                    runs(dst), src, weights[:, k:k + 1], runs(dst), ALU.mult, ALU.add))

            taps = [(fir_s, short_w, K_SHORT, k) for k in range(K_SHORT)]
            taps += [(fir_l, long_w, K_LONG, k) for k in range(K_LONG)]
            d = None
            for dst, weights, n, k in taps:
                if d:
                    dve.wait(d)
                d = tap(dve, dst, weights, n, k, k == 0)
                yield
            tok["fir", w] = d

        def finish(w):
            par = w % 2
            while ("inverse_d", w) not in tok or ("v_b", w) not in tok:
                yield
            sp.wait(tok["inverse_d", w], tok["zeroed"], *had(("w_T ps", w - 1)))
            for b in range(SEQS):
                n0 = b * CPW * HEADS
                tok["inv_bd", w] = in_inv_bd.dma(
                    sp, inv_bd[CHUNK * b:CHUNK * b + CHUNK, :, :, b, :].rearrange("p c h i -> p (c h) i"),
                    inverse_d[par, n0:n0 + CPW * HEADS].rearrange("n k i -> k n i"))
            for _ in range(6):
                yield
            bk, ps = yield from take()
            pe.wait(tok["inv_bd", w], tok["v_b", w], tok["k_b", w])
            for c in range(CPW):
                for h in range(HEADS):
                    cols = slice(HD * h, HD * h + HD)
                    u = pe.do(lambda t, c=c, h=h, cols=cols, ps=ps: t.matmul(
                        ps[:, c * D + HD * h:c * D + HD * h + HD],
                        inv_bd[:, c, h, :, :].rearrange("p b i -> p (b i)"), v_b[par][:, c, cols], start=True, stop=True))
            yield
            act.wait(u, *had(("fuse2", w - 1)))
            uc = act.do(lambda a, ps=ps: a.activation(u_sb[:].rearrange("p c d -> p (c d)"), ps[:, :], ACT.Copy))
            bk.leave(uc)
            yield
            bk, ps = yield from take()
            pe.wait(uc)
            for c in range(CPW):
                for h in range(HEADS):
                    cols = slice(HD * h, HD * h + HD)
                    wt = pe.do(lambda t, c=c, h=h, cols=cols, ps=ps: t.matmul(
                        ps[cols, c * P:(c + 1) * P], k_b[par][:, c, cols],
                        inv_bd[:, c, h, :, :].rearrange("p b i -> p (b i)"), start=True, stop=True,
                        tile_position=(0, HD * h)))
                if c % 2:
                    yield
            tok["w_T ps", w] = wt
            act.wait(wt, *had(("recurred", w - 1), ("fuse2", w - 1)))
            wc = act.do(lambda a, ps=ps: a.activation(w_T[:].rearrange("p c b i -> p (c b i)"), ps[:, :], ACT.Copy))
            bk.leave(wc)
            yield
            for c in range(CPW):
                last_chunk = w == WINDOWS - 1 and c == CPW - 1
                cp = (w * CPW + c) % 2
                act.wait(tok["zeroed"], *had(("state ps", cp)))
                for b in range(SEQS):
                    rows = slice(CHUNK * b, CHUNK * b + CHUNK)
                    kd = act.do(lambda a, b=b, rows=rows, c=c, cp=cp: a.activation(
                        kn_bd[cp][rows, b, :], k_n[par][rows, c, :], ACT.Copy))
                dve.wait(tok["local", w], tok["masks"], *had(("local read", cp)))
                ld = dve.do(lambda v, c=c, cp=cp: v.tensor_tensor(
                    local_bd[cp][:, :, :, :], over(local[par][:, c, :, :].unsqueeze(2), P, HEADS, SEQS, CHUNK),
                    over(causal_bd[:, :].rearrange("p (b i) -> p b i", b=SEQS).unsqueeze(1), P, HEADS, SEQS, CHUNK), ALU.mult))
                bk, ps = yield from take()
                pe.wait(wc, tok["q_T", w], tok["zeroed"], *had("state"))
                for b in range(SEQS):
                    rows = slice(CHUNK * b, CHUNK * b + CHUNK)
                    ws = pe.do(lambda t, b=b, rows=rows, c=c, ps=ps: t.matmul(
                        ps[rows, 0:D], w_T[:, c, b, :], state[:, b, :], start=True, stop=True, tile_position=(0, CHUNK * b)))
                for b in range(SEQS):
                    rows = slice(CHUNK * b, CHUNK * b + CHUNK)
                    qs = pe.do(lambda t, b=b, rows=rows, c=c, ps=ps: t.matmul(
                        ps[rows, D:2 * D], q_T[par][:, c, b, :], state[:, b, :], start=True, stop=False,
                        tile_position=(0, CHUNK * b), skip_group_check=True))
                yield
                dve.wait(qs, *had("u_adj read"))
                ua = dve.do(lambda v, c=c, ps=ps: v.tensor_tensor(u_adj[:, :], u_sb[:, c, :], ps[:, 0:D], ALU.subtract))
                yield
                pe.wait(ua, kd, ld)
                if not last_chunk:
                    for b in range(SEQS):
                        sps = pe.do(lambda t, b=b, cp=cp, first=(w == 0 and c == 0 and b == 0): t.matmul(
                            ps_state[:, b * D:(b + 1) * D], kn_bd[cp][:, b, :], u_adj[:, :], start=first, stop=True,
                            skip_group_check=True))
                    tok["state ps", cp] = sps
                for h in range(HEADS):
                    cols = slice(HD * h, HD * h + HD)
                    lo = pe.do(lambda t, h=h, cols=cols, cp=cp, ps=ps: t.matmul(
                        ps[:, D + HD * h:D + HD * h + HD], local_bd[cp][:, h, :, :].rearrange("p b i -> p (b i)"),
                        u_adj[:, cols], start=False, stop=True, skip_group_check=True))
                tok["u_adj read"] = tok["local read", cp] = lo
                yield
                if not last_chunk:
                    dve.wait(sps)
                    tok["state"] = dve.do(lambda v: v.tensor_tensor(
                        state[:, :, :], ps_state[:, :].rearrange("p (b n) -> p b n", b=SEQS),
                        over(block_mask[:, :].unsqueeze(1), P, SEQS, D), ALU.mult))
                act.wait(lo, *had(("mixed", w - 1)))
                dl = act.do(lambda a, c=c, ps=ps: a.activation(delta[:, c, :], ps[:, D:2 * D], ACT.Copy))
                bk.leave(dl)
                if c == CPW - 1:
                    tok["recurred", w] = lo
                yield
            yield
            bk, ps = yield from take()
            t = transposed(bk, [dl], [delta[:, c, :] for c in range(CPW)])
            yield
            act.wait(t, *had(("fuse read", w - 1), ("v mixed", w - 1)))
            dT = act.do(lambda a, ps=ps: a.activation(delta_T[:, :], ps[:, :], ACT.Copy))
            bk.leave(dT)
            yield
            while ("fir", w) not in tok:
                yield
            for m in range(2):
                bk, ps = yield from take()
                pe.wait(dT, tok["fir", w], tok["xf", w])
                rhs = [xf[par][:, :], fir_s[:].rearrange("p c b i -> p (c b i)"),
                       fir_l[:].rearrange("p c b i -> p (c b i)"), delta_T[:, :]]
                for k in range(4):
                    f = pe.do(lambda t, k=k, m=m, r=rhs[k], ps=ps: t.matmul(
                        ps[:, :], w_f1[:, k, m * P:(m + 1) * P], r,
                        start=k == 0, stop=k == 3))
                    if k % 2:
                        yield
                act.wait(f, tok["bias"])
                hp = act.do(lambda a, m=m, ps=ps: a.activation(
                    hid[m][:, :], ps[:, :], ACT.Identity, bias=bias_cols[:, 4 * nb + m:4 * nb + m + 1]))
                bk.leave(hp)
                yield
            act.wait(hp)
            for m in range(2):
                tok["hid"] = act.do(lambda a, m=m: a.activation(hid[m][:, :], hid[m][:, :], ACT.Gelu))
            yield
            tok["fuse read", w] = f
            yield
            bk, ps = yield from take()
            pe.wait(tok["hid"])
            for c in range(CPW):
                for m in range(2):
                    f2 = pe.do(lambda t, c=c, m=m, ps=ps: t.matmul(
                        ps[:, c * 16:(c + 1) * 16], hid[m][:, c * P:(c + 1) * P], w_f2[:, m, :], start=m == 0, stop=m == 1))
            tok["fuse2", w] = f2
            yield
            dve.wait(f2, *had("p used"))
            l = dve.do(lambda v, ps=ps: v.tensor_tensor(
                lg[:].rearrange("p c h k -> p c (h k)"), ps[:, 0:CPW * 16].rearrange("p (c n) -> p c n", n=16),
                over(bf2_row[:, :].unsqueeze(1), P, CPW, 16), ALU.add))
            bk.leave(l)
            act.wait(l)
            s = act.do(lambda a: a.activation(p_raw[:, :, :], lg[:, :, :, 3], ACT.Sigmoid))
            dve.wait(l, tok["inv_tau"])
            l = dve.do(lambda v: v.tensor_tensor(
                l3[:, :, :, :], lg[:, :, :, 0:3],
                over(inv_tau[:, :].unsqueeze(1).unsqueeze(3), P, CPW, HEADS, 3), ALU.mult))
            dve.wait(l)
            l = dve.do(lambda v: v.tensor_reduce(l3max[:, :, :], l3[:, :, :, :], AX.X, ALU.max))
            dve.wait(l)
            l = dve.do(lambda v: v.tensor_tensor(
                l3[:, :, :, :], l3[:, :, :, :], over(l3max[:, :, :].unsqueeze(3), P, CPW, HEADS, 3), ALU.subtract))
            act.wait(l)
            act.do(lambda a: a.activation(l3sig[:, 0], l3[:, :, :, :], ACT.Sigmoid))
            sg = act.do(lambda a: a.activation(l3sig[:, 1], l3[:, :, :, :], ACT.Sigmoid, scale=-1.0))
            dve.wait(s)
            a1 = dve.do(lambda v: v.tensor_scalar(p_val[:, :, :], p_raw[:, :, :], FLOOR_MAX - FLOOR_MIN, 1.0 - FLOOR_MAX, ALU.mult, ALU.add))
            dve.wait(a1)
            a1 = dve.do(lambda v: v.tensor_tensor(p_val[:, :, :], p_val[:, :, :], p_raw[:, :, :], ALU.mult))
            dve.wait(a1)
            a1 = dve.do(lambda v: v.tensor_scalar(p_rest[:, :, :], p_val[:, :, :], -1.0, 1.0, ALU.mult, ALU.add))
            yield
            dve.wait(sg)
            r = dve.do(lambda v: v.reciprocal(l3sig[:, 1], l3sig[:, 1]))
            dve.wait(r)
            r = dve.do(lambda v: v.tensor_tensor(l3sig[:, 0], l3sig[:, 0], l3sig[:, 1], ALU.mult))
            dve.wait(r)
            r = dve.do(lambda v: v.tensor_reduce(l3sum[:, :, :], l3sig[:, 0], AX.X, ALU.add))
            dve.wait(r)
            r = dve.do(lambda v: v.reciprocal(l3sum[:, :, :], l3sum[:, :, :]))
            dve.wait(r, a1)
            r = dve.do(lambda v: v.tensor_tensor(l3sum[:, :, :], l3sum[:, :, :], p_rest[:, :, :], ALU.mult))
            dve.wait(r)
            pc = dve.do(lambda v: v.tensor_tensor(
                l3[:, :, :, :], l3sig[:, 0], over(l3sum[:, :, :].unsqueeze(3), P, CPW, HEADS, 3), ALU.mult))
            yield
            yield
            bk, ps = yield from take()
            t = transposed(bk, [], chunks(fir_s))
            pool.wait(pc, dl, *had(("mixed", w - 1), ("out ps", w - 1)))
            m2 = pool.do(lambda g: g.tensor_tensor(
                mix_part[1][:, :, :, :], as_heads(delta[:].rearrange("p c d -> p (c d)")), heads_bc(l3[:, :, :, 2]), ALU.mult))
            yield
            dve.wait(t, pc, *had(("o_T ps", w - 1)))
            m0 = dve.do(lambda v, ps=ps: v.tensor_tensor(
                mix[:, :, :, :], as_heads(ps[:, :]), heads_bc(l3[:, :, :, 0]), ALU.mult))
            bk.leave(m0)
            yield
            yield
            bk, ps = yield from take()
            t = tok["fir T", w] = transposed(bk, [], chunks(fir_l))
            pool.wait(m0, m2)
            s = pool.do(lambda g: g.tensor_tensor(mix[:, :, :, :], mix[:, :, :, :], mix_part[1][:, :, :, :], ALU.add))
            yield
            dve.wait(t)
            m1 = dve.do(lambda v, ps=ps: v.tensor_tensor(
                mix_part[0][:, :, :, :], as_heads(ps[:, :]), heads_bc(l3[:, :, :, 1]), ALU.mult))
            bk.leave(m1)
            pool.wait(m1, s)
            s = pool.do(lambda g: g.tensor_tensor(mix[:, :, :, :], mix[:, :, :, :], mix_part[0][:, :, :, :], ALU.add))
            yield
            pool.wait(tok["fuse read", w])
            vc = tok["v again", w] = pool.do(lambda g: g.tensor_copy(
                runs_flat(delta_T[:, :]), v_act[par][:, :, HALO:]))
            yield
            yield
            bk, ps = yield from take()
            t = tok["v mixed", w] = transposed(bk, [vc], [delta_T[:, c * P:(c + 1) * P] for c in range(CPW)])
            yield
            dve.wait(t, s)
            m1 = tok["p used"] = dve.do(lambda v, ps=ps: v.tensor_tensor(
                mix_part[1][:, :, :, :], as_heads(ps[:, :]), heads_bc(p_val[:, :, :]), ALU.mult))
            bk.leave(m1)
            dve.wait(m1)
            s = tok["mixed", w] = dve.do(lambda v: v.tensor_tensor(mix[:, :, :, :], mix[:, :, :, :], mix_part[1][:, :, :, :], ALU.add))
            act.wait(s)
            s = act.do(lambda a: a.activation(mix_part[0][:, :, :, :], mix[:, :, :, :], ACT.Square))
            yield
            yield
            dve.wait(s)
            s = dve.do(lambda v: v.tensor_reduce(ssq_o[:, :, :], mix_part[0][:, :, :, :], AX.X, ALU.add))
            pool.wait(s)
            flat = ssq_o[:, :, :].rearrange("p c h -> p (c h)")
            s = pool.do(lambda g: g.tensor_scalar(flat, flat, 1.0 / HD, RMS_EPS, ALU.mult, ALU.add))
            pool.wait(s)
            s = pool.do(lambda g: g.tensor_tensor(flat, flat, minus_half[:, :], ALU.pow))
            pool.wait(s)
            s = tok["mixed", w] = pool.do(lambda g: g.tensor_tensor(
                mix[:, :, :, :], mix[:, :, :, :], heads_bc(ssq_o[:, :, :]), ALU.mult))
            yield
            sp.wait(*had(("stored", w - 1)))
            for b in range(SEQS):
                tok["x_res", w] = in_xres.dma(sp, x_res[CHUNK * b:CHUNK * b + CHUNK, :, :],
                                              hidden[b, rows_of(b, w), :].rearrange("(c i) d -> i c d", i=CHUNK))
            yield
            yield
            bk, ps = yield from take()
            t = tok["o_T ps", w] = transposed(bk, [s], [mix[:, c, :, :].rearrange("p h e -> p (h e)") for c in range(CPW)])
            yield
            act.wait(t, *had(("out ps", w - 1)))
            oT = act.do(lambda a, ps=ps: a.activation(o_T, ps[:, :], ACT.Copy))
            bk.leave(oT)
            yield
            while ("y_T", w) not in tok:
                yield
            bk, ps = yield from take()
            pe.wait(oT, tok["y_T", w], tok["w_on"])
            for c in range(CPW):
                pe.do(lambda t, c=c, ps=ps: t.matmul(ps[:, c * D:(c + 1) * D], o_T[:, c * P:(c + 1) * P], w_on[:, :], start=True, stop=False))
                t = pe.do(lambda t, c=c, ps=ps: t.matmul(ps[:, c * D:(c + 1) * D], y_T[par][:, c * P:(c + 1) * P], ident[:, :], start=False, stop=True))
            tok["out ps", w] = t
            yield
            dve.wait(t, tok["x_res", w])
            s = tok["summed", w] = dve.do(lambda v, ps=ps: v.tensor_tensor(
                x_res[:].rearrange("p c d -> p (c d)"), ps[:, :], x_res[:].rearrange("p c d -> p (c d)"), ALU.add))
            bk.leave(s)
            sp.wait(s)
            for b in range(SEQS):
                tok["stored", w] = in_out.dma(
                    sp, out[b, rows_of(b, w), :].rearrange("(c i) d -> i c d", i=CHUNK), x_res[CHUNK * b:CHUNK * b + CHUNK, :, :])
            yield

        def load_route(w, e):
            slot = (w * EXPERTS + e) % 3
            while ("route_d", w) not in tok:
                yield
            sp.wait(tok["route_d", w], *had(("sigc", slot)))
            tok["route_bc", w, e] = in_route_bc[slot].dma(
                sp, route_bc[slot][:, :], route_d[w % 2, e, :].partition_broadcast(P))
            if e == EXPERTS - 1:
                tok["route_bc last", w] = tok["route_bc", w, e]

        def up(w, e, j):
            par, cols, zb = w % 2, slice(j * P, (j + 1) * P), z[e % 2][j]
            pe.wait(tok["xf", w], tok["expert", e], *had("up1"))
            x1 = pe.do(lambda t: t.matmul(ps_x1[:, :], w_up[:, e, 0, cols], xf[par][:, :], start=True, stop=True))
            pe.wait(*had("z"))
            x2 = pe.do(lambda t: t.matmul(ps_x2[:, :], w_up[:, e, 1, cols], xf[par][:, :], start=True, stop=True))
            if e == EXPERTS - 1 and j == FJ - 1:
                tok["ffn read", w] = x2
            act.wait(x1, tok["bias"], *had("z"))
            a = tok["up1"] = act.do(lambda a: a.activation(up1[:, :], ps_x1[:, :], ACT.Identity, bias=bias_of(0, e, j)))
            dve.wait(a, x2, *had(("z read", e % 2)))
            tok["z"] = tok["z", w, e, j] = dve.do(lambda v: v.scalar_tensor_tensor(
                zb[:, :], ps_x2[:, :], bias_of(1, e, j), up1[:, :], ALU.add, ALU.mult))

        def mid(w, e, j):
            cols, slot = slice(j * P, (j + 1) * P), (w * EXPERTS + e) % 3
            pe.wait(tok["z", w, e, 0], tok["z", w, e, 1], tok["expert", e], *had("t"))
            for k in range(FJ):
                g = pe.do(lambda t, k=k: t.matmul(ps_g[:, :], w_gl[:, e, k, 0, cols], z[e % 2][k][:, :], start=k == 0, stop=k == FJ - 1))
            act.wait(g, *had(("o", j)))
            s = act.do(lambda a: a.activation(sig[j][:, :], ps_g[:, :], ACT.Sigmoid, bias=bias_of(2, e, j)))
            yield
            pe.wait(*had("o"))
            for k in range(FJ):
                l = pe.do(lambda t, k=k: t.matmul(ps_l[:, :], w_gl[:, e, k, 1, cols], z[e % 2][k][:, :], start=k == 0, stop=k == FJ - 1))
            tok["z read", e % 2] = l
            pool.wait(s, tok["route_bc", w, e])
            c = tok["sigc", slot] = pool.do(lambda g: g.tensor_tensor(sig[j][:, :], sig[j][:, :], route_bc[slot][:, :], ALU.mult))
            yield
            dve.wait(c, g)
            t = tok["t"] = dve.do(lambda v: v.scalar_tensor_tensor(
                sig[j][:, :], ps_g[:, :], bias_of(2, e, j), sig[j][:, :], ALU.add, ALU.mult))
            dve.wait(t, l, *had(("y read", j)))
            tok["o"] = tok["o", j] = dve.do(lambda v: v.scalar_tensor_tensor(
                gated[j][:, :], ps_l[:, :], bias_of(3, e, j), sig[j][:, :], ALU.add, ALU.mult))

        def down(w, e, j):
            pe.wait(tok["o", j])
            if e == 0 and j == 0:
                pe.wait(tok["route_T", w], tok["small"], *had(("y_T", w - 1)))
                tok["b3", w] = pe.do(lambda t: t.matmul(ps_y[:, :], b3_sb[:, :], route_T[:, :], start=True, stop=False))
            last = e == EXPERTS - 1 and j == FJ - 1
            tok["y ps"] = tok["y read", j] = pe.do(lambda t: t.matmul(
                ps_y[:, :], w_dn[:, e, j, :], gated[j][:, :], start=False, stop=last))

        def experts():
            order = [(w, e) for w in range(WINDOWS) for e in range(EXPERTS)]

            def y_out(w):
                act.wait(tok["y ps"], *had(("out ps", w - 2)))
                tok["y_T", w] = act.do(lambda a: a.activation(y_T[w % 2][:, :], ps_y[:, :], ACT.Copy))

            def need(w):
                while ("xf", w) not in tok:
                    yield

            for w, e in order[:2]:
                yield from load_route(w, e)
            yield from need(0)
            for j in range(FJ):
                up(0, 0, j)
                yield
            for n, (w, e) in enumerate(order):
                nxt = order[n + 1] if n + 1 < len(order) else None
                if n + 2 < len(order):
                    yield from load_route(*order[n + 2])
                if nxt:
                    yield from need(nxt[0])
                for j in range(FJ):
                    if nxt:
                        up(*nxt, j)
                        yield
                    yield from mid(w, e, j)
                    if j or n:
                        pj, pe_ = (0, (w, e)) if j else (1, order[n - 1])
                        while pe_[0] >= 2 and ("out ps", pe_[0] - 2) not in tok:
                            yield
                        down(*pe_, pj)
                        if not j and pe_[1] == EXPERTS - 1:
                            y_out(pe_[0])
                    yield
            down(*order[-1], 1)
            y_out(WINDOWS - 1)

        def windows(step):
            for w in range(WINDOWS):
                yield from step(w)

        streams = [experts()] + [windows(step) for step in (finish, invert, prepare, attend, filters)]
        while streams:
            for s in list(streams):
                if next(s, "ended") == "ended":
                    streams.remove(s)
        sp.wait(tok["stored", WINDOWS - 1])

        block = ctx.enter_context(nc.Block())

        @block.sync
        def _(eng):
            sp.play(eng)

        @block.gpsimd
        def _(eng):
            pool.play(eng)

        @block.scalar
        def _(eng):
            act.play(eng)

        @block.vector
        def _(eng):
            dve.play(eng)

        @block.tensor
        def _(eng):
            pe.play(eng)


NAMES = ["L0_attn_" + n for n in (
    "hidden_states W_q W_k W_v W_b conv_w_q conv_w_k conv_w_v fir_short_w fir_long_w W_fuse1 b_fuse1 "
    "W_fuse2 b_fuse2 others_log_tau norm_w W_o").split()]
NAMES += ["L0_ffn_" + n for n in "Wgate bgate W1 b1 W2 b2 Wg bg Wl bl W3 b3".split()]


def kernel(**inputs):
    import numpy as np
    import concourse.bacc as bacc
    from concourse.bass_utils import run_bass_kernel_spmd

    nc = bacc.Bacc("TRN2", target_bir_lowering=False, num_devices=1)
    arrays = {n: np.ascontiguousarray(inputs[n]) for n in NAMES}
    aps = [nc.dram_tensor(n, a.shape, mybir.dt.from_np(a.dtype), kind="ExternalInput").ap() for n, a in arrays.items()]
    out = nc.dram_tensor("out", (SEQS, STEPS, D), FP, kind="ExternalOutput").ap()
    layer(nc, *aps, out)
    return run_bass_kernel_spmd(nc, [arrays], core_ids=[0]).results[0]["out"]
```

```python
import concourse.bass as bass
from concourse import mybir
from contextlib import ExitStack

FP = mybir.dt.float32
FR = mybir.dt.float32r
ALU = mybir.AluOpType
ACT = mybir.ActivationFunctionType
AX = mybir.AxisListType

SEQS, STEPS, D = 4, 1024, 128
HEADS, HD = 4, 32
CHUNK = 32
CPW = 4
WSTEPS = CHUNK * CPW
WINDOWS = STEPS // WSTEPS
WTOK = SEQS * WSTEPS
P = 128
EXPERTS, FF = 8, 256
FJ = FF // P
K_CONV, K_SHORT, K_LONG = 4, 3, 31
HALO = K_LONG - 1
RUNS = CPW * SEQS
BLOCKS = SEQS * CPW * HEADS
KH = CHUNK // 2
GL_SLOTS = 3
RAW_SLOTS = 4
LN_EPS, L2_EPS, RMS_EPS = 1e-5, 1e-6, 1e-5
FLOOR_MIN, FLOOR_MAX = 0.01, 0.1


class Queue:

    def __init__(self, sem):
        self.sem, self.count, self.waited, self.steps = sem, 0, {}, []

    def wait(self, *tokens):
        for sem, value in tokens:
            if self.waited.get(sem.name, 0) < value:
                self.waited[sem.name] = value
                self.steps.append(lambda eng, s=sem, v=value: eng.wait_ge(s, v))

    def more(self, call):
        self.steps.append(call)

    def do(self, call):
        self.count += 1
        self.steps.append(lambda eng, s=self.sem: call(eng).then_inc(s, 1))
        return (self.sem, self.count)

    def fence(self):
        if self.count:
            self.wait((self.sem, self.count))

    def play(self, eng):
        for step in self.steps:
            step(eng)


class Arrivals:

    def __init__(self, sem):
        self.sem, self.count = sem, 0

    def dma(self, queue, out, in_):
        self.count += 16
        queue.steps.append(lambda eng, s=self.sem: eng.dma_start(out, in_).then_inc(s, 16))
        return (self.sem, self.count)


class Bank:

    def __init__(self, tile):
        self.tile, self.held, self.read = tile, False, []

    def leave(self, *tokens):
        self.read, self.held = list(tokens), False


def layer(nc, hidden, W_q, W_k, W_v, W_b, conv_w_q, conv_w_k, conv_w_v, fir_short_w, fir_long_w,
          W_fuse1, b_fuse1, W_fuse2, b_fuse2, others_log_tau, norm_w, W_o,
          Wgate, bgate, W1, b1, W2, b2, Wg, bg, Wl, bl, W3, b3, out):
    ctx = ExitStack()
    with ctx:
        def sb(name, *shape, dt=FP):
            return ctx.enter_context(nc.sbuf_tensor(name, list(shape), dt))

        def bank(name):
            return ctx.enter_context(nc.psum_tensor(name, [P, 512], FP))

        def sem(name):
            return ctx.enter_context(nc.semaphore(name))

        def arrivals(name):
            return Arrivals(sem(name))

        route_d = nc.dram_tensor("route_d", (2, EXPERTS, WTOK), FP, kind="Internal").ap()
        system_d = nc.dram_tensor("system_d", (2, BLOCKS, CHUNK, CHUNK), FP, kind="Internal").ap()
        gl_d = nc.dram_tensor("gl_d", (EXPERTS * FJ, P, 2 * FJ * 2 * P), FP, kind="Internal").ap()
        inverse_d = nc.dram_tensor("inverse_d", (2, BLOCKS, CHUNK, CHUNK), FP, kind="Internal").ap()

        w_up = [sb(f"w_up{n}", P, EXPERTS, 2, FF, dt=FR) for n in range(2)]
        w_gl = [sb(f"w_gl{n}", P, 2, FJ, 2, P, dt=FR) for n in range(GL_SLOTS)]
        w_dn = sb("w_dn", P, EXPERTS, FJ, D)
        bias_cols = sb("bias_cols", P, 4 * EXPERTS * FJ + 2)
        b3_sb = sb("b3_sb", EXPERTS, D)
        w_qkv = [sb(f"w_qkv{n}", P, 3, D, dt=FR) for n in range(2)]
        w_rb = sb("w_rb", P, EXPERTS + HEADS)
        conv_w = sb("conv_w", P, 3, K_CONV)
        short_w = sb("short_w", P, K_SHORT)
        long_w = sb("long_w", P, K_LONG)
        w_f1 = sb("w_f1", P, 3, 2 * D)
        w_fx = [sb(f"w_fx{n}", P, 2 * D, dt=FR) for n in range(2)]
        w_f2 = sb("w_f2", P, 2, HEADS * 4)
        w_on = sb("w_on", P, D)
        nw_col = sb("nw_col", P, 1)
        bgate_row = sb("bgate_row", P, EXPERTS)
        bf2_row = sb("bf2_row", P, HEADS * 4)
        tau_row = sb("tau_row", P, HEADS)
        inv_tau = sb("inv_tau", P, HEADS)

        ident = sb("ident", P, P)
        block_mask = sb("block_mask", P, P)
        causal_bd = sb("causal_bd", P, P)
        before_bd = sb("before_bd", P, P)
        before = sb("before", P, CHUNK)
        diagonal = sb("diagonal", P, CHUNK)
        earlier8 = sb("earlier8", P, EXPERTS, EXPERTS)
        minus_half = sb("minus_half", P, 16)

        xt = sb("xt", P, CPW, D)
        stats = sb("stats", P, CPW, 6)
        moments = sb("moments", P, CPW, 2)
        rstd = sb("rstd", P, CPW)
        xf = [[sb(f"xf{n}{part}", P, WTOK, dt=FR) for part in range(2)] for n in range(3)]
        glog = sb("glog", P, CPW, EXPERTS)
        rank = sb("rank", P, CPW * EXPERTS)
        gmax = sb("gmax", P, CPW)
        gsig = sb("gsig", P, 2, CPW, EXPERTS)
        gsum = sb("gsum", P, CPW)
        route = sb("route", P, CPW, EXPERTS)
        route_T = sb("route_T", EXPERTS, WTOK)
        beta_ring = [sb(f"beta{n}", P, CPW, HEADS) for n in range(2)]
        beta_mask = sb("beta_mask", P, CPW, HEADS, CHUNK)
        pre = sb("pre", P, RUNS, K_CONV - 1 + CHUNK)
        conv_halo = sb("conv_halo", P, 3, SEQS, K_CONV - 1)
        acc = sb("acc", P, CPW, SEQS, CHUNK)
        gate = sb("gate", P, CPW, SEQS, CHUNK)
        beats, ties = (sb(n, P, CPW, EXPERTS, EXPERTS) for n in ("beats", "ties"))
        v_act = [sb(f"v_act{n}", P, RUNS, HALO + CHUNK) for n in range(2)]
        square = sb("square", P, CPW, HEADS, HD)
        sumsq = sb("sumsq", P, CPW, HEADS)
        q_n = square[:].rearrange("p c h e -> p c (h e)")
        k_n = [sb(f"k_n{n}", P, CPW, D) for n in range(2)]
        k_b = [sb(f"k_b{n}", P, CPW, D) for n in range(2)]
        v_b = [sb(f"v_b{n}", P, CPW, D) for n in range(2)]
        q_T = [sb(f"q_T{n}", P, CPW, SEQS, CHUNK) for n in range(2)]
        k_T = sb("k_T", P, CPW, SEQS, CHUNK)
        kq_bd = sb("kq_bd", P, SEQS, 2, HEADS, CHUNK)
        system = sb("system", P, CPW, HEADS, CHUNK)
        local = [sb(f"local{n}", P, CPW, HEADS, CHUNK) for n in range(2)]
        solve_L = sb("solve_L", P, CHUNK, CHUNK)
        solve_T = sb("solve_T", P, KH, CHUNK)
        solve_prod = sb("solve_prod", P, KH * CHUNK)

        inv_bd = sb("inv_bd", P, CPW, HEADS, SEQS, CHUNK)
        kn_bd = [sb(f"kn_bd{n}", P, SEQS, D) for n in range(2)]
        local_bd = sb("local_bd", P, HEADS, SEQS, CHUNK)
        state = sb("state", P, SEQS, D)
        u_adj = sb("u_adj", P, D)
        delta = sb("delta", P, CPW, D)
        delta_T = sb("delta_T", P, WTOK)
        fir_s = sb("fir_s", P, CPW, SEQS, CHUNK)
        fir_l = sb("fir_l", P, CPW, SEQS, CHUNK)
        hid = [sb(f"hid{n}", P, WTOK) for n in range(2)]
        u_sb = hid[0][:, :].rearrange("p (c d) -> p c d", c=CPW)
        w_T = hid[1][:, :].rearrange("p (c b i) -> p c b i", c=CPW, b=SEQS)
        lg = sb("lg", P, CPW, HEADS, 4)
        p_raw = sb("p_raw", P, CPW, HEADS)
        p_val = sb("p_val", P, CPW, HEADS)
        p_rest = sb("p_rest", P, CPW, HEADS)
        l3 = sb("l3", P, CPW, HEADS, 3)
        l3max = sb("l3max", P, CPW, HEADS)
        l3sig = sb("l3sig", P, 2, CPW, HEADS, 3)
        l3sum = sb("l3sum", P, CPW, HEADS)
        mix = sb("mix", P, CPW, HEADS, HD)
        mix_part = [sb(f"mix_part{n}", P, CPW, HEADS, HD) for n in range(2)]
        ssq_o = sb("ssq_o", P, CPW, HEADS)
        o_T = mix_part[1][:].rearrange("p c h e -> p (c h e)")
        x_res = sb("x_res", P, CPW, D)
        y_T = [sb(f"y_T{n}", P, WTOK) for n in range(2)]

        up1 = [sb(f"up1{n}", P, WTOK) for n in range(2)]
        z = [[[sb(f"z{e}{j}{part}", P, WTOK, dt=FR) for part in range(2)] for j in range(FJ)] for e in range(2)]
        gated = [sb(f"gated{n}", P, WTOK) for n in range(2)]
        route_bc = [sb(f"route_bc{n}", P, WTOK) for n in range(2)]

        up_raw = [t[:].rearrange({2: "p n -> p n", 3: "p a b -> p (a b)", 4: "p a b c -> p (a b c)"}[len(t.shape)])
                  for t in (hid[0], hid[1], mix, mix_part[0], mix_part[1], delta, delta_T, x_res)]
        bias_rows = kn_bd[0][:].rearrange("p b d -> p (b d)")[0:4 * EXPERTS * FJ + 2, 0:P]
        gl_raw = [inv_bd[:, n].rearrange("p h b i -> p (h b i)") for n in range(RAW_SLOTS)]
        qkv_raw, fx_raw = y_T[0][:, 0:3 * D], y_T[1][:, 0:2 * D]

        ps_x1, ps_x2, ps_g, ps_l, ps_y = (bank(n) for n in ("ps_x1", "ps_x2", "ps_g", "ps_l", "ps_y"))
        ps_state = bank("ps_state")
        shared = [Bank(bank(f"ps_shared{n}")) for n in range(2)]

        pe, act, dve, pool = (Queue(sem(n)) for n in ("s_pe", "s_act", "s_dve", "s_pool"))
        sp = Queue(None)
        in_first, in_small, in_out = (arrivals(n) for n in ("in_first", "in_small", "in_out"))
        in_up = [arrivals(f"in_up{e}") for e in range(EXPERTS)]
        in_down, in_qkv = arrivals("in_down"), arrivals("in_qkv")
        in_gl_raw = [arrivals(f"in_gl_raw{n}") for n in range(RAW_SLOTS)]
        in_gl_d = [arrivals(f"in_gl_d{n}") for n in range(GL_SLOTS)]
        in_gl = [arrivals(f"in_gl{n}") for n in range(GL_SLOTS)]
        in_x = arrivals("in_x")
        in_xres = arrivals("in_xres")
        in_route = [arrivals(f"in_route{n}") for n in range(2)]
        in_route_bc = [arrivals(f"in_route_bc{n}") for n in range(2)]
        in_system, in_solve, in_inverse, in_inv_bd = (
            arrivals(n) for n in ("in_system", "in_solve", "in_inverse", "in_inv_bd"))
        tok = {}

        def pause(rounds):
            for _ in range(rounds):
                yield

        def had(*keys):
            return [tok[k] for k in keys if k in tok]

        def runs(tile):
            return tile[:].rearrange("p c b i -> p (c b) i")

        def runs_flat(ap):
            return ap.rearrange("p (r i) -> p r i", i=CHUNK)

        def spread_halo(tile, halo):
            return pool.do(lambda g: g.tensor_copy(tile[:, SEQS:, 0:halo], tile[:, 0:RUNS - SEQS, CHUNK:CHUNK + halo]))

        def chunks(tile):
            flat = tile[:].rearrange("p c b i -> p c (b i)")
            return [flat[:, c, :] for c in range(CPW)]

        def over(ap, *shape):
            return ap.to_broadcast(list(shape))

        def heads_bc(ap):
            return over(ap.unsqueeze(3), P, CPW, HEADS, HD)

        def as_heads(ap):
            return ap.rearrange("p (c h e) -> p c h e", c=CPW, h=HEADS)

        def rows_of(b, w):
            return slice(w * WSTEPS, (w + 1) * WSTEPS)

        for b in range(SEQS):
            tok["x", 0] = in_x.dma(sp, xt[CHUNK * b:CHUNK * b + CHUNK, :, :],
                                      hidden[b, rows_of(b, 0), :].rearrange("(c i) d -> i c d", i=CHUNK))
        nb = EXPERTS * FJ
        first = [(w_rb[:, 0:EXPERTS], Wgate), (w_rb[:, EXPERTS:], W_b),
                 (bgate_row[:, :], bgate.partition_broadcast(P))]
        first += [(bias_rows[n * nb:(n + 1) * nb, :], t.rearrange("e (k p) -> (e k) p", p=P))
                  for n, t in enumerate((b1, b2, bg, bl))]
        first += [(bias_rows[4 * nb:4 * nb + 2, :], b_fuse1.rearrange("(k p) -> k p", p=P))]
        loads = [(conv_w[:, n, :], t) for n, t in enumerate((conv_w_q, conv_w_k, conv_w_v))]
        loads += [(b3_sb[:, :], b3), (tau_row[:, :], others_log_tau.partition_broadcast(P)),
                  (bf2_row[:, :], b_fuse2.partition_broadcast(P)),
                  (short_w[:, :], fir_short_w.rearrange("h e k -> (h e) k")),
                  (long_w[:, :], fir_long_w.rearrange("h e k -> (h e) k")),
                  (w_f1[:, :, :], W_fuse1[D:, :].rearrange("(k p) n -> p k n", p=P)), (fx_raw, W_fuse1[0:D, :]),
                  (w_f2[:, :, :], W_fuse2.rearrange("(k p) n -> p k n", p=P)), (w_on[:, :], W_o)]
        loads += [(nw_col[HD * h:HD * h + HD, :], norm_w.rearrange("(e a) -> e a", a=1)) for h in range(HEADS)]
        for dst, src in first:
            tok["first"] = in_first.dma(sp, dst, src)

        def load_up(e):
            for n, t in enumerate((W1, W2)):
                tok["up raw", e] = in_up[e].dma(sp, up_raw[e][:, n * FF:(n + 1) * FF], t[e])

        def load_gl_raw(n):
            e, cols, slot = n // FJ, slice(n % FJ * P, (n % FJ + 1) * P), n % RAW_SLOTS
            if n >= RAW_SLOTS:
                sp.wait(*tok["gl", n - RAW_SLOTS])
            view = gl_raw[slot].rearrange("p (k n f) -> p k n f", k=FJ, n=2)
            for k, t in enumerate((Wg, Wl)):
                tok["gl raw", n] = in_gl_raw[slot].dma(
                    sp, view[:, :, k, :], t[e][:, cols].rearrange("(k p) n -> p k n", p=P))

        load_up(0)
        for n, t in enumerate((W_q, W_k, W_v)):
            tok["qkv raw"] = in_qkv.dma(sp, qkv_raw[:, n * D:(n + 1) * D], t)
        load_up(1)
        for n in range(RAW_SLOTS):
            load_gl_raw(n)
        for dst, src in loads:
            tok["small"] = in_small.dma(sp, dst, src)
        for e in range(EXPERTS):
            tok["down"] = in_down.dma(sp, w_dn[:, e, :, :], W3[e].rearrange("(k p) n -> p k n", p=P))
            if e >= 2:
                load_up(e)

        pool.do(lambda g: g.memset(ident[:, :], 0.0))
        pool.do(lambda g: g.memset(causal_bd[:, :], 1.0))
        pool.do(lambda g: g.memset(before_bd[:, :], 1.0))
        pool.do(lambda g: g.memset(earlier8[:, :, :], 1.0))
        pool.do(lambda g: g.memset(block_mask[:, :], 0.0))
        filled = pool.do(lambda g: g.memset(minus_half[:, :], -0.5))
        pool.wait(filled)
        tok["ident"] = pool.do(lambda g: g.affine_select(
            out=ident[:, :], in_=ident[:, :], compare_op=ALU.not_equal, fill=1.0, base=0,
            pattern=[[-1, P]], channel_multiplier=1))
        pool.do(lambda g: g.affine_select(
            out=causal_bd[:, :], in_=causal_bd[:, :], compare_op=ALU.is_ge, fill=0.0, base=0,
            pattern=[[1, P]], channel_multiplier=-1))
        pool.do(lambda g: g.affine_select(
            out=before_bd[:, :], in_=before_bd[:, :], compare_op=ALU.is_gt, fill=0.0, base=0,
            pattern=[[-1, P]], channel_multiplier=1))
        pool.do(lambda g: g.affine_select(
            out=earlier8[:, :, :], in_=earlier8[:, :, :], compare_op=ALU.is_gt, fill=0.0, base=0,
            pattern=[[1, EXPERTS], [-1, EXPERTS]], channel_multiplier=0))
        for h in range(HEADS):
            pool.fence()
            masks = pool.do(lambda g, h=h: g.memset(block_mask[HD * h:HD * h + HD, HD * h:HD * h + HD], 1.0))
        pool.wait(masks)
        pool.do(lambda g: g.tensor_tensor(causal_bd[:, :], causal_bd[:, :], block_mask[:, :], ALU.mult))
        tok["masks"] = pool.do(lambda g: g.tensor_tensor(before_bd[:, :], before_bd[:, :], block_mask[:, :], ALU.mult))
        for t in (conv_halo, v_act[1], kq_bd, kn_bd[1], state):
            flat = t[:].rearrange({3: "p a b -> p (a b)", 4: "p a b c -> p (a b c)", 5: "p a b c d -> p (a b c d)",
                                   6: "p a b c d e -> p (a b c d e)"}[len(t.shape)])
            tok["zeroed"] = pool.do(lambda g, flat=flat: g.memset(flat, 0.0))
        dve.wait(tok["masks"])
        dve.do(lambda v: v.tensor_reduce(before[:, :], before_bd[:, :].rearrange("p (b j) -> p j b", b=SEQS),
                                         AX.X, ALU.add))
        tok["diag"] = dve.do(lambda v: v.tensor_reduce(
            diagonal[:, :], ident[:, :].rearrange("p (b j) -> p j b", b=SEQS), AX.X, ALU.add))

        pe.wait(tok["first"], tok["ident"])
        nrows = 4 * nb + 2
        tok["bias_ps"] = pe.do(lambda t: t.transpose(shared[1].tile[:, 0:nrows], bias_rows, ident[0:nrows, 0:nrows]))
        act.wait(tok["bias_ps"])
        tok["bias"] = act.do(lambda a: a.activation(bias_cols[:, :], shared[1].tile[:, 0:nrows], ACT.Copy))
        shared[1].leave(tok["bias"])

        def fold_small():
            act.wait(tok["small"])
            tok["inv_tau"] = act.do(lambda a: a.activation(inv_tau[:, :], tau_row[:, :], ACT.Exp, scale=-1.0))
            dve.wait(tok["small"])
            tok["w_on"] = dve.do(lambda v: v.tensor_scalar(w_on[:, :], w_on[:, :], nw_col[:, 0:1], None, ALU.mult))

        def bias_of(n, e, j):
            c = n * nb + e * FJ + j
            return bias_cols[:, c:c + 1]

        def split(raw, parts, *tokens):
            high, low = parts
            act.wait(*tokens)
            h = act.do(lambda a: a.activation(high, raw, ACT.Copy))
            dve.wait(h, *tokens)
            return h, dve.do(lambda v: v.tensor_tensor(low, raw, high.bitcast(FP), ALU.subtract))

        def product(ps, w, x, start=True, stop=True):
            for n, (a, b) in enumerate(((0, 0), (0, 1), (1, 0))):
                p = pe.do(lambda t, a=a, b=b, n=n: t.matmul(ps, w[a], x[b], start=start and n == 0, stop=stop and n == 2))
            return p

        def load_gl(m):
            slot, n = m % GL_SLOTS, m % (EXPERTS * FJ)
            flat = w_gl[slot][:].rearrange("p a k n f -> p (a k n f)")
            half = 2 * FJ * P
            if m < EXPERTS * FJ:
                tok["gl", m] = split(gl_raw[n % RAW_SLOTS], (flat[:, 0:half], flat[:, half:]),
                                     tok["gl raw", n], *had(("gl read", slot), ("gl kept", m - GL_SLOTS)))
                sp.wait(*tok["gl", m])
                tok["gl kept", m] = in_gl_d[slot].dma(sp, gl_d[n], flat.bitcast(FP))
                if n + RAW_SLOTS < EXPERTS * FJ:
                    load_gl_raw(n + RAW_SLOTS)
            else:
                sp.wait(tok["gl kept", n], tok["gl read", slot], *had(("gl kept", m - GL_SLOTS)))
                tok["gl", m] = [in_gl[slot].dma(sp, flat.bitcast(FP), gl_d[n])]

        def take():
            while all(b.held for b in shared):
                yield
            got = next(b for b in shared if not b.held)
            got.held = True
            pe.wait(*got.read)
            return got, got.tile

        def transposed(to, tokens, pieces, rows=P):
            pe.wait(*tokens, tok["ident"])
            for n, piece in enumerate(pieces):
                t = pe.do(lambda t, n=n, piece=piece: t.transpose(to.tile[0:rows, n * P:(n + 1) * P], piece, ident[:, :]))
            return t

        def prepare(w):
            par, x, beta = w % 2, xt, beta_ring[w % 2]
            dve.wait(tok["x", w])
            for c in range(CPW):
                s = dve.do(lambda v, c=c: v.bn_stats(stats[:, c, :], x[:, c, :]))
            dve.wait(s)
            for c in range(CPW):
                m = dve.do(lambda v, c=c: v.bn_aggr(moments[:, c, :], stats[:, c, :]))
            pool.wait(m)
            r = pool.do(lambda g: g.tensor_scalar(rstd[:, :], moments[:, :, 1], LN_EPS, None, ALU.add))
            pool.wait(r)
            r = pool.do(lambda g: g.tensor_tensor(rstd[:, :], rstd[:, :], minus_half[:, 0:CPW], ALU.pow))
            yield from pause(2)
            dve.wait(r)
            for c in range(CPW):
                n = dve.do(lambda v, c=c: v.tensor_scalar(x[:, c, :], x[:, c, :], moments[:, c, 0:1],
                                                          rstd[:, c:c + 1], ALU.subtract, ALU.mult))
            tok["normed", w] = n
            yield from pause(3)
            while w >= 3 and (("ffn read", w - 3) not in tok or ("fuse read", w - 3) not in tok
                              or ("qkv read", w - 3) not in tok):
                yield
            yield from pause(5)
            bk, ps = yield from take()
            tok["xn T", w] = transposed(bk, [n], [x[:, c, :] for c in range(CPW)])
            yield from pause(3)
            tok["xf high", w], tok["xf", w] = split(
                ps[:, :], [part[:, :] for part in xf[w % 3]], tok["xn T", w],
                *had(("ffn read", w - 3), ("fuse read", w - 3), ("qkv read", w - 3)))
            if w + 1 < WINDOWS:
                sp.wait(tok["xn T", w])
                for b in range(SEQS):
                    tok["x", w + 1] = in_x.dma(
                        sp, xt[CHUNK * b:CHUNK * b + CHUNK, :, :],
                        hidden[b, rows_of(b, w + 1), :].rearrange("(c i) d -> i c d", i=CHUNK))
            bk.leave(tok["xf", w])
            yield
            while w >= 2 and (("v_b", w - 2) not in tok or ("beta_mask", w - 2) not in tok):
                yield
            bk, ps = yield from take()
            pe.wait(tok["xf high", w], tok["xf", w], tok["first"])
            nr = EXPERTS + HEADS
            for c in range(CPW):
                for k, part in enumerate(xf[w % 3]):
                    lgt = pe.do(lambda t, c=c, k=k, part=part, ps=ps: t.matmul(
                        ps[:, c * nr:(c + 1) * nr], part[:, c * P:(c + 1) * P].bitcast(FP), w_rb[:, :],
                        start=k == 0, stop=k == 1))
            yield
            view = ps[:, 0:CPW * nr].rearrange("p (c n) -> p c n", n=nr)
            dve.wait(lgt, tok["first"])
            g = dve.do(lambda v, view=view: v.tensor_tensor(
                glog[:, :, :], view[:, :, 0:EXPERTS], over(bgate_row[:, :].unsqueeze(1), P, CPW, EXPERTS), ALU.add))
            act.wait(g, *had(("v_b", w - 2), ("beta_mask", w - 2), ("k_b", w - 2)))
            tok["beta", w] = act.do(
                lambda a, view=view: a.activation(beta[:, :, :], view[:, :, EXPERTS:], ACT.Sigmoid))
            bk.leave(tok["beta", w])
            dve.wait(g)
            full = (P, CPW, EXPERTS, EXPERTS)
            other = over(glog[:, :, :].unsqueeze(2), *full)
            own = over(glog[:, :, :].unsqueeze(3), *full)
            dve.do(lambda v: v.tensor_tensor(ties[:, :, :, :], other, own, ALU.is_equal))
            bt = dve.do(lambda v: v.tensor_tensor(beats[:, :, :, :], other, own, ALU.is_gt))
            mx = dve.do(lambda v: v.tensor_reduce(gmax[:, :], glog[:, :, :], AX.X, ALU.max))
            dve.wait(bt, mx)
            d = dve.do(lambda v: v.tensor_tensor(
                glog[:, :, :], glog[:, :, :], over(gmax[:, :].unsqueeze(2), P, CPW, EXPERTS), ALU.subtract))
            t = dve.do(lambda v: v.tensor_tensor(
                ties[:, :, :, :], ties[:, :, :, :], over(earlier8[:, :, :].unsqueeze(1), *full), ALU.mult))
            act.wait(d)
            act.do(lambda a: a.activation(gsig[:, 0, :, :], glog[:, :, :], ACT.Sigmoid))
            sg = act.do(lambda a: a.activation(gsig[:, 1, :, :], glog[:, :, :], ACT.Sigmoid, scale=-1.0))
            dve.wait(t)
            t = dve.do(lambda v: v.tensor_tensor(beats[:, :, :, :], beats[:, :, :, :], ties[:, :, :, :], ALU.add))
            dve.wait(t)
            t = dve.do(lambda v: v.tensor_reduce(
                rank[:, :], beats[:, :, :, :].rearrange("p c e j -> p (c e) j"), AX.X, ALU.add))
            yield from pause(2)
            dve.wait(sg)
            rc = dve.do(lambda v: v.reciprocal(gsig[:, 1, :, :], gsig[:, 1, :, :]))
            dve.wait(rc, t)
            ex = dve.do(lambda v: v.tensor_tensor(gsig[:, 0, :, :], gsig[:, 0, :, :], gsig[:, 1, :, :], ALU.mult))
            dve.wait(ex)
            gv = gsig[:, 0, :, :].rearrange("p c e -> p (c e)")
            ex = dve.do(lambda v: v.scalar_tensor_tensor(gv, rank[:, :], 1.5, gv, ALU.is_lt, ALU.mult))
            dve.wait(ex)
            sm = dve.do(lambda v: v.tensor_reduce(gsum[:, :], gsig[:, 0, :, :], AX.X, ALU.add))
            dve.wait(sm)
            rc = dve.do(lambda v: v.reciprocal(gsum[:, :], gsum[:, :]))
            dve.wait(rc, *had(("route T", w - 1)))
            rt = dve.do(lambda v: v.tensor_tensor(
                route[:, :, :], gsig[:, 0, :, :], over(gsum[:, :].unsqueeze(2), P, CPW, EXPERTS), ALU.mult))
            yield from pause(7)
            while w >= 1 and ("b3", w - 1) not in tok:
                yield
            bk, ps = yield from take()
            tok["route T", w] = transposed(bk, [rt], [route[:, c, :] for c in range(CPW)], rows=EXPERTS)
            yield from pause(2)
            act.wait(tok["route T", w], *had(("b3", w - 1), ("route_d", w - 1)))
            tok["route_T", w] = act.do(
                lambda a, ps=ps: a.activation(route_T[:, :], ps[0:EXPERTS, :], ACT.Copy))
            bk.leave(tok["route_T", w])
            sp.wait(tok["route_T", w], *had(("route_bc last", w - 2)))
            tok["route_d", w] = in_route[par].dma(sp, route_d[par], route_T[:, :])
            yield

        def project(w, n):
            par = w % 2
            bk, ps = yield from take()
            pe.wait(tok["xf high", w], tok["xf", w], *tok["qkv split"])
            pr = product(ps[:, :], [part[:, n, :] for part in w_qkv], [part[:, :] for part in xf[w % 3]])
            act.wait(pr, *had("halo kept", "conv"))
            cp = act.do(lambda a, ps=ps: a.activation(
                pre[:, :, K_CONV - 1:], runs_flat(ps[:, :]), ACT.Copy))
            bk.leave(cp)
            if n == 2:
                tok["qkv read", w] = pr
            pool.wait(tok["zeroed"], *had("conv"))
            hl = pool.do(lambda g: g.tensor_copy(pre[:, 0:SEQS, 0:K_CONV - 1], conv_halo[:, n, :, :]))
            pool.wait(cp, hl)
            hl = spread_halo(pre, K_CONV - 1)
            tok["halo kept"] = pool.do(lambda g: g.tensor_copy(conv_halo[:, n, :, :], pre[:, RUNS - SEQS:, CHUNK:]))
            yield from pause(2)
            act.wait(cp, hl, tok["small"], *had("silu"))
            c = act.do(lambda a: a.activation(runs(acc), pre[:, :, 0:CHUNK], ACT.Copy, scale=conv_w[:, n, 0:1]))
            yield
            dve.wait(cp, hl, tok["small"])
            for k in range(1, K_CONV):
                dve.wait(c)
                c = dve.do(lambda v, k=k: v.scalar_tensor_tensor(
                    runs(acc), pre[:, :, k:k + CHUNK], conv_w[:, n, k:k + 1], runs(acc), ALU.mult, ALU.add))
                yield
            tok["conv"] = c
            act.wait(c, *had("silu", "qk T", ("v act", w - 1)))
            sg = act.do(lambda a: a.activation(gate[:, :, :, :], acc[:, :, :, :], ACT.Sigmoid))
            yield from pause(2)
            dve.wait(sg)
            tok["silu"] = dve.do(lambda v: v.tensor_tensor(gate[:, :, :, :], acc[:, :, :, :], gate[:, :, :, :], ALU.mult))
            yield

        def normed(w, dst, last_reader):
            yield from pause(2)
            bk, ps = yield from take()
            t = tok["qk T"] = transposed(bk, [tok["silu"]], chunks(gate))
            act.wait(t, *had("sumsq", ("q_n T", w)))
            sq = act.do(lambda a, ps=ps: a.activation(square[:].rearrange("p c h e -> p (c h e)"), ps[:, :], ACT.Square))
            yield from pause(2)
            dve.wait(sq, *had("rnorm read"))
            s = tok["sumsq"] = dve.do(lambda v: v.tensor_reduce(sumsq[:, :, :], square[:, :, :, :], AX.X, ALU.add))
            flat = sumsq[:, :, :].rearrange("p c h -> p (c h)")
            pool.wait(s)
            a = pool.do(lambda g: g.tensor_scalar(flat, flat, L2_EPS, None, ALU.add))
            pool.wait(a)
            r = pool.do(lambda g: g.tensor_tensor(flat, flat, minus_half[:, :], ALU.pow))
            yield from pause(2)
            dve.wait(r, *had(*last_reader))
            tok["rnorm read"] = tok["normed qk"] = dve.do(
                lambda v, ps=ps: v.tensor_tensor(dst[:, :, :].rearrange("p c (h e) -> p c h e", h=HEADS), as_heads(ps[:, :]), heads_bc(sumsq[:, :, :]), ALU.mult))
            bk.leave(tok["rnorm read"])
            yield from pause(2)

        def attend(w):
            par, beta = w % 2, beta_ring[w % 2]
            while ("beta", w) not in tok:
                yield
            if w == 0:
                tok["qkv split"] = split(qkv_raw, [part[:].rearrange("p n d -> p (n d)") for part in w_qkv], tok["qkv raw"])
                tok["fx split"] = split(fx_raw, [part[:, :] for part in w_fx], tok["small"])
            yield
            yield from project(w, 0)
            yield from normed(w, q_n, [("q_n T", w - 1)])
            while w >= 2 and ("recurred", w - 2) not in tok:
                yield
            yield
            bk, ps = yield from take()
            tok["q_n T", w] = transposed(bk, [tok["normed qk"]], [q_n[:, c, :] for c in range(CPW)])
            act.wait(tok["q_n T", w], *had(("recurred", w - 2)))
            tok["q_T", w] = act.do(
                lambda a, ps=ps: a.activation(q_T[par][:].rearrange("p c b i -> p (c b i)"), ps[:, :], ACT.Copy))
            bk.leave(tok["q_T", w])
            yield from project(w, 1)
            yield from normed(w, k_n[par], [("recurred", w - 2)])
            tok["k_n", w] = tok["normed qk"]
            yield from project(w, 2)
            while w >= 2 and ("v again", w - 2) not in tok:
                yield
            pool.wait(tok["silu"], tok["zeroed"], *had(("fir", w - 2), ("v again", w - 2), ("v act", w - 1)))
            pool.do(lambda g: g.tensor_copy(v_act[par][:, 0:SEQS, 0:HALO], v_act[1 - par][:, RUNS - SEQS:, CHUNK:]))
            vc = pool.do(lambda g: g.tensor_copy(v_act[par][:, :, HALO:], runs(gate)))
            pool.wait(vc)
            tok["v act", w] = spread_halo(v_act[par], HALO)
            yield from pause(5)
            bk, ps = yield from take()
            vt = tok["qk T"] = transposed(bk, [tok["silu"]], chunks(gate))
            yield from pause(4)
            dve.wait(vt, tok["beta", w], *had(("recurred", w - 2)))
            tok["v_b", w] = dve.do(lambda v, ps=ps: v.tensor_tensor(
                as_heads(v_b[par][:, :, :].rearrange("p c d -> p (c d)")), as_heads(ps[:, :]), heads_bc(beta[:, :, :]), ALU.mult))
            bk.leave(tok["v_b", w])
            yield from pause(3)

        def triangles(w):
            par, beta = w % 2, beta_ring[w % 2]
            while ("k_n", w) not in tok:
                yield
            yield
            bk, ps = yield from take()
            kt = transposed(bk, [tok["k_n", w]], [k_n[par][:, c, :] for c in range(CPW)])
            pool.wait(tok["k_n", w], tok["beta", w], *had(("recurred", w - 2)))
            tok["k_b", w] = pool.do(lambda g: g.tensor_tensor(
                as_heads(k_b[par][:, :, :].rearrange("p c d -> p (c d)")),
                as_heads(k_n[par][:, :, :].rearrange("p c d -> p (c d)")), heads_bc(beta[:, :, :]), ALU.mult))
            pool.wait(tok["diag"], *had(("system", w - 1)))
            tok["beta_mask", w] = pool.do(lambda g: g.tensor_tensor(
                beta_mask[:, :, :, :], heads_bc(beta[:, :, :]),
                over(before[:, :].unsqueeze(1), P, CPW * HEADS, CHUNK).rearrange("p (c h) j -> p c h j", c=CPW), ALU.mult))
            yield from pause(2)
            act.wait(kt, *had(("products", w - 1), ("kq_bd", w - 1)))
            kT = act.do(lambda a, ps=ps: a.activation(k_T[:].rearrange("p c b i -> p (c b i)"), ps[:, :], ACT.Copy))
            bk.leave(kT)
            for c in range(CPW):
                pool.wait(kT, tok["q_T", w], tok["zeroed"], *had("products"))
                act.wait(kT, *had("products"), tok["zeroed"])
                for h in range(HEADS):
                    rows = slice(HD * h, HD * h + HD)
                    pool.fence()
                    cq = pool.do(lambda g, h=h, rows=rows, c=c: g.tensor_copy(
                        kq_bd[rows, :, 1, h, :], q_T[par][rows, c, :, :]))
                    ck = act.do(lambda a, h=h, rows=rows, c=c: a.activation(
                        kq_bd[rows, :, 0, h, :], k_T[rows, c, :, :], ACT.Copy))
                pool.fence()
                tok["kq_bd", w] = cq
                yield from pause(3)
                bk, ps = yield from take()
                pe.wait(kT, cq, ck)
                for b in range(SEQS):
                    pr = pe.do(lambda t, c=c, b=b, ps=ps: t.matmul(
                        ps[CHUNK * b:CHUNK * b + CHUNK, 0:256], k_T[:, c, b, :],
                        kq_bd[:, b, :, :, :].rearrange("p s h i -> p (s h i)"), start=True, stop=True,
                        tile_position=(0, CHUNK * b)))
                tok["products"] = tok["products", w] = pr
                yield
                view = ps[:, 0:256].rearrange("p (s h i) -> p s h i", s=2, h=HEADS)
                dve.wait(pr, tok["beta_mask", w], *had(("system_d", w - 1)))
                L = dve.do(lambda v, c=c, view=view: v.tensor_tensor(
                    system[:, c, :, :], view[:, 0], beta_mask[:, c, :, :], ALU.mult))
                act.wait(L, *had(("recurred", w - 2)))
                tok["local", w] = act.do(lambda a, c=c, view=view: a.activation(
                    local[par][:, c, :, :], view[:, 1], ACT.Copy))
                bk.leave(tok["local", w])
                yield
            pool.wait(L)
            flat = system[:].rearrange("p c h j -> p (c h) j")
            tok["system", w] = pool.do(lambda g: g.tensor_tensor(
                flat, flat, over(diagonal[:, :].unsqueeze(1), P, CPW * HEADS, CHUNK), ALU.subtract))
            sp.wait(tok["system", w], *had(("solve in", w - 2)))
            for b in range(SEQS):
                n0 = b * CPW * HEADS
                tok["system_d", w] = in_system.dma(
                    sp, system_d[par, n0:n0 + CPW * HEADS].rearrange("n i j -> i n j"),
                    flat[CHUNK * b:CHUNK * b + CHUNK])
            while w >= 1 and ("solved", w - 1) not in tok:
                yield
            sp.wait(tok["system_d", w], *had(("solved", w - 1)))
            for half in range(2):
                tok["solve in", w] = in_solve.dma(
                    sp, solve_L[64 * half:64 * half + 64, :, :], system_d[par])

        def invert(w):
            par = w % 2
            while ("solve in", w) not in tok:
                yield
            while w >= 2 and ("inv_bd", w - 2) not in tok:
                yield
            pool.wait(*had(("inverse_d", w - 1)))
            pool.do(lambda g: g.memset(solve_T[:, :, :], 0.0))
            for half in range(2):
                part = solve_T[64 * half:64 * half + 64, :, :]
                pool.fence()
                st = pool.do(lambda g, part=part, half=half: g.affine_select(
                    out=part, in_=part, compare_op=ALU.not_equal, fill=1.0, base=KH * half,
                    pattern=[[1, KH], [-1, CHUNK]], channel_multiplier=0))
            pool.fence()
            yield from pause(7)
            dve.wait(tok["solve in", w], st)
            last = st
            for i in range(1, CHUNK):
                k = min(i, KH)
                prod = solve_prod[:, 0:k * (i + 1)].rearrange("p (k j) -> p k j", k=k)
                dve.wait(last)
                m = dve.do(lambda v, i=i, k=k, prod=prod: v.tensor_tensor(
                    prod, solve_T[:, 0:k, 0:i + 1], over(solve_L[:, i, 0:i + 1].unsqueeze(1), P, k, i + 1), ALU.mult))
                if i % 4 == 0:
                    yield from pause(2)
                dve.wait(m)
                last = dve.do(lambda v, i=i, k=k, prod=prod: v.tensor_reduce(
                    solve_T[:, 0:k, i], prod, AX.X, ALU.add, negate=True))
                if i > 16 or i % 2:
                    yield
            tok["solved", w] = last
            sp.wait(last, *had(("inv_bd", w - 2)))
            for half in range(2):
                tok["inverse_d", w] = in_inverse.dma(
                    sp, inverse_d[par, :, KH * half:KH * half + KH, :], solve_T[64 * half:64 * half + 64, :, :])
            yield from pause(7)

        def filters(w):
            par = w % 2
            while ("v act", w) not in tok:
                yield
            while w >= 1 and ("fir T", w - 1) not in tok:
                yield
            v = v_act[par]
            ready = [tok["v act", w], tok["small"], *had(("fir T", w - 1), ("fuse read", w - 1))]

            def tap(dst, weights, taps, k):
                src, weight = v[:, :, HALO - taps + 1 + k:HALO - taps + 1 + k + CHUNK], weights[:, k:k + 1]
                if k == 0:
                    act.wait(*ready)
                    return act.do(lambda e: e.activation(runs(dst), src, ACT.Copy, scale=weight))
                return dve.do(lambda e: e.scalar_tensor_tensor(runs(dst), src, weight, runs(dst), ALU.mult, ALU.add))

            done = {}
            for k in range(K_LONG):
                for dst, weights, n in ((fir_s, short_w, K_SHORT), (fir_l, long_w, K_LONG)):
                    if k < n:
                        if k:
                            dve.wait(*ready, done[n])
                        done[n] = tap(dst, weights, n, k)
                yield
            tok["fir", w] = done[K_LONG]
            tok["fir short", w] = done[K_SHORT]

        def recur(w):
            par = w % 2
            while ("inverse_d", w) not in tok or ("v_b", w) not in tok:
                yield
            if w == 0:
                while ("up split", EXPERTS - 1) not in tok or ("gl", EXPERTS * FJ - 1) not in tok:
                    yield
                fold_small()
                for q in (sp, act, dve, pool):
                    q.wait(*(t for e in range(EXPERTS) for t in tok["up split", e]), tok["bias_ps"],
                           *(t for n in range(EXPERTS * FJ) for t in tok["gl", n]))
                pool.do(lambda g: g.memset(kn_bd[0][:].rearrange("p b d -> p (b d)"), 0.0))
                tok["zeroed"] = pool.do(lambda g: g.memset(inv_bd[:].rearrange("p c h b i -> p (c h b i)"), 0.0))
            sp.wait(tok["inverse_d", w], tok["zeroed"], *had(("w_T ps", w - 1)))
            for b in range(SEQS):
                n0 = b * CPW * HEADS
                tok["inv_bd", w] = in_inv_bd.dma(
                    sp, inv_bd[CHUNK * b:CHUNK * b + CHUNK, :, :, b, :].rearrange("p c h i -> p (c h) i"),
                    inverse_d[par, n0:n0 + CPW * HEADS].rearrange("n k i -> k n i"))
            for _ in range(6):
                yield
            while w >= 1 and ("fuse2", w - 1) not in tok:
                yield
            bk, ps = yield from take()
            pe.wait(tok["inv_bd", w], tok["v_b", w], tok["k_b", w])
            for c in range(CPW):
                for h in range(HEADS):
                    cols = slice(HD * h, HD * h + HD)
                    u = pe.do(lambda t, c=c, h=h, cols=cols, ps=ps: t.matmul(
                        ps[:, c * D + HD * h:c * D + HD * h + HD],
                        inv_bd[:, c, h, :, :].rearrange("p b i -> p (b i)"), v_b[par][:, c, cols], start=True, stop=True))
            yield from pause(2)
            act.wait(u, *had(("fuse2", w - 1)))
            uc = act.do(lambda a, ps=ps: a.activation(u_sb[:].rearrange("p c d -> p (c d)"), ps[:, :], ACT.Copy))
            bk.leave(uc)
            yield
            bk, ps = yield from take()
            pe.wait(uc)
            for c in range(CPW):
                for h in range(HEADS):
                    cols = slice(HD * h, HD * h + HD)
                    wt = pe.do(lambda t, c=c, h=h, cols=cols, ps=ps: t.matmul(
                        ps[cols, c * P:(c + 1) * P], k_b[par][:, c, cols],
                        inv_bd[:, c, h, :, :].rearrange("p b i -> p (b i)"), start=True, stop=True,
                        tile_position=(0, HD * h)))
                if c % 2:
                    yield
            tok["w_T ps", w] = wt
            act.wait(wt, *had(("recurred", w - 1), ("fuse2", w - 1)))
            wc = act.do(lambda a, ps=ps: a.activation(w_T[:].rearrange("p c b i -> p (c b i)"), ps[:, :], ACT.Copy))
            bk.leave(wc)
            yield from pause(2)
            while w >= 1 and ("delta read", w - 1) not in tok:
                yield
            for c in range(CPW):
                last_chunk = w == WINDOWS - 1 and c == CPW - 1
                cp = (w * CPW + c) % 2
                act.wait(tok["zeroed"], *had(("state ps", cp)))
                for b in range(SEQS):
                    rows = slice(CHUNK * b, CHUNK * b + CHUNK)
                    kd = act.do(lambda a, b=b, rows=rows, c=c, cp=cp: a.activation(
                        kn_bd[cp][rows, b, :], k_n[par][rows, c, :], ACT.Copy))
                pool.wait(tok["local", w], tok["masks"], *had("local read"))
                ld = pool.do(lambda g, c=c: g.tensor_tensor(
                    local_bd[:, :, :, :], over(local[par][:, c, :, :].unsqueeze(2), P, HEADS, SEQS, CHUNK),
                    over(causal_bd[:, :].rearrange("p (b i) -> p b i", b=SEQS).unsqueeze(1), P, HEADS, SEQS, CHUNK), ALU.mult))
                bk, ps = yield from take()
                pe.wait(wc, tok["q_T", w], tok["zeroed"], *had("state"))
                for b in range(SEQS):
                    rows = slice(CHUNK * b, CHUNK * b + CHUNK)
                    ws = pe.do(lambda t, b=b, rows=rows, c=c, ps=ps: t.matmul(
                        ps[rows, 0:D], w_T[:, c, b, :], state[:, b, :], start=True, stop=True, tile_position=(0, CHUNK * b)))
                for b in range(SEQS):
                    rows = slice(CHUNK * b, CHUNK * b + CHUNK)
                    qs = pe.do(lambda t, b=b, rows=rows, c=c, ps=ps: t.matmul(
                        ps[rows, D:2 * D], q_T[par][:, c, b, :], state[:, b, :], start=True, stop=False,
                        tile_position=(0, CHUNK * b), skip_group_check=True))
                yield from pause(2)
                dve.wait(qs, *had("u_adj read"))
                ua = dve.do(lambda v, c=c, ps=ps: v.tensor_tensor(u_adj[:, :], u_sb[:, c, :], ps[:, 0:D], ALU.subtract))
                yield from pause(3)
                pe.wait(ua, kd, ld)
                if not last_chunk:
                    for b in range(SEQS):
                        sps = pe.do(lambda t, b=b, cp=cp, first=(w == 0 and c == 0 and b == 0): t.matmul(
                            ps_state[:, b * D:(b + 1) * D], kn_bd[cp][:, b, :], u_adj[:, :], start=first, stop=True,
                            skip_group_check=True))
                    tok["state ps", cp] = sps
                for h in range(HEADS):
                    cols = slice(HD * h, HD * h + HD)
                    lo = pe.do(lambda t, h=h, cols=cols, cp=cp, ps=ps: t.matmul(
                        ps[:, D + HD * h:D + HD * h + HD], local_bd[:, h, :, :].rearrange("p b i -> p (b i)"),
                        u_adj[:, cols], start=False, stop=True, skip_group_check=True))
                tok["u_adj read"] = tok["local read"] = lo
                if not last_chunk:
                    act.wait(sps)
                    for h in range(HEADS):
                        rows = slice(HD * h, HD * h + HD)
                        tok["state"] = act.do(lambda a, rows=rows: a.activation(
                            state[rows, :, rows], ps_state[rows, :].rearrange("p (b n) -> p b n", b=SEQS)[:, :, rows],
                            ACT.Copy))
                act.wait(lo, *had(("delta read", w - 1)))
                dl = tok["delta", w, c] = act.do(lambda a, c=c, ps=ps: a.activation(delta[:, c, :], ps[:, D:2 * D], ACT.Copy))
                bk.leave(dl)
                if c == CPW - 1:
                    tok["recurred", w] = lo
                yield from pause(2)

        def finish(w):
            par = w % 2
            while ("recurred", w) not in tok:
                yield
            yield from pause(2)
            dl = tok["delta", w, CPW - 1]
            bk, ps = yield from take()
            t = transposed(bk, [dl], [delta[:, c, :] for c in range(CPW)])
            yield
            act.wait(t, *had(("fuse read", w - 1), ("v mixed", w - 1)))
            dT = act.do(lambda a, ps=ps: a.activation(delta_T[:, :], ps[:, :], ACT.Copy))
            bk.leave(dT)
            yield from pause(2)
            while ("fir", w) not in tok:
                yield
            for m in range(2):
                bk, ps = yield from take()
                pe.wait(dT, tok["fir short", w], tok["fir", w], tok["xf high", w], tok["xf", w], *tok["fx split"])
                rhs = [None, fir_s[:].rearrange("p c b i -> p (c b i)"),
                       fir_l[:].rearrange("p c b i -> p (c b i)"), delta_T[:, :]]
                product(ps[:, :], [part[:, m * P:(m + 1) * P] for part in w_fx], [part[:, :] for part in xf[w % 3]], stop=False)
                yield from pause(3)
                for k in range(1, 4):
                    f = pe.do(lambda t, k=k, m=m, r=rhs[k], ps=ps: t.matmul(
                        ps[:, :], w_f1[:, k - 1, m * P:(m + 1) * P], r,
                        start=False, stop=k == 3))
                    if k % 2:
                        yield
                act.wait(f, tok["bias"])
                hp = act.do(lambda a, m=m, ps=ps: a.activation(
                    hid[m][:, :], ps[:, :], ACT.Identity, bias=bias_cols[:, 4 * nb + m:4 * nb + m + 1]))
                bk.leave(hp)
                yield
            act.wait(hp)
            for m in range(2):
                tok["hid"] = act.do(lambda a, m=m: a.activation(hid[m][:, :], hid[m][:, :], ACT.Gelu))
            tok["fuse read", w] = f
            yield from pause(3)
            bk, ps = yield from take()
            pe.wait(tok["hid"])
            for c in range(CPW):
                for m in range(2):
                    f2 = pe.do(lambda t, c=c, m=m, ps=ps: t.matmul(
                        ps[:, c * 16:(c + 1) * 16], hid[m][:, c * P:(c + 1) * P], w_f2[:, m, :], start=m == 0, stop=m == 1))
            tok["fuse2", w] = f2
            yield
            dve.wait(f2, *had("p used"))
            l = dve.do(lambda v, ps=ps: v.tensor_tensor(
                lg[:].rearrange("p c h k -> p c (h k)"), ps[:, 0:CPW * 16].rearrange("p (c n) -> p c n", n=16),
                over(bf2_row[:, :].unsqueeze(1), P, CPW, 16), ALU.add))
            bk.leave(l)
            act.wait(l)
            s = act.do(lambda a: a.activation(p_raw[:, :, :], lg[:, :, :, 3], ACT.Sigmoid))
            dve.wait(l, tok["inv_tau"])
            l = dve.do(lambda v: v.tensor_tensor(
                l3[:, :, :, :], lg[:, :, :, 0:3],
                over(inv_tau[:, :].unsqueeze(1).unsqueeze(3), P, CPW, HEADS, 3), ALU.mult))
            dve.wait(l)
            l = dve.do(lambda v: v.tensor_reduce(l3max[:, :, :], l3[:, :, :, :], AX.X, ALU.max))
            dve.wait(l)
            l = dve.do(lambda v: v.tensor_tensor(
                l3[:, :, :, :], l3[:, :, :, :], over(l3max[:, :, :].unsqueeze(3), P, CPW, HEADS, 3), ALU.subtract))
            act.wait(l)
            act.do(lambda a: a.activation(l3sig[:, 0], l3[:, :, :, :], ACT.Sigmoid))
            sg = act.do(lambda a: a.activation(l3sig[:, 1], l3[:, :, :, :], ACT.Sigmoid, scale=-1.0))
            dve.wait(s)
            a1 = dve.do(lambda v: v.tensor_scalar(p_val[:, :, :], p_raw[:, :, :], FLOOR_MAX - FLOOR_MIN, 1.0 - FLOOR_MAX, ALU.mult, ALU.add))
            dve.wait(a1)
            a1 = dve.do(lambda v: v.tensor_tensor(p_val[:, :, :], p_val[:, :, :], p_raw[:, :, :], ALU.mult))
            dve.wait(a1)
            a1 = dve.do(lambda v: v.tensor_scalar(p_rest[:, :, :], p_val[:, :, :], -1.0, 1.0, ALU.mult, ALU.add))
            yield
            dve.wait(sg)
            r = dve.do(lambda v: v.reciprocal(l3sig[:, 1], l3sig[:, 1]))
            dve.wait(r)
            r = dve.do(lambda v: v.tensor_tensor(l3sig[:, 0], l3sig[:, 0], l3sig[:, 1], ALU.mult))
            dve.wait(r)
            r = dve.do(lambda v: v.tensor_reduce(l3sum[:, :, :], l3sig[:, 0], AX.X, ALU.add))
            dve.wait(r)
            r = dve.do(lambda v: v.reciprocal(l3sum[:, :, :], l3sum[:, :, :]))
            dve.wait(r, a1)
            r = dve.do(lambda v: v.tensor_tensor(l3sum[:, :, :], l3sum[:, :, :], p_rest[:, :, :], ALU.mult))
            dve.wait(r)
            pc = dve.do(lambda v: v.tensor_tensor(
                l3[:, :, :, :], l3sig[:, 0], over(l3sum[:, :, :].unsqueeze(3), P, CPW, HEADS, 3), ALU.mult))
            yield
            yield from pause(3)
            bk, ps = yield from take()
            t = transposed(bk, [], chunks(fir_s))
            pool.wait(pc, dl, *had(("mixed", w - 1), ("out ps", w - 1)))
            m2 = tok["delta read", w] = pool.do(lambda g: g.tensor_tensor(
                mix_part[1][:, :, :, :], as_heads(delta[:].rearrange("p c d -> p (c d)")), heads_bc(l3[:, :, :, 2]), ALU.mult))
            yield
            dve.wait(t, pc, *had(("o_T ps", w - 1)))
            m0 = dve.do(lambda v, ps=ps: v.tensor_tensor(
                mix[:, :, :, :], as_heads(ps[:, :]), heads_bc(l3[:, :, :, 0]), ALU.mult))
            bk.leave(m0)
            yield
            bk, ps = yield from take()
            t = tok["fir T", w] = transposed(bk, [], chunks(fir_l))
            pool.wait(m0, m2)
            s = pool.do(lambda g: g.tensor_tensor(mix[:, :, :, :], mix[:, :, :, :], mix_part[1][:, :, :, :], ALU.add))
            dve.wait(t)
            m1 = dve.do(lambda v, ps=ps: v.tensor_tensor(
                mix_part[0][:, :, :, :], as_heads(ps[:, :]), heads_bc(l3[:, :, :, 1]), ALU.mult))
            bk.leave(m1)
            pool.wait(m1, s)
            s = pool.do(lambda g: g.tensor_tensor(mix[:, :, :, :], mix[:, :, :, :], mix_part[0][:, :, :, :], ALU.add))
            yield
            pool.wait(tok["fuse read", w])
            vc = tok["v again", w] = pool.do(lambda g: g.tensor_copy(
                runs_flat(delta_T[:, :]), v_act[par][:, :, HALO:]))
            yield from pause(4)
            bk, ps = yield from take()
            t = tok["v mixed", w] = transposed(bk, [vc], [delta_T[:, c * P:(c + 1) * P] for c in range(CPW)])
            yield
            dve.wait(t, s)
            m1 = tok["p used"] = dve.do(lambda v, ps=ps: v.tensor_tensor(
                mix_part[1][:, :, :, :], as_heads(ps[:, :]), heads_bc(p_val[:, :, :]), ALU.mult))
            bk.leave(m1)
            dve.wait(m1)
            s = tok["mixed", w] = dve.do(lambda v: v.tensor_tensor(mix[:, :, :, :], mix[:, :, :, :], mix_part[1][:, :, :, :], ALU.add))
            act.wait(s)
            s = act.do(lambda a: a.activation(mix_part[0][:, :, :, :], mix[:, :, :, :], ACT.Square))
            yield from pause(2)
            yield from pause(8)
            dve.wait(s)
            s = dve.do(lambda v: v.tensor_reduce(ssq_o[:, :, :], mix_part[0][:, :, :, :], AX.X, ALU.add))
            pool.wait(s)
            flat = ssq_o[:, :, :].rearrange("p c h -> p (c h)")
            s = pool.do(lambda g: g.tensor_scalar(flat, flat, 1.0 / HD, RMS_EPS, ALU.mult, ALU.add))
            pool.wait(s)
            s = pool.do(lambda g: g.tensor_tensor(flat, flat, minus_half[:, :], ALU.pow))
            pool.wait(s)
            s = tok["mixed", w] = pool.do(lambda g: g.tensor_tensor(
                mix[:, :, :, :], mix[:, :, :, :], heads_bc(ssq_o[:, :, :]), ALU.mult))
            yield from pause(4)
            sp.wait(*had(("stored", w - 1)))
            for b in range(SEQS):
                tok["x_res", w] = in_xres.dma(sp, x_res[CHUNK * b:CHUNK * b + CHUNK, :, :],
                                              hidden[b, rows_of(b, w), :].rearrange("(c i) d -> i c d", i=CHUNK))
            yield
            bk, ps = yield from take()
            t = tok["o_T ps", w] = transposed(bk, [s], [mix[:, c, :, :].rearrange("p h e -> p (h e)") for c in range(CPW)])
            yield
            act.wait(t, *had(("out ps", w - 1)))
            oT = act.do(lambda a, ps=ps: a.activation(o_T, ps[:, :], ACT.Copy))
            bk.leave(oT)
            yield from pause(3)
            while ("y_T", w) not in tok:
                yield
            bk, ps = yield from take()
            pe.wait(oT, tok["y_T", w], tok["w_on"])
            for c in range(CPW):
                pe.do(lambda t, c=c, ps=ps: t.matmul(ps[:, c * D:(c + 1) * D], o_T[:, c * P:(c + 1) * P], w_on[:, :], start=True, stop=False))
                t = pe.do(lambda t, c=c, ps=ps: t.matmul(ps[:, c * D:(c + 1) * D], y_T[par][:, c * P:(c + 1) * P], ident[:, :], start=False, stop=True))
            tok["out ps", w] = t
            yield
            dve.wait(t, tok["x_res", w])
            s = tok["summed", w] = dve.do(lambda v, ps=ps: v.tensor_tensor(
                x_res[:].rearrange("p c d -> p (c d)"), ps[:, :], x_res[:].rearrange("p c d -> p (c d)"), ALU.add))
            bk.leave(s)
            sp.wait(s)
            for b in range(SEQS):
                tok["stored", w] = in_out.dma(
                    sp, out[b, rows_of(b, w), :].rearrange("(c i) d -> i c d", i=CHUNK), x_res[CHUNK * b:CHUNK * b + CHUNK, :, :])
            yield from pause(8)

        def load_route(w, e):
            slot = e % 2
            while ("route_d", w) not in tok:
                yield
            sp.wait(tok["route_d", w], *had(("sigc", slot)))
            tok["route_bc", w, e] = in_route_bc[slot].dma(
                sp, route_bc[slot][:, :], route_d[w % 2, e, :].partition_broadcast(P))
            if e == EXPERTS - 1:
                tok["route_bc last", w] = tok["route_bc", w, e]

        def up(w, e, j):
            cols, (high, low), x = slice(j * P, (j + 1) * P), z[e % 2][j], [part[:, :] for part in xf[w % 3]]
            if ("up split", e) not in tok:
                tok["up split", e] = split(up_raw[e], [part[:, e, :, :].rearrange("p n f -> p (n f)") for part in w_up],
                                           tok["up raw", e])
            pe.wait(tok["xf high", w], tok["xf", w], *tok["up split", e], *had("up1"))
            x1 = product(ps_x1[:, :], [part[:, e, 0, cols] for part in w_up], x)
            pe.wait(*had("z"))
            x2 = product(ps_x2[:, :], [part[:, e, 1, cols] for part in w_up], x)
            if e == EXPERTS - 1 and j == FJ - 1:
                tok["ffn read", w] = x2
            act.wait(x1, tok["bias"], *had(("low", j)))
            a = tok["up1"] = act.do(lambda a: a.activation(up1[j][:, :], ps_x1[:, :], ACT.Identity, bias=bias_of(0, e, j)))
            yield
            dve.wait(a, x2)
            zt = tok["z"] = dve.do(lambda v: v.scalar_tensor_tensor(
                up1[j][:, :], ps_x2[:, :], bias_of(1, e, j), up1[j][:, :], ALU.add, ALU.mult))
            act.wait(zt, *had(("z read", e % 2)))
            h = act.do(lambda a: a.activation(high[:, :], up1[j][:, :], ACT.Copy))
            pool.wait(h, zt, *had(("z read", e % 2)))
            tok["low", j] = pool.do(lambda g: g.tensor_tensor(low[:, :], up1[j][:, :], high[:, :].bitcast(FP), ALU.subtract))
            tok["z", w, e, j] = h, tok["low", j]

        def mid(w, e, j):
            m = (w * EXPERTS + e) * FJ + j
            slot, gl = e % 2, w_gl[m % GL_SLOTS]
            if m + 2 < WINDOWS * EXPERTS * FJ:
                load_gl(m + 2)
            pe.wait(*tok["z", w, e, 0], *tok["z", w, e, 1], *tok["gl", m], *had("t"))
            for k in range(FJ):
                g = product(ps_g[:, :], [gl[:, part, k, 0, :] for part in range(2)], [part[:, :] for part in z[e % 2][k]],
                            start=k == 0, stop=k == FJ - 1)
            act.wait(g, *had(("y read", j)))
            s = act.do(lambda a: a.activation(gated[j][:, :], ps_g[:, :], ACT.Sigmoid, bias=bias_of(2, e, j)))
            pe.wait(*had("o"))
            for k in range(FJ):
                l = product(ps_l[:, :], [gl[:, part, k, 1, :] for part in range(2)], [part[:, :] for part in z[e % 2][k]],
                            start=k == 0, stop=k == FJ - 1)
            tok["z read", e % 2] = tok["gl read", m % GL_SLOTS] = l
            yield
            dve.wait(s, g)
            t = tok["t"] = dve.do(lambda v: v.scalar_tensor_tensor(
                gated[j][:, :], ps_g[:, :], bias_of(2, e, j), gated[j][:, :], ALU.add, ALU.mult))
            dve.wait(t, l)
            tok["o"] = dve.do(lambda v: v.scalar_tensor_tensor(
                gated[j][:, :], ps_l[:, :], bias_of(3, e, j), gated[j][:, :], ALU.add, ALU.mult))
            pool.wait(tok["o"], tok["route_bc", w, e])
            tok["routed", j] = tok["sigc", slot] = pool.do(lambda g: g.tensor_tensor(
                gated[j][:, :], gated[j][:, :], route_bc[slot][:, :], ALU.mult))

        def down(w, e, j):
            pe.wait(tok["routed", j])
            if e == 0 and j == 0:
                pe.wait(tok["route_T", w], tok["small"], tok["down"], *had(("y_T", w - 1)))
                tok["b3", w] = pe.do(lambda t: t.matmul(ps_y[:, :], b3_sb[:, :], route_T[:, :], start=True, stop=False))
            last = e == EXPERTS - 1 and j == FJ - 1
            tok["y ps"] = tok["y read", j] = pe.do(lambda t: t.matmul(
                ps_y[:, :], w_dn[:, e, j, :], gated[j][:, :], start=False, stop=last))

        def experts():
            order = [(w, e) for w in range(WINDOWS) for e in range(EXPERTS)]

            def y_out(w):
                act.wait(tok["y ps"], *tok["qkv split"], *tok["fx split"], *had(("out ps", w - 2)))
                tok["y_T", w] = act.do(lambda a: a.activation(y_T[w % 2][:, :], ps_y[:, :], ACT.Copy))

            def need(w):
                while ("xf", w) not in tok:
                    yield

            load_gl(0)
            load_gl(1)
            yield from load_route(0, 0)
            yield from need(0)
            for j in range(FJ):
                yield from up(0, 0, j)
                yield
            for n, (w, e) in enumerate(order):
                nxt = order[n + 1] if n + 1 < len(order) else None
                if nxt:
                    yield from load_route(*nxt)
                    yield from need(nxt[0])
                for j in range(FJ):
                    if nxt:
                        yield from up(*nxt, j)
                        yield
                    yield from mid(w, e, j)
                    if j or n:
                        pj, pe_ = (0, (w, e)) if j else (1, order[n - 1])
                        while pe_[0] >= 2 and ("out ps", pe_[0] - 2) not in tok:
                            yield
                        down(*pe_, pj)
                        if not j and pe_[1] == EXPERTS - 1:
                            y_out(pe_[0])
                    yield
            down(*order[-1], 1)
            y_out(WINDOWS - 1)

        def windows(step):
            for w in range(WINDOWS):
                yield from step(w)

        streams = [windows(recur), windows(prepare), windows(triangles), windows(attend), windows(invert),
                   experts(), windows(finish), windows(filters)]
        while streams:
            for s in list(streams):
                if next(s, "ended") == "ended":
                    streams.remove(s)
        sp.wait(tok["stored", WINDOWS - 1])

        block = ctx.enter_context(nc.Block())

        @block.sync
        def _(eng):
            sp.play(eng)

        @block.gpsimd
        def _(eng):
            pool.play(eng)

        @block.scalar
        def _(eng):
            act.play(eng)

        @block.vector
        def _(eng):
            dve.play(eng)

        @block.tensor
        def _(eng):
            pe.play(eng)


NAMES = ["L0_attn_" + n for n in (
    "hidden_states W_q W_k W_v W_b conv_w_q conv_w_k conv_w_v fir_short_w fir_long_w W_fuse1 b_fuse1 "
    "W_fuse2 b_fuse2 others_log_tau norm_w W_o").split()]
NAMES += ["L0_ffn_" + n for n in "Wgate bgate W1 b1 W2 b2 Wg bg Wl bl W3 b3".split()]


def kernel(**inputs):
    import numpy as np
    import concourse.bacc as bacc
    from concourse.bass_utils import run_bass_kernel_spmd

    nc = bacc.Bacc("TRN2", target_bir_lowering=False, num_devices=1)
    arrays = {n: np.ascontiguousarray(inputs[n]) for n in NAMES}
    aps = [nc.dram_tensor(n, a.shape, mybir.dt.from_np(a.dtype), kind="ExternalInput").ap() for n, a in arrays.items()]
    out = nc.dram_tensor("out", (SEQS, STEPS, D), FP, kind="ExternalOutput").ap()
    layer(nc, *aps, out)
    return run_bass_kernel_spmd(nc, [arrays], core_ids=[0]).results[0]["out"]
```
